# Optimizing a Trainium2 kernel written in Bass

```python
import numpy as np
import jax
import jax.numpy as jnp

def _softmax(x, axis=-1):
    return jax.nn.softmax(x, axis=axis)

def _gelu(x):
    return jax.nn.gelu(x, approximate=True)

def _silu(x):
    return jax.nn.silu(x)

def _sigmoid(x):
    return jax.nn.sigmoid(x)

def _layernorm(x, axis=-1, eps=1e-05):
    m = jnp.mean(x, axis=axis, keepdims=True)
    v = jnp.var(x, axis=axis, keepdims=True)
    return (x - m) / jnp.sqrt(v + eps)

def _scatter_add(tgt, idx, src, axis=0):
    return tgt.at[idx].add(src)

def _segment_sum(src, seg, n):
    return jax.ops.segment_sum(src, seg, n)
kernel_name = 'mk_lm_tower_d1_tok_ids512_r4_a46a65'

def setup_inputs(seed: int=0):
    np.random.seed(seed)
    _w = jnp.asarray

    def _rec_inputs():
        import jax
        import jax.numpy as jnp
        _rk = jax.random.key(seed)
        x = jax.random.randint(jax.random.fold_in(_rk, 1), (8, 512), 0, 50226, jnp.int32)
        return x
    x = _rec_inputs()

    def _L0_tok_setup():
        import jax, jax.numpy as jnp
        import numpy as np
        import math
        V, S, D, B = (50257, 512, 128, 4)
        DFF = 4 * D
        EPS = 1e-05

        def layer_norm(z, g, b):
            mu = jnp.mean(z, axis=-1, keepdims=True)
            var = jnp.mean((z - mu) ** 2, axis=-1, keepdims=True)
            return (z - mu) * jax.lax.rsqrt(var + EPS) * g + b

        def pos_embedding(seq_len, d_model):
            pos = jnp.arange(seq_len, dtype=jnp.float32)[:, None]
            i = jnp.arange(d_model, dtype=jnp.float32)[None, :]
            ang = pos / jnp.power(10000.0, 2.0 * i / d_model)
            even = (jnp.arange(d_model) % 2 == 0)[None, :]
            return jnp.where(even, jnp.sin(ang), jnp.cos(ang))
        key = jax.random.key(seed)
        ks = jax.random.split(key, 14)
        w = lambda k, sh: jax.random.normal(k, sh, dtype=jnp.float32) * 0.02
        return {'input_seq': jax.random.randint(ks[0], (B, S), 0, V), 'emb': w(ks[1], (V, D)), 'wk': w(ks[2], (D, D)), 'bk': jnp.zeros((D,), jnp.float32), 'wq': w(ks[3], (D, D)), 'bq': jnp.zeros((D,), jnp.float32), 'wv': w(ks[4], (D, D)), 'bv': jnp.zeros((D,), jnp.float32), 'ln_g': jnp.ones((D,), jnp.float32), 'ln_b': jnp.zeros((D,), jnp.float32), 'w1': w(ks[5], (D, DFF)), 'b1': jnp.zeros((DFF,), jnp.float32), 'w2': w(ks[6], (DFF, D)), 'b2': jnp.zeros((D,), jnp.float32)}
    _L0_tok_all = _L0_tok_setup()
    _L0_tok_in = {k: v for k, v in _L0_tok_all.items() if k in ('emb', 'wk', 'bk', 'wq', 'bq', 'wv', 'bv', 'ln_g', 'ln_b', 'w1', 'b1', 'w2', 'b2')}
    del _L0_tok_all

    def _L0_attn_setup():
        import jax, jax.numpy as jnp
        import numpy as np
        DEPTH, DIM, HEADS, SEQ, BATCH = (4, 128, 8, 1024, 2)
        DH = DIM // HEADS
        BUCKET = 64
        FF = 4 * DIM
        EPS_ATTN = 0.001
        EPS_LN = 1e-05

        def layer_norm(x, g, b):
            mu = jnp.mean(x, axis=-1, keepdims=True)
            var = jnp.mean(jnp.square(x - mu), axis=-1, keepdims=True)
            return (x - mu) * jax.lax.rsqrt(var + EPS_LN) * g + b

        def causal_linear_attn(q, k, v, bucket_size=BUCKET, eps=EPS_ATTN):
            b, h, n, e = q.shape
            q = jax.nn.softmax(q, axis=-1) * e ** (-0.5)
            k = jnp.exp(k)
            bucket = lambda t: t.reshape(b, h, n // bucket_size, bucket_size, e)
            b_q, b_k, b_v = (bucket(q), bucket(k), bucket(v))
            b_k_cumsum = jnp.cumsum(b_k.sum(axis=-2), axis=-2)
            context = jnp.cumsum(jnp.einsum('bhund,bhune->bhude', b_k, b_v), axis=2)
            if bucket_size > 1:
                context = jnp.pad(context, ((0, 0), (0, 0), (1, 0), (0, 0), (0, 0)))[:, :, :-1]
                b_k_cumsum = jnp.pad(b_k_cumsum, ((0, 0), (0, 0), (1, 0), (0, 0)))[:, :, :-1]
            D = jnp.einsum('bhud,bhund->bhun', b_k_cumsum, b_q)
            D_inv = 1.0 / jnp.clip(D, eps, None)
            out = jnp.einsum('bhund,bhude,bhun->bhune', b_q, context, D_inv)
            return out.reshape(b, h, n, e)
        key = jax.random.key(seed)
        ks = jax.random.split(key, 10)
        s = 0.02
        f32 = jnp.float32
        return {'x': jax.random.normal(ks[0], (BATCH, SEQ, DIM), f32), 'ln1_g': jnp.ones((DEPTH, DIM), f32), 'ln1_b': jnp.zeros((DEPTH, DIM), f32), 'wq': jax.random.normal(ks[1], (DEPTH, DIM, DIM), f32) * s, 'wk': jax.random.normal(ks[2], (DEPTH, DIM, DIM), f32) * s, 'wv': jax.random.normal(ks[3], (DEPTH, DIM, DIM), f32) * s, 'wo': jax.random.normal(ks[4], (DEPTH, DIM, DIM), f32) * s, 'bo': jnp.zeros((DEPTH, DIM), f32), 'ln2_g': jnp.ones((DEPTH, DIM), f32), 'ln2_b': jnp.zeros((DEPTH, DIM), f32), 'w1': jax.random.normal(ks[5], (DEPTH, DIM, FF), f32) * s, 'b1': jnp.zeros((DEPTH, FF), f32), 'w2': jax.random.normal(ks[6], (DEPTH, FF, DIM), f32) * s, 'b2': jnp.zeros((DEPTH, DIM), f32)}
    _L0_attn_all = _L0_attn_setup()
    _L0_attn_in = {k: v for k, v in _L0_attn_all.items() if k in ('ln1_g', 'ln1_b', 'wq', 'wk', 'wv', 'wo', 'bo', 'ln2_g', 'ln2_b', 'w1', 'b1', 'w2', 'b2')}
    del _L0_attn_all

    def _L0_ffn_setup():
        import jax, jax.numpy as jnp
        import numpy as np
        K = 2
        key = jax.random.key(seed)
        ks = jax.random.split(key, 6)
        B, T, d, E, dff = (2, 512, 128, 8, 512)
        x = jax.random.normal(ks[0], (B, T, d), dtype=jnp.float32)
        Wg = jax.random.normal(ks[1], (d, E), dtype=jnp.float32) * 0.02
        W1 = jax.random.normal(ks[2], (E, d, dff), dtype=jnp.float32) * 0.02
        b1 = jnp.zeros((E, dff), dtype=jnp.float32)
        W2 = jax.random.normal(ks[3], (E, dff, d), dtype=jnp.float32) * 0.02
        b2 = jnp.zeros((E, d), dtype=jnp.float32)
        return {'x': x, 'Wg': Wg, 'W1': W1, 'b1': b1, 'W2': W2, 'b2': b2}
    _L0_ffn_all = _L0_ffn_setup()
    _L0_ffn_in = {k: v for k, v in _L0_ffn_all.items() if k in ('Wg', 'W1', 'b1', 'W2', 'b2')}
    del _L0_ffn_all
    return {'x': x, 'L0_tok_emb': _L0_tok_in['emb'], 'L0_tok_wk': _L0_tok_in['wk'], 'L0_tok_bk': _L0_tok_in['bk'], 'L0_tok_wq': _L0_tok_in['wq'], 'L0_tok_bq': _L0_tok_in['bq'], 'L0_tok_wv': _L0_tok_in['wv'], 'L0_tok_bv': _L0_tok_in['bv'], 'L0_tok_ln_g': _L0_tok_in['ln_g'], 'L0_tok_ln_b': _L0_tok_in['ln_b'], 'L0_tok_w1': _L0_tok_in['w1'], 'L0_tok_b1': _L0_tok_in['b1'], 'L0_tok_w2': _L0_tok_in['w2'], 'L0_tok_b2': _L0_tok_in['b2'], 'L0_attn_ln1_g': _L0_attn_in['ln1_g'], 'L0_attn_ln1_b': _L0_attn_in['ln1_b'], 'L0_attn_wq': _L0_attn_in['wq'], 'L0_attn_wk': _L0_attn_in['wk'], 'L0_attn_wv': _L0_attn_in['wv'], 'L0_attn_wo': _L0_attn_in['wo'], 'L0_attn_bo': _L0_attn_in['bo'], 'L0_attn_ln2_g': _L0_attn_in['ln2_g'], 'L0_attn_ln2_b': _L0_attn_in['ln2_b'], 'L0_attn_w1': _L0_attn_in['w1'], 'L0_attn_b1': _L0_attn_in['b1'], 'L0_attn_w2': _L0_attn_in['w2'], 'L0_attn_b2': _L0_attn_in['b2'], 'L0_ffn_Wg': _L0_ffn_in['Wg'], 'L0_ffn_W1': _L0_ffn_in['W1'], 'L0_ffn_b1': _L0_ffn_in['b1'], 'L0_ffn_W2': _L0_ffn_in['W2'], 'L0_ffn_b2': _L0_ffn_in['b2']}

def reference(x, L0_tok_emb, L0_tok_wk, L0_tok_bk, L0_tok_wq, L0_tok_bq, L0_tok_wv, L0_tok_bv, L0_tok_ln_g, L0_tok_ln_b, L0_tok_w1, L0_tok_b1, L0_tok_w2, L0_tok_b2, L0_attn_ln1_g, L0_attn_ln1_b, L0_attn_wq, L0_attn_wk, L0_attn_wv, L0_attn_wo, L0_attn_bo, L0_attn_ln2_g, L0_attn_ln2_b, L0_attn_w1, L0_attn_b1, L0_attn_w2, L0_attn_b2, L0_ffn_Wg, L0_ffn_W1, L0_ffn_b1, L0_ffn_W2, L0_ffn_b2):
    import jax
    import jax.numpy as jnp

    def _L0_tok_ref(input_seq, emb, wk, bk, wq, bq, wv, bv, ln_g, ln_b, w1, b1, w2, b2):
        import jax, jax.numpy as jnp
        import numpy as np
        import math
        V, S, D, B = (50257, 512, 128, 4)
        DFF = 4 * D
        EPS = 1e-05

        def layer_norm(z, g, b):
            mu = jnp.mean(z, axis=-1, keepdims=True)
            var = jnp.mean((z - mu) ** 2, axis=-1, keepdims=True)
            return (z - mu) * jax.lax.rsqrt(var + EPS) * g + b

        def pos_embedding(seq_len, d_model):
            pos = jnp.arange(seq_len, dtype=jnp.float32)[:, None]
            i = jnp.arange(d_model, dtype=jnp.float32)[None, :]
            ang = pos / jnp.power(10000.0, 2.0 * i / d_model)
            even = (jnp.arange(d_model) % 2 == 0)[None, :]
            return jnp.where(even, jnp.sin(ang), jnp.cos(ang))
        x = emb[input_seq]
        x = (x + pos_embedding(S, D)) * math.sqrt(D)
        k = x @ wk + bk
        q = x @ wq + bq
        v = x @ wv + bv
        scores = jnp.einsum('bid,bjd->bij', k, q) / math.sqrt(D)
        attn = jax.nn.softmax(scores, axis=-1) @ v
        r = layer_norm(x + attn, ln_g, ln_b)
        ff = jax.nn.gelu(r @ w1 + b1, approximate=False) @ w2 + b2
        out = layer_norm(r + ff, ln_g, ln_b)
        return out

    def _L0_attn_ref(x, ln1_g, ln1_b, wq, wk, wv, wo, bo, ln2_g, ln2_b, w1, b1, w2, b2):
        import jax, jax.numpy as jnp
        import numpy as np
        DEPTH, DIM, HEADS, SEQ, BATCH = (4, 128, 8, 1024, 2)
        DH = DIM // HEADS
        BUCKET = 64
        FF = 4 * DIM
        EPS_ATTN = 0.001
        EPS_LN = 1e-05

        def layer_norm(x, g, b):
            mu = jnp.mean(x, axis=-1, keepdims=True)
            var = jnp.mean(jnp.square(x - mu), axis=-1, keepdims=True)
            return (x - mu) * jax.lax.rsqrt(var + EPS_LN) * g + b

        def causal_linear_attn(q, k, v, bucket_size=BUCKET, eps=EPS_ATTN):
            b, h, n, e = q.shape
            q = jax.nn.softmax(q, axis=-1) * e ** (-0.5)
            k = jnp.exp(k)
            bucket = lambda t: t.reshape(b, h, n // bucket_size, bucket_size, e)
            b_q, b_k, b_v = (bucket(q), bucket(k), bucket(v))
            b_k_cumsum = jnp.cumsum(b_k.sum(axis=-2), axis=-2)
            context = jnp.cumsum(jnp.einsum('bhund,bhune->bhude', b_k, b_v), axis=2)
            if bucket_size > 1:
                context = jnp.pad(context, ((0, 0), (0, 0), (1, 0), (0, 0), (0, 0)))[:, :, :-1]
                b_k_cumsum = jnp.pad(b_k_cumsum, ((0, 0), (0, 0), (1, 0), (0, 0)))[:, :, :-1]
            D = jnp.einsum('bhud,bhund->bhun', b_k_cumsum, b_q)
            D_inv = 1.0 / jnp.clip(D, eps, None)
            out = jnp.einsum('bhund,bhude,bhun->bhune', b_q, context, D_inv)
            return out.reshape(b, h, n, e)
        b, n, d = x.shape
        split = lambda t: t.reshape(b, n, HEADS, DH).transpose(0, 2, 1, 3)
        for i in range(DEPTH):
            h = layer_norm(x, ln1_g[i], ln1_b[i])
            q, k, v = (split(h @ wq[i]), split(h @ wk[i]), split(h @ wv[i]))
            att = causal_linear_attn(q, k, v)
            att = att.transpose(0, 2, 1, 3).reshape(b, n, d)
            x = x + (att @ wo[i] + bo[i])
            h = layer_norm(x, ln2_g[i], ln2_b[i])
            x = x + (jax.nn.gelu(h @ w1[i] + b1[i], approximate=False) @ w2[i] + b2[i])
        return x

    def _L0_ffn_ref(x, Wg, W1, b1, W2, b2):
        import jax, jax.numpy as jnp
        import numpy as np
        K = 2
        logits = jnp.einsum('btd,de->bte', x, Wg)
        probs = jax.nn.softmax(logits, axis=-1)
        top_p, _top_i = jax.lax.top_k(probs, K)
        top_p = top_p / jnp.sum(top_p, axis=-1, keepdims=True)
        b2_sum = jnp.sum(b2, axis=0)
        out = jnp.zeros_like(x)
        for i in range(K):
            w_in = x * top_p[..., i:i + 1]
            h = jax.nn.gelu(jnp.einsum('btd,edf->ebtf', w_in, W1) + b1[:, None, None, :], approximate=False)
            out = out + jnp.einsum('ebtf,efd->btd', h, W2) + b2_sum
        return out
    h = _L0_tok_ref(x, L0_tok_emb, L0_tok_wk, L0_tok_bk, L0_tok_wq, L0_tok_bq, L0_tok_wv, L0_tok_bv, L0_tok_ln_g, L0_tok_ln_b, L0_tok_w1, L0_tok_b1, L0_tok_w2, L0_tok_b2)
    h = h + _L0_attn_ref(_layernorm(h, axis=-1), L0_attn_ln1_g, L0_attn_ln1_b, L0_attn_wq, L0_attn_wk, L0_attn_wv, L0_attn_wo, L0_attn_bo, L0_attn_ln2_g, L0_attn_ln2_b, L0_attn_w1, L0_attn_b1, L0_attn_w2, L0_attn_b2)
    h = h + _L0_ffn_ref(_layernorm(h, axis=-1), L0_ffn_Wg, L0_ffn_W1, L0_ffn_b1, L0_ffn_W2, L0_ffn_b2)
    return h

_drawn_inputs = setup_inputs


def setup_inputs(seed=0):
    import zlib

    import numpy as np

    out = dict(_drawn_inputs(seed))
    spreads = {'L0_tok_bk': (0.0, 2.0),
     'L0_tok_bq': (0.0, 2.0),
     'L0_tok_bv': (0.0, 0.607),
     'L0_tok_ln_g': (1.0, 0.2),
     'L0_tok_ln_b': (0.0, 0.1),
     'L0_tok_b1': (0.0, 0.404),
     'L0_tok_b2': (0.0, 0.1),
     'L0_attn_ln1_g': (1.0, 0.6),
     'L0_attn_ln1_b': (0.0, 0.8),
     'L0_attn_bo': (0.0, 0.1),
     'L0_attn_ln2_g': (1.0, 0.6),
     'L0_attn_ln2_b': (0.0, 0.8),
     'L0_attn_b1': (0.0, 0.336),
     'L0_attn_b2': (0.0, 0.1),
     'L0_ffn_b1': (0.0, 0.1),
     'L0_ffn_b2': (0.0, 0.1)}
    factors = {'L0_attn_wq': 33.171, 'L0_attn_wk': 27.69, 'L0_ffn_Wg': 64.0}
    for name, (base, spread) in spreads.items():
        noise = np.random.default_rng([zlib.crc32(name.encode()), seed]).standard_normal(out[name].shape)
        drawn = base * np.exp(spread * noise) if base else spread * noise
        out[name] = jnp.asarray(drawn.astype(out[name].dtype))
    for name, factor in factors.items():
        out[name] = (out[name] * factor).astype(out[name].dtype)
    return out
```

```python
from contextlib import ExitStack

import numpy as np

import concourse.bass as bass
from concourse import mybir

P = 128
B = 8
S = 512
T = S // P
PAIRS = B // 2
LAYERS = 4
HEADS = 8
DH = P // HEADS
BUCKET = 64
NB = S // BUCKET
FF = 512
J = FF // P
E = 8
CW = P + HEADS
EPS_LN = 1e-5
EPS_ATTN = 1e-3
LA_COLS = 4 * P + 2
F_COLS = 2 * FF + 2 + J + 1

DVE_STEPS = dict(ta=10, tf=22, la=18, lf=8, mg=16)
POOL_STEPS = dict(ta=4, tf=8, la=12, lf=2, mg=2)


class Steps:

    def __init__(self, eng, sem, base, per):
        self.eng, self.sem, self.base, self.per, self.n = eng, sem, base, per, 0

    def done(self, ins):
        self.n += 1
        ins.then_inc(self.sem, 1)
        self.eng.wait_ge(self.sem, self.base + self.n)

    def close(self):
        assert self.n == self.per, (self.n, self.per)


def build(nc, ids, emb, pos, consts, tok_w, tok_rows, attn_w, attn_bo, ffn_w, moe_w, moe_c, out):
    ACT = mybir.ActivationFunctionType
    ALU = mybir.AluOpType
    AX = mybir.AxisListType
    F32 = mybir.dt.float32
    I32 = mybir.dt.int32
    U32 = mybir.dt.uint32
    ctx = ExitStack()
    with ctx:
        def sb(name, shape, dt=F32):
            return ctx.enter_context(nc.sbuf_tensor(name, shape, dt))

        def sem(name):
            return ctx.enter_context(nc.semaphore(name))

        def sem2(name):
            return [sem(f"{name}_{s}") for s in range(2)]

        x = sb("x", [P, B * T, P])
        h_tok = sb("h_tok", [P, B * T, P])
        mean = sb("mean", [P, B * T])
        rstd = sb("rstd", [P, B * T])
        idx = sb("idx", [P, B * T], I32)
        pos_sb = sb("pos_sb", [P, T, P])
        con = sb("con", [P, P + CW])
        ident = con[:, 0:P]
        head_mask = con[:, P:P + CW]
        w_tok = sb("w_tok", [P, 3 * P + 2])
        rows = sb("rows", [P, 3, P])
        w_la = sb("w_la", [P, LA_COLS])
        bo = sb("bo", [P, P])
        w_f = sb("w_f", [P, F_COLS])
        w_moe = sb("w_moe", [P, E, 2 * FF])
        c_moe = sb("c_moe", [P, E + J * E + E])
        scratch = sb("scratch", [P, 1])
        b2_sum = sb("b2_sum", [P, 1])
        b2_twice = sb("b2_twice", [P, 1])
        eps_t = sb("eps_t", [P, T])
        mhalf_t = sb("mhalf_t", [P, T])

        n = [sb(f"n{s}", [P, T, P]) for s in range(2)]
        hT = [sb(f"hT{s}", [P, S]) for s in range(2)]
        nrm = [sb(f"nrm{s}", [P, T, P]) for s in range(2)]
        aff = [sb(f"aff{s}", [P, T, P]) for s in range(2)]
        st = [sb(f"st{s}", [P, T, 6]) for s in range(2)]
        st_sum = [sb(f"st_sum{s}", [P, T]) for s in range(2)]
        st_dif = [sb(f"st_dif{s}", [P, T]) for s in range(2)]
        st_m2 = [sb(f"st_m2{s}", [P, T]) for s in range(2)]
        st_dd = [sb(f"st_dd{s}", [P, T]) for s in range(2)]
        st_mean = [sb(f"st_mean{s}", [P, T]) for s in range(2)]
        st_var = [sb(f"st_var{s}", [P, T]) for s in range(2)]
        st_ve = [sb(f"st_ve{s}", [P, T]) for s in range(2)]
        st_rs = [sb(f"st_rs{s}", [P, T]) for s in range(2)]

        kT = [sb(f"kT{s}", [P, S]) for s in range(2)]
        qT = [sb(f"qT{s}", [P, S]) for s in range(2)]
        v = [sb(f"v{s}", [P, T, CW]) for s in range(2)]
        pr = [[sb(f"pr{s}{i}", [P, S]) for i in range(2)] for s in range(2)]
        prT = [[sb(f"prT{s}{i}", [P, T, P]) for i in range(2)] for s in range(2)]
        nmax = [sb(f"nmax{s}", [P, T]) for s in range(2)]
        psums = [sb(f"psums{s}", [P, T]) for s in range(2)]
        rsum = [sb(f"rsum{s}", [P, T]) for s in range(2)]

        ek = [sb(f"ek{s}", [P, T, P]) for s in range(2)]
        qs = [pr[s][0] for s in range(2)]
        eq = [pr[s][1] for s in range(2)]
        qmax = [sb(f"qmax{s}", [P, T * HEADS]) for s in range(2)]
        qsum = [sb(f"qsum{s}", [P, T * HEADS]) for s in range(2)]
        qeps = [sb(f"qeps{s}", [P, T * HEADS]) for s in range(2)]
        den = [sb(f"den{s}", [P, T * HEADS]) for s in range(2)]
        rden = [sb(f"rden{s}", [P, T * HEADS]) for s in range(2)]
        cm = [sb(f"cm{s}", [P, NB - 1, CW]) for s in range(2)]
        zero_ctx = sb("zero_ctx", [P, CW])
        att = [sb(f"att{s}", [P, T, P]) for s in range(2)]
        aT = [kT[s] for s in range(2)]

        g = [sb(f"g{i}", [P, S]) for i in range(3)]
        yT = [sb(f"yT{s}", [P, S]) for s in range(2)]

        x1T = sb("x1T", [P, B * S])
        rb = sb("rb", [P, B * S])
        lg = [sb(f"lg{s}", [P, T, E]) for s in range(2)]
        top = [sb(f"top{s}", [P, T, 8]) for s in range(2)]
        gap = [sb(f"gap{s}", [P, T]) for s in range(2)]
        ratio = [sb(f"ratio{s}", [P, T]) for s in range(2)]
        gden = [sb(f"gden{s}", [P, T]) for s in range(2)]
        p1 = [sb(f"p1{s}", [P, T]) for s in range(2)]
        z2 = [hT[i] for i in range(2)]
        g1 = [pr[0][0], pr[0][1]]
        g2 = [pr[1][0], pr[1][1]]
        hid = [kT[0], kT[1], qT[0], qT[1]]

        ps = ctx.enter_context(nc.psum_tensor("ps", [P, 8, 512], F32))

        def bank(i):
            return ps[:, i, :]

        TB = [0, 1]
        UB = [[2, 3, 4], [5, 6, 7]]
        QB, KVB, GB = 2, [3, 4], [5, 6, 7]
        ZB, YB = [2, 3, 4, 5], [6, 7]

        d_idx, d_con, d_tok, d_rows, d_pos = (sem(f"d_{k}") for k in ("idx", "con", "tok", "rows", "pos"))
        d_la, d_bo, d_f, d_moe, d_cmoe, d_gather, d_out = (
            sem(f"d_{k}") for k in ("la", "bo", "f", "moe", "cmoe", "gather", "out"))
        setup_pool, setup_dve = sem("setup_pool"), sem("setup_dve")
        dve_steps = {k: sem(f"dve_steps_{k}") for k in ("su", *DVE_STEPS)}
        pool_steps = {k: sem(f"pool_steps_{k}") for k in POOL_STEPS}
        stats_ready, ln_rstd, next_rstd = sem2("stats_ready"), sem2("ln_rstd"), sem2("next_rstd")
        nrm_ready = sem2("nrm_ready")
        n_ready, nT_ps, hT_ready, t_free = sem2("n_ready"), sem2("nT_ps"), sem2("hT_ready"), sem2("t_free")
        tok_x, tok_xbv, tok_xT_ps, tok_xT = sem2("tok_x"), sem2("tok_xbv"), sem2("tok_xT_ps"), sem2("tok_xT")
        tok_kqv_ps, tok_kT, tok_qT, tok_v = sem2("tok_kqv_ps"), sem2("tok_kT"), sem2("tok_qT"), sem2("tok_v")
        tok_s_ps, tok_max, tok_p, tok_pT_ps, tok_pT, tok_o_ps, tok_r = (
            sem2(f"tok_{k}") for k in ("s_ps", "max", "p", "pT_ps", "pT", "o_ps", "r"))
        q_ps, kv_ps, qs_ready, v_ready, eq_ready, g_ps, qT_ps, qT_ready = (
            sem2(k) for k in ("q_ps", "kv_ps", "qs_ready", "v_ready", "eq_ready", "g_ps", "qT_ps", "qT_ready"))
        cm_ready, ctx_ready, o_ps, att_ready, aT_ps, aT_ready, wo_ps, bo_added = (
            sem2(k) for k in ("cm_ready", "ctx_ready", "o_ps", "att_ready", "aT_ps", "aT_ready", "wo_ps", "bo_added"))
        z_ps, g_ready, y_ps, yT_ready, yT_ps = sem("z_ps"), sem("g_ready"), sem2("y_ps"), sem2("yT_ready"), sem2("yT_ps")
        h_aff = sem2("h_aff")
        gx_ready, gxT_ps, gxT, gl_ps, gap_ready, ratio_ready, xs_ready, xs_ps, xs_done = (
            sem2(k) for k in ("gx_ready", "gxT_ps", "gxT", "gl_ps", "gap_ready", "ratio_ready", "xs_ready", "xs_ps",
                              "xs_done"))
        mz_ps, mz2_ready, mg_ready, mh_ready, my_ps, myT_ready, myT_ps, out_ready = (
            sem(k) for k in ("mz_ps", "mz2_ready", "mg_ready", "mh_ready", "my_ps", "myT_ready", "myT_ps",
                             "out_ready"))

        def tiles(pair, s):
            return bass.ds(pair * (2 * T) + s * T, T)

        def transposes(pe, dst, src_tile):
            for t in range(T):
                last = pe.transpose(bank(dst)[:, t * P:(t + 1) * P], src_tile(t), ident)
            return last

        block = ctx.enter_context(nc.Block())

        @block.sync
        def _(sp):
            sp.dma_start(idx[:, :], ids).then_inc(d_idx, 16)
            sp.dma_start(con[:, :], consts).then_inc(d_con, 16)
            sp.dma_start(pos_sb[:, :, :], pos).then_inc(d_pos, 16)
            sp.dma_start(w_tok[:, :], tok_w).then_inc(d_tok, 16)
            sp.dma_start(rows[:, :, :], tok_rows.partition_broadcast(P)).then_inc(d_rows, 16)
            sp.dma_start(w_f[:, :], ffn_w[0]).then_inc(d_f, 16)
            sp.dma_start(w_la[:, :], attn_w[0]).then_inc(d_la, 16)
            sp.dma_start(bo[:, :], attn_bo[0].partition_broadcast(P)).then_inc(d_bo, 16)
            sp.dma_start(c_moe[:, :], moe_c).then_inc(d_cmoe, 16)
            sp.dma_start(w_moe[:, :, :], moe_w).then_inc(d_moe, 16)
            with sp.Fori(0, LAYERS - 1) as l:
                sp.wait_ge(yT_ready[1], PAIRS * l + PAIRS)
                sp.dma_start(w_f[:, :], ffn_w[bass.ds(l + 1, 1)].rearrange("a p c -> (a p) c")).then_inc(d_f, 16)
                sp.wait_ge(wo_ps[1], PAIRS * l + PAIRS)
                sp.dma_start(w_la[:, :], attn_w[bass.ds(l + 1, 1)].rearrange("a p c -> (a p) c")).then_inc(d_la, 16)
                sp.wait_ge(bo_added[0], PAIRS * l + PAIRS)
                sp.wait_ge(bo_added[1], PAIRS * l + PAIRS)
                sp.dma_start(bo[:, :], attn_bo[bass.ds(l + 1, 1)].rearrange("a d -> (a d)").partition_broadcast(P)
                             ).then_inc(d_bo, 16)
            sp.wait_ge(yT_ready[1], PAIRS * LAYERS)
            sp.dma_start(w_f[:, :], ffn_w[LAYERS]).then_inc(d_f, 16)
            with sp.Fori(0, B) as b:
                sp.wait_ge(out_ready, b + 1)
                sp.dma_start(out[bass.ds(b, 1)].rearrange("b (t p) d -> p (b t) d", p=P),
                             h_tok[:, bass.ds(b * T, T), :]).then_inc(d_out, 16)
            sp.wait_ge(d_out, 16 * B)

        @block.gpsimd
        def _(pool):
            def pool_rstd(stp, s, count, dst, done):
                pool.wait_ge(stats_ready[s], count)
                stp.done(pool.tensor_tensor(st_ve[s][:, :], st_var[s][:, :], eps_t[:, :], ALU.add))
                pool.tensor_tensor(dst, st_ve[s][:, :], mhalf_t[:, :], ALU.pow).then_inc(done[s], 1)

            def affine(stp, s, dst, done):
                gain = rows[:, 1, :].unsqueeze(1).broadcast_to([P, T, P])
                bias = rows[:, 2, :].unsqueeze(1).broadcast_to([P, T, P])
                stp.done(pool.tensor_tensor(aff[s][:, :, :], aff[s][:, :, :], gain, ALU.mult))
                pool.tensor_tensor(dst, aff[s][:, :, :], bias, ALU.add).then_inc(done[s], 1)

            pool.wait_ge(d_idx, 16)
            for p in range(PAIRS):
                if p >= 2:
                    pool.wait_ge(d_gather, 16 * 2 * T * p)
                for t in range(2 * T * p, 2 * T * (p + 1)):
                    if p == 1 and t == 2 * T:
                        pool.wait_ge(d_gather, 16 * 2 * T)
                    pool.indirect_dma_start(x[:, t, :], None, emb,
                                            bass.IndirectOffsetOnAxis(ap=idx[:, t:t + 1], axis=0)).then_inc(d_gather, 16)
                if p == 0:
                    pool.memset(eps_t[:, :], EPS_LN).then_inc(setup_pool, 1)
                    pool.memset(mhalf_t[:, :], -0.5).then_inc(setup_pool, 1)
                    for q in range(PAIRS):
                        for s in range(2):
                            a = (2 * q + s) * T
                            pool.memset(mean[:, a:a + T], 0.0).then_inc(setup_pool, 1)
                            pool.memset(rstd[:, a:a + T], 1.0).then_inc(next_rstd[s], 1)
                    pool.wait_ge(setup_pool, 2 + 2 * PAIRS)
            pool.wait_ge(d_rows, 16)

            with pool.Fori(0, PAIRS) as pair:
                stp = Steps(pool, pool_steps["ta"], pair * POOL_STEPS["ta"], POOL_STEPS["ta"])
                for s in range(2):
                    pool.wait_ge(tok_x[s], pair + 1)
                    pool.tensor_tensor(nrm[s][:, :, :], n[s][:, :, :],
                                       rows[:, 0, :].unsqueeze(1).broadcast_to([P, T, P]),
                                       ALU.add).then_inc(tok_xbv[s], 1)
                for s in range(2):
                    pool_rstd(stp, s, pair + 1, st_rs[s][:, :], ln_rstd)
                for s in range(2):
                    pool.wait_ge(nrm_ready[s], pair + 1)
                    affine(stp, s, x[:, tiles(pair, s), :], tok_r)
                stp.close()

            with pool.Fori(0, PAIRS) as pair:
                stp = Steps(pool, pool_steps["tf"], pair * POOL_STEPS["tf"], POOL_STEPS["tf"])
                for s in range(2):
                    pool_rstd(stp, s, PAIRS + 3 * pair + 1, st_rs[s][:, :], ln_rstd)
                    pool.wait_ge(nrm_ready[s], PAIRS + pair + 1)
                    affine(stp, s, h_tok[:, tiles(pair, s), :], h_aff)
                    pool_rstd(stp, s, PAIRS + 3 * pair + 2, st_rs[s][:, :], ln_rstd)
                    pool_rstd(stp, s, PAIRS + 3 * pair + 3, rstd[:, tiles(pair, s)], next_rstd)
                stp.close()

            with pool.Fori(0, LAYERS) as layer:
                with pool.Fori(0, PAIRS) as pair:
                    a = layer * PAIRS + pair
                    k = layer * (2 * PAIRS) + pair + PAIRS
                    stp = Steps(pool, pool_steps["la"], a * POOL_STEPS["la"], POOL_STEPS["la"])
                    pool.wait_ge(d_bo, layer * 16 + 16)
                    for s in range(2):
                        pool.wait_ge(n_ready[s], k + 1)
                        xs_ = x[:, tiles(pair, s), :]
                        pool.tensor_tensor(xs_, xs_, bo[:, :].unsqueeze(1).broadcast_to([P, T, P]),
                                           ALU.add).then_inc(bo_added[s], 1)
                    for s in range(2):
                        pool.wait_ge(cm_ready[s], a + 1)
                        for u in range(1, NB - 1):
                            ins = pool.tensor_tensor(cm[s][:, u, :], cm[s][:, u - 1, :], cm[s][:, u, :], ALU.add)
                            if u < NB - 2:
                                stp.done(ins)
                        ins.then_inc(ctx_ready[s], 1)
                    for s in range(2):
                        pool_rstd(stp, s, k + 13, rstd[:, tiles(pair, s)], next_rstd)
                    stp.close()
                with pool.Fori(0, PAIRS) as pair:
                    a = layer * PAIRS + pair
                    k = layer * (2 * PAIRS) + pair + 2 * PAIRS
                    stp = Steps(pool, pool_steps["lf"], a * POOL_STEPS["lf"], POOL_STEPS["lf"])
                    for s in range(2):
                        pool_rstd(stp, s, k + 13, rstd[:, tiles(pair, s)], next_rstd)
                    stp.close()

            with pool.Fori(0, PAIRS) as pair:
                stp = Steps(pool, pool_steps["mg"], pair * POOL_STEPS["mg"], POOL_STEPS["mg"])
                for s in range(2):
                    pool_rstd(stp, s, pair + (4 * PAIRS + 2 * LAYERS * PAIRS + 1), st_rs[s][:, :], ln_rstd)
                stp.close()

        @block.vector
        def _(dve):
            def carry_wait():
                dve.memset(scratch[:, :], 0.0)

            def stats(stp, s, src, mean_dst, count, first=None):
                carry_wait()
                for t in range(T):
                    ins = dve.bn_stats(st[s][:, t, :], src(t))
                    if t == 0 and first is not None:
                        ins.then_inc(first, 1)
                stp.done(ins)
                dve.tensor_tensor(st_sum[s][:, :], st[s][:, :, 1], st[s][:, :, 4], ALU.add)
                dve.tensor_tensor(st_dif[s][:, :], st[s][:, :, 1], st[s][:, :, 4], ALU.subtract)
                stp.done(dve.tensor_tensor(st_m2[s][:, :], st[s][:, :, 2], st[s][:, :, 5], ALU.add))
                dve.tensor_scalar(mean_dst, st_sum[s][:, :], 0.5, None, ALU.mult)
                stp.done(dve.scalar_tensor_tensor(st_dd[s][:, :], st_dif[s][:, :], 0.25, st_dif[s][:, :],
                                                  ALU.mult, ALU.mult))
                if count is not None:
                    dve.wait_ge(next_rstd[s], count)
                dve.scalar_tensor_tensor(st_var[s][:, :], st_m2[s][:, :], 1.0 / P, st_dd[s][:, :],
                                         ALU.mult, ALU.add).then_inc(stats_ready[s], 1)

            def normalise(dst, src, mean_of, rstd_of):
                for t in range(T):
                    ins = dve.tensor_scalar(dst(t), src(t), mean_of(t), rstd_of(t), ALU.subtract, ALU.mult)
                return ins

            def one(tensor, pair, s, t):
                at = bass.ds(pair * (2 * T) + (s * T + t), 1)
                if len(tensor.shape) == 2:
                    return tensor[:, at]
                return tensor[:, at, :].rearrange("p a d -> p (a d)")

            def prepare(pair, k):
                nxt = (pair + 1) % PAIRS
                for s in range(2):
                    dve.wait_ge(nT_ps[s], k + 1)
                    dve.wait_ge(next_rstd[s], k + 2)
                    normalise(lambda t: n[s][:, t, :], lambda t: one(x, nxt, s, t),
                              lambda t: one(mean, nxt, s, t), lambda t: one(rstd, nxt, s, t)
                              ).then_inc(n_ready[s], 1)

            def inner(s):
                return lambda t: st_mean[s][:, t:t + 1], lambda t: st_rs[s][:, t:t + 1]

            dve.memset(zero_ctx[:, :], 0.0).then_inc(setup_dve, 1)
            dve.wait_ge(d_cmoe, 16)
            dve.tensor_reduce(b2_sum[:, :], c_moe[:, E + J * E:], AX.X, ALU.add).then_inc(dve_steps["su"], 1)
            dve.wait_ge(dve_steps["su"], 1)
            dve.tensor_scalar(b2_twice[:, :], b2_sum[:, :], 2.0, None, ALU.mult).then_inc(setup_dve, 1)
            dve.wait_ge(d_pos, 16)
            dve.wait_ge(d_tok, 16)

            with dve.Fori(0, PAIRS) as pair:
                stp = Steps(dve, dve_steps["ta"], pair * DVE_STEPS["ta"], DVE_STEPS["ta"])
                dve.wait_ge(d_gather, pair * (16 * 2 * T) + 16 * 2 * T)
                for s in range(2):
                    dve.scalar_tensor_tensor(n[s][:, :, :], x[:, tiles(pair, s), :], float(P) ** 0.5, pos_sb[:, :, :],
                                             ALU.mult, ALU.add).then_inc(tok_x[s], 1)
                for s in range(2):
                    dve.wait_ge(tok_kqv_ps[s], pair * 3 + 2)
                    dve.tensor_scalar(qT[s][:, :], bank(UB[s][1]), w_tok[:, 3 * P + 1:3 * P + 2], float(P) ** -0.5,
                                      ALU.add, ALU.mult).then_inc(tok_qT[s], 1)
                for i in range(T + 1):
                    for s in range(2):
                        if i < T:
                            dve.wait_ge(tok_s_ps[s], pair * T + (i + 1))
                            dve.tensor_reduce(nmax[s][:, i:i + 1], bank(UB[s][i % 2]), AX.X, ALU.max,
                                              negate=True).then_inc(tok_max[s], 1)
                    for s in range(2):
                        if i >= 1:
                            dve.wait_ge(tok_pT_ps[s], pair * T + i)
                            dve.tensor_copy(prT[s][(i - 1) % 2][:, :, :],
                                            bank(TB[s]).rearrange("p (t q) -> p t q", t=T)).then_inc(tok_pT[s], 1)
                for s in range(2):
                    stp.done(dve.reciprocal(rsum[s][:, :], psums[s][:, :]))
                    dve.wait_ge(tok_o_ps[s], pair + 1)
                    dve.wait_ge(tok_xbv[s], pair + 1)
                    for t in range(T):
                        ins = dve.scalar_tensor_tensor(nrm[s][:, t, :], bank(UB[s][2])[:, t * P:(t + 1) * P],
                                                       rsum[s][:, t:t + 1], nrm[s][:, t, :], ALU.mult, ALU.add)
                    stp.done(ins)
                    stats(stp, s, lambda t: nrm[s][:, t, :], st_mean[s][:, :], None)
                for s in range(2):
                    dve.wait_ge(ln_rstd[s], pair + 1)
                    normalise(lambda t: aff[s][:, t, :], lambda t: nrm[s][:, t, :], *inner(s)
                              ).then_inc(nrm_ready[s], 1)
                stp.close()

            for s in range(2):
                dve.memset(v[s][:, :, P:CW], 1.0).then_inc(t_free[s], 1)
                dve.wait_ge(tok_r[s], PAIRS)
                dve.wait_ge(next_rstd[s], 1)
                normalise(lambda t: n[s][:, t, :], lambda t: x[:, s * T + t, :],
                          lambda t: mean[:, s * T + t:s * T + t + 1], lambda t: rstd[:, s * T + t:s * T + t + 1]
                          ).then_inc(n_ready[s], 1)

            with dve.Fori(0, PAIRS) as pair:
                stp = Steps(dve, dve_steps["tf"], pair * DVE_STEPS["tf"], DVE_STEPS["tf"])
                prepare(pair, pair)
                for s in range(2):
                    dve.wait_ge(yT_ps[s], pair + 1)
                    stp.done(dve.tensor_tensor(nrm[s][:, :, :], bank(TB[s]).rearrange("p (t q) -> p t q", t=T),
                                               x[:, tiles(pair, s), :], ALU.add))
                    stats(stp, s, lambda t: nrm[s][:, t, :], st_mean[s][:, :], pair + PAIRS, t_free[s])
                    dve.wait_ge(ln_rstd[s], pair * 2 + (PAIRS + 1))
                    normalise(lambda t: aff[s][:, t, :], lambda t: nrm[s][:, t, :], *inner(s)
                              ).then_inc(nrm_ready[s], 1)
                    dve.wait_ge(h_aff[s], pair + 1)
                    stats(stp, s, lambda t: one(h_tok, pair, s, t), st_mean[s][:, :], None)
                    dve.wait_ge(ln_rstd[s], pair * 2 + (PAIRS + 2))
                    stp.done(normalise(lambda t: one(x, pair, s, t), lambda t: one(h_tok, pair, s, t), *inner(s)))
                    stats(stp, s, lambda t: one(x, pair, s, t), mean[:, tiles(pair, s)], None)
                stp.close()

            def tail(stp, s, pair, k):
                xs_ = x[:, tiles(pair, s), :]
                stp.done(dve.tensor_tensor(xs_, bank(TB[s]).rearrange("p (t q) -> p t q", t=T), xs_, ALU.add))
                stats(stp, s, lambda t: one(x, pair, s, t), mean[:, tiles(pair, s)], k + PAIRS, t_free[s])

            with dve.Fori(0, LAYERS) as layer:
                with dve.Fori(0, PAIRS) as pair:
                    a = layer * PAIRS + pair
                    k = layer * (2 * PAIRS) + pair + PAIRS
                    stp = Steps(dve, dve_steps["la"], a * DVE_STEPS["la"], DVE_STEPS["la"])
                    prepare(pair, k)
                    for s in range(2):
                        dve.wait_ge(q_ps[s], a + 1)
                        q = bank(QB).rearrange("p (g d) -> p g d", d=DH)
                        stp.done(dve.tensor_reduce(qmax[s][:, :], q, AX.X, ALU.max))
                        dve.tensor_tensor(qs[s][:, :].rearrange("p (g d) -> p g d", d=DH), q,
                                          qmax[s][:, :].unsqueeze(2).broadcast_to([P, T * HEADS, DH]),
                                          ALU.subtract).then_inc(qs_ready[s], 1)
                    for s in range(2):
                        dve.wait_ge(eq_ready[s], a + 1)
                        stp.done(dve.tensor_reduce(qsum[s][:, :], eq[s][:, :].rearrange("p (g d) -> p g d", d=DH),
                                                   AX.X, ALU.add))
                        stp.done(dve.tensor_scalar(qeps[s][:, :], qsum[s][:, :], EPS_ATTN * float(DH) ** 0.5, None,
                                                   ALU.mult))
                        dve.wait_ge(g_ps[s], a + 1)
                        for r in range(2):
                            dve.tensor_tensor(cm[s][:, r:NB - 2:2, :],
                                              bank(GB[r])[:, 0:3 * CW].rearrange("p (u c) -> p u c", c=CW),
                                              head_mask.unsqueeze(1).broadcast_to([P, 3, CW]), ALU.mult)
                        dve.tensor_tensor(cm[s][:, NB - 2, :], bank(GB[2])[:, 0:CW], head_mask,
                                          ALU.mult).then_inc(cm_ready[s], 1)
                    for s in range(2):
                        dve.wait_ge(o_ps[s], a + 1)
                        for i in range(2):
                            o = bank(KVB[i])[:, 0:2 * CW].rearrange("p (t c) -> p t c", c=CW)
                            w = slice(2 * i * HEADS, 2 * (i + 1) * HEADS)
                            ins = dve.tensor_tensor(den[s][:, w].rearrange("p (t h) -> p t h", h=HEADS), o[:, :, P:CW],
                                                    qeps[s][:, w].rearrange("p (t h) -> p t h", h=HEADS), ALU.max)
                        stp.done(ins)
                        stp.done(dve.reciprocal(rden[s][:, :], den[s][:, :]))
                        for t in range(T):
                            o = bank(KVB[t // 2])[:, (t % 2) * CW:(t % 2) * CW + P].rearrange("p (h d) -> p h d", d=DH)
                            ins = dve.tensor_tensor(att[s][:, t, :].rearrange("p (h d) -> p h d", d=DH), o,
                                                    rden[s][:, t * HEADS:(t + 1) * HEADS].unsqueeze(2)
                                                    .broadcast_to([P, HEADS, DH]), ALU.mult)
                        ins.then_inc(att_ready[s], 1)
                    for s in range(2):
                        dve.wait_ge(wo_ps[s], a + 1)
                        dve.wait_ge(bo_added[s], a + 1)
                        tail(stp, s, pair, k)
                    stp.close()
                with dve.Fori(0, PAIRS) as pair:
                    a = layer * PAIRS + pair
                    k = layer * (2 * PAIRS) + pair + 2 * PAIRS
                    stp = Steps(dve, dve_steps["lf"], a * DVE_STEPS["lf"], DVE_STEPS["lf"])
                    prepare(pair, k)
                    for s in range(2):
                        dve.wait_ge(yT_ps[s], a + (PAIRS + 1))
                        tail(stp, s, pair, k)
                    stp.close()

            dve.wait_ge(n_ready[0], 1)
            for s in range(2):
                dve.wait_ge(next_rstd[s], 2 * PAIRS + 2 * LAYERS * PAIRS)
            with dve.Fori(0, PAIRS) as pair:
                stp = Steps(dve, dve_steps["mg"], pair * DVE_STEPS["mg"], DVE_STEPS["mg"])
                for s in range(2):
                    hs = h_tok[:, tiles(pair, s), :]
                    stp.done(dve.tensor_tensor(hs, hs, x[:, tiles(pair, s), :], ALU.add))
                    stats(stp, s, lambda t: one(h_tok, pair, s, t), st_mean[s][:, :], None)
                for s in range(2):
                    dve.wait_ge(ln_rstd[s], pair + (3 * PAIRS + 1))
                    normalise(lambda t: n[s][:, t, :], lambda t: one(h_tok, pair, s, t), *inner(s)
                              ).then_inc(gx_ready[s], 1)
                for s in range(2):
                    dve.wait_ge(gl_ps[s], pair + 1)
                    lg_ins = dve.tensor_copy(lg[s][:, :, :], bank(2 + s)[:, 0:T * E].rearrange("p (t e) -> p t e", e=E))
                    stp.done(lg_ins)
                    carry_wait()
                    for t in range(T):
                        ins = dve.max(top[s][:, t, :], lg[s][:, t, :])
                    stp.done(ins)
                    dve.tensor_tensor(gap[s][:, :], top[s][:, :, 1], top[s][:, :, 0],
                                      ALU.subtract).then_inc(gap_ready[s], 1)
                for s in range(2):
                    dve.wait_ge(ratio_ready[s], pair + 1)
                    stp.done(dve.tensor_scalar(gden[s][:, :], ratio[s][:, :], 1.0, None, ALU.add))
                    stp.done(dve.reciprocal(p1[s][:, :], gden[s][:, :]))
                    dve.tensor_tensor(nrm[s][:, :, :], n[s][:, :, :], p1[s][:, :].unsqueeze(2).broadcast_to([P, T, P]),
                                      ALU.mult)
                    dve.tensor_copy(aff[s][:, :, :], ratio[s][:, :].unsqueeze(2).broadcast_to([P, T, P])
                                    ).then_inc(xs_ready[s], 1)
                stp.close()

            with dve.Fori(0, B) as b:
                u0 = b * (E * J)
                for u in range(E * J + 1):
                    if u < E * J:
                        dve.wait_ge(mz_ps, u0 + (u + 1))
                        dve.tensor_tensor(z2[u % 2][:, :], bank(u % 4), rb[:, bass.ds(b * S, S)],
                                          ALU.mult).then_inc(mz2_ready, 1)
                    if u >= 1:
                        dve.wait_ge(mg_ready, u0 + u)
                        dve.tensor_tensor(hid[(u - 1) % 4][:, :], g1[(u - 1) % 2][:, :], g2[(u - 1) % 2][:, :],
                                          ALU.add).then_inc(mh_ready, 1)
                dve.wait_ge(myT_ps, b + 1)
                hs = h_tok[:, bass.ds(b * T, T), :]
                dve.tensor_tensor(hs, bank(4).rearrange("p (t q) -> p t q", t=T), hs, ALU.add).then_inc(out_ready, 1)

        @block.scalar
        def _(act):
            act.wait_ge(d_tok, 16)
            with act.Fori(0, PAIRS) as pair:
                for s in range(2):
                    act.wait_ge(tok_xT_ps[s], pair + 1)
                    act.activation(hT[s][:, :], bank(TB[s]), ACT.Copy).then_inc(tok_xT[s], 1)
                for s in range(2):
                    act.wait_ge(tok_kqv_ps[s], pair * 3 + 1)
                    act.activation(kT[s][:, :], bank(UB[s][0]), ACT.Identity,
                                   bias=w_tok[:, 3 * P:3 * P + 1]).then_inc(tok_kT[s], 1)
                    act.wait_ge(tok_kqv_ps[s], pair * 3 + 3)
                    act.activation(v[s][:, :, 0:P], bank(UB[s][2]).rearrange("p (t q) -> p t q", t=T),
                                   ACT.Copy).then_inc(tok_v[s], 1)
                for i in range(T):
                    for s in range(2):
                        act.wait_ge(tok_max[s], pair * T + (i + 1))
                        act.activation(pr[s][i % 2][:, :], bank(UB[s][i % 2]), ACT.Exp, bias=nmax[s][:, i:i + 1],
                                       accum_out=psums[s][:, i:i + 1]).then_inc(tok_p[s], 1)

            def norm_affine(w, at, k):
                for s in range(2):
                    act.wait_ge(nT_ps[s], k + 1)
                    act.activation(hT[s][:, :], bank(TB[s]), ACT.Identity, scale=w[:, at:at + 1],
                                   bias=w[:, at + 1:at + 2]).then_inc(hT_ready[s], 1)

            def feed_forward(k, f):
                norm_affine(w_f, 2 * FF, k)

                def out_bias(s):
                    act.wait_ge(y_ps[s], f + 1)
                    act.activation(yT[s][:, :], bank(YB[s]), ACT.Identity,
                                   bias=w_f[:, F_COLS - 1:F_COLS]).then_inc(yT_ready[s], 1)

                for u in range(2 * J):
                    act.wait_ge(z_ps, f * (2 * J) + (u + 1))
                    c = 2 * FF + 2 + u % J
                    act.activation(g[u % 3][:, :], bank(ZB[u % 4]), ACT.Gelu, bias=w_f[:, c:c + 1]).then_inc(g_ready, 1)
                    if u == J + 1:
                        out_bias(0)
                out_bias(1)

            with act.Fori(0, PAIRS) as pair:
                act.wait_ge(d_f, 16)
                feed_forward(pair, pair)
            with act.Fori(0, LAYERS) as layer:
                with act.Fori(0, PAIRS) as pair:
                    a = layer * PAIRS + pair
                    act.wait_ge(d_la, layer * 16 + 16)
                    norm_affine(w_la, 4 * P, layer * (2 * PAIRS) + pair + PAIRS)
                    for s in range(2):
                        for i in range(2):
                            act.wait_ge(kv_ps[s], a * 2 + (i + 1))
                            kv = bank(KVB[i]).rearrange("p (t c) -> p t c", t=2)
                            act.activation(ek[s][:, 2 * i:2 * i + 2, :], kv[:, :, 0:P], ACT.Exp)
                            ins = act.activation(v[s][:, 2 * i:2 * i + 2, 0:P], kv[:, :, P:2 * P], ACT.Copy)
                        ins.then_inc(v_ready[s], 1)
                        act.wait_ge(qs_ready[s], a + 1)
                        act.activation(eq[s][:, :], qs[s][:, :], ACT.Exp).then_inc(eq_ready[s], 1)
                    for s in range(2):
                        act.wait_ge(qT_ps[s], a + 1)
                        act.activation(qT[s][:, :], bank(TB[s]), ACT.Copy).then_inc(qT_ready[s], 1)
                    for s in range(2):
                        act.wait_ge(aT_ps[s], a + 1)
                        act.activation(aT[s][:, :], bank(TB[s]), ACT.Copy).then_inc(aT_ready[s], 1)
                with act.Fori(0, PAIRS) as pair:
                    a = layer * PAIRS + pair
                    act.wait_ge(d_f, layer * 16 + 32)
                    feed_forward(layer * (2 * PAIRS) + pair + 2 * PAIRS, a + PAIRS)

            with act.Fori(0, PAIRS) as pair:
                for s in range(2):
                    act.wait_ge(gxT_ps[s], pair + 1)
                    act.activation(hT[s][:, :], bank(TB[s]), ACT.Copy).then_inc(gxT[s], 1)
                for s in range(2):
                    act.wait_ge(gap_ready[s], pair + 1)
                    act.activation(ratio[s][:, :], gap[s][:, :], ACT.Exp).then_inc(ratio_ready[s], 1)
                for s in range(2):
                    cols = bass.ds(pair * (2 * S) + s * S, S)
                    act.wait_ge(xs_ps[s], pair * 2 + 1)
                    act.activation(x1T[:, cols], bank(TB[s]), ACT.Copy)
                    act.wait_ge(xs_ps[s], pair * 2 + 2)
                    act.activation(rb[:, cols], bank(4 + s), ACT.Copy).then_inc(xs_done[s], 1)

            act.wait_ge(d_cmoe, 16)
            act.wait_ge(setup_dve, 2)
            with act.Fori(0, B) as b:
                for u in range(E * J):
                    act.wait_ge(mz2_ready, b * (E * J) + (u + 1))
                    b1 = c_moe[:, E + u:E + u + 1]
                    act.activation(g1[u % 2][:, :], bank(u % 4), ACT.Gelu, bias=b1)
                    act.activation(g2[u % 2][:, :], z2[u % 2][:, :], ACT.Gelu, bias=b1).then_inc(mg_ready, 1)
                act.wait_ge(my_ps, b + 1)
                act.activation(yT[0][:, :], bank(5), ACT.Identity, bias=b2_twice[:, 0:1]).then_inc(myT_ready, 1)

        @block.tensor
        def _(pe):
            pe.wait_ge(d_con, 16)
            pe.wait_ge(d_tok, 16)
            with pe.Fori(0, PAIRS) as pair:
                for s in range(2):
                    pe.wait_ge(tok_x[s], pair + 1)
                    transposes(pe, TB[s], lambda t: n[s][:, t, :]).then_inc(tok_xT_ps[s], 1)
                for s in range(2):
                    pe.wait_ge(tok_xT[s], pair + 1)
                    for i in range(2):
                        pe.matmul(bank(UB[s][i]), w_tok[:, i * P:(i + 1) * P], hT[s][:, :],
                                  start=True, stop=True).then_inc(tok_kqv_ps[s], 1)
                    for t in range(T):
                        ins = pe.matmul(bank(UB[s][2])[:, t * P:(t + 1) * P], hT[s][:, t * P:(t + 1) * P],
                                        w_tok[:, 2 * P:3 * P], start=True, stop=True)
                    ins.then_inc(tok_kqv_ps[s], 1)
                for i in range(T + 2):
                    for s in range(2):
                        if i < T:
                            if i == 0:
                                pe.wait_ge(tok_kT[s], pair + 1)
                                pe.wait_ge(tok_qT[s], pair + 1)
                            pe.matmul(bank(UB[s][i % 2]), kT[s][:, i * P:(i + 1) * P], qT[s][:, :],
                                      start=True, stop=True).then_inc(tok_s_ps[s], 1)
                    for s in range(2):
                        if 1 <= i <= T:
                            pe.wait_ge(tok_p[s], pair * T + i)
                            if i >= 2:
                                pe.wait_ge(tok_pT[s], pair * T + (i - 1))
                            transposes(pe, TB[s], lambda t: pr[s][(i - 1) % 2][:, t * P:(t + 1) * P]
                                       ).then_inc(tok_pT_ps[s], 1)
                    for s in range(2):
                        if i >= 2:
                            if i == 2:
                                pe.wait_ge(tok_v[s], pair + 1)
                            pe.wait_ge(tok_pT[s], pair * T + (i - 1))
                            for t in range(T):
                                ins = pe.matmul(bank(UB[s][2])[:, (i - 2) * P:(i - 1) * P], prT[s][i % 2][:, t, :],
                                                v[s][:, t, 0:P], start=(t == 0), stop=(t == T - 1))
                            if i == T + 1:
                                ins.then_inc(tok_o_ps[s], 1)

            def norm_transposes(k):
                for s in range(2):
                    pe.wait_ge(n_ready[s], k + 1)
                    pe.wait_ge(t_free[s], k + 1)
                    transposes(pe, TB[s], lambda t: n[s][:, t, :]).then_inc(nT_ps[s], 1)

            def feed_forward(k, f):
                norm_transposes(k)
                lag = 2
                for u in range(2 * J + lag):
                    if u < 2 * J:
                        s, j = divmod(u, J)
                        if j == 0:
                            pe.wait_ge(hT_ready[s], k + 1)
                        pe.matmul(bank(ZB[u % 4]), w_f[:, j * P:(j + 1) * P], hT[s][:, :],
                                  start=True, stop=True).then_inc(z_ps, 1)
                    if u >= lag:
                        s, j = divmod(u - lag, J)
                        pe.wait_ge(g_ready, f * (2 * J) + (u - lag + 1))
                        ins = pe.matmul(bank(YB[s]), w_f[:, FF + j * P:FF + (j + 1) * P], g[(u - lag) % 3][:, :],
                                        start=(j == 0), stop=(j == J - 1))
                        if j == J - 1:
                            ins.then_inc(y_ps[s], 1)
                for s in range(2):
                    pe.wait_ge(yT_ready[s], f + 1)
                    transposes(pe, TB[s], lambda t: yT[s][:, t * P:(t + 1) * P]).then_inc(yT_ps[s], 1)

            with pe.Fori(0, PAIRS) as pair:
                pe.wait_ge(d_f, 16)
                feed_forward(pair, pair)
            with pe.Fori(0, LAYERS) as layer:
                with pe.Fori(0, PAIRS) as pair:
                    a = layer * PAIRS + pair
                    k = layer * (2 * PAIRS) + pair + PAIRS
                    pe.wait_ge(d_la, layer * 16 + 16)
                    norm_transposes(k)
                    for s in range(2):
                        pe.wait_ge(hT_ready[s], k + 1)
                        if s == 1:
                            pe.wait_ge(qs_ready[0], a + 1)
                        for t in range(T):
                            ins = pe.matmul(bank(QB)[:, t * P:(t + 1) * P], hT[s][:, t * P:(t + 1) * P], w_la[:, 0:P],
                                            start=True, stop=True)
                        ins.then_inc(q_ps[s], 1)
                        if s == 1:
                            pe.wait_ge(v_ready[0], a + 1)
                        for t in range(T):
                            c = (t % 2) * 2 * P
                            ins = pe.matmul(bank(KVB[t // 2])[:, c:c + 2 * P], hT[s][:, t * P:(t + 1) * P],
                                            w_la[:, P:3 * P], start=True, stop=True)
                            if t % 2:
                                ins.then_inc(kv_ps[s], 1)
                    for s in range(2):
                        pe.wait_ge(v_ready[s], a + 1)
                        if s == 1:
                            pe.wait_ge(cm_ready[0], a + 1)
                        for u in range(NB - 1):
                            r = BUCKET * (u % 2)
                            dst = bank(GB[2])[:, 0:CW] if u == NB - 2 else bank(GB[u % 2])[:, (u // 2) * CW:(u // 2 + 1) * CW]
                            ins = pe.matmul(dst, ek[s][r:r + BUCKET, u // 2, :], v[s][r:r + BUCKET, u // 2, :],
                                            start=True, stop=True)
                        ins.then_inc(g_ps[s], 1)
                        pe.wait_ge(eq_ready[s], a + 1)
                        transposes(pe, TB[s], lambda t: eq[s][:, t * P:(t + 1) * P]).then_inc(qT_ps[s], 1)
                    pe.wait_ge(setup_dve, 1)
                    for s in range(2):
                        pe.wait_ge(qT_ready[s], a + 1)
                        pe.wait_ge(ctx_ready[s], a + 1)
                        if s == 1:
                            pe.wait_ge(att_ready[0], a + 1)
                        for u in range(NB):
                            t, r = u // 2, BUCKET * (u % 2)
                            ctx_u = zero_ctx[:, :] if u == 0 else cm[s][:, u - 1, :]
                            ins = pe.matmul(bank(KVB[t // 2])[r:r + BUCKET, (t % 2) * CW:(t % 2 + 1) * CW],
                                            qT[s][:, u * BUCKET:(u + 1) * BUCKET], ctx_u, start=True, stop=True)
                        ins.then_inc(o_ps[s], 1)
                    for s in range(2):
                        pe.wait_ge(att_ready[s], a + 1)
                        transposes(pe, TB[s], lambda t: att[s][:, t, :]).then_inc(aT_ps[s], 1)
                    for s in range(2):
                        pe.wait_ge(aT_ready[s], a + 1)
                        for t in range(T):
                            ins = pe.matmul(bank(TB[s])[:, t * P:(t + 1) * P], aT[s][:, t * P:(t + 1) * P],
                                            w_la[:, 3 * P:4 * P], start=True, stop=True)
                        ins.then_inc(wo_ps[s], 1)
                with pe.Fori(0, PAIRS) as pair:
                    pe.wait_ge(d_f, layer * 16 + 32)
                    feed_forward(layer * (2 * PAIRS) + pair + 2 * PAIRS, layer * PAIRS + pair + PAIRS)

            pe.wait_ge(d_cmoe, 16)
            with pe.Fori(0, PAIRS) as pair:
                for s in range(2):
                    pe.wait_ge(gx_ready[s], pair + 1)
                    transposes(pe, TB[s], lambda t: n[s][:, t, :]).then_inc(gxT_ps[s], 1)
                for s in range(2):
                    pe.wait_ge(gxT[s], pair + 1)
                    for t in range(T):
                        ins = pe.matmul(bank(2 + s)[:, t * E:(t + 1) * E], hT[s][:, t * P:(t + 1) * P], c_moe[:, 0:E],
                                        start=True, stop=True)
                    ins.then_inc(gl_ps[s], 1)
                for s in range(2):
                    pe.wait_ge(xs_ready[s], pair + 1)
                    transposes(pe, TB[s], lambda t: nrm[s][:, t, :]).then_inc(xs_ps[s], 1)
                    transposes(pe, 4 + s, lambda t: aff[s][:, t, :]).then_inc(xs_ps[s], 1)
                for s in range(2):
                    pe.wait_ge(xs_done[s], pair + 1)

            pe.wait_ge(d_moe, 16)

            def up(b, u):
                e, j = divmod(u, J)
                pe.matmul(bank(u % 4), w_moe[:, e, j * P:(j + 1) * P], x1T[:, bass.ds(b * S, S)],
                          start=True, stop=True).then_inc(mz_ps, 1)

            lead = 3
            for u in range(lead):
                up(0, u)
            with pe.Fori(0, B) as b:
                for u in range(E * J):
                    e, j = divmod(u, J)
                    up(b if u + lead < E * J else (b + 1) % B, (u + lead) % (E * J))
                    pe.wait_ge(mh_ready, b * (E * J) + (u + 1))
                    ins = pe.matmul(bank(5), w_moe[:, e, FF + j * P:FF + (j + 1) * P], hid[u % 4][:, :],
                                    start=(u == 0), stop=(u == E * J - 1))
                ins.then_inc(my_ps, 1)
                pe.wait_ge(myT_ready, b + 1)
                transposes(pe, 4, lambda t: yT[0][:, t * P:(t + 1) * P]).then_inc(myT_ps, 1)


def position_code():
    at = np.arange(S, dtype=np.float32)[:, None]
    i = np.arange(P, dtype=np.float32)[None, :]
    ang = at / np.power(np.float32(10000.0), np.float32(2.0) * i / np.float32(P))
    code = np.where((np.arange(P) % 2 == 0)[None, :], np.sin(ang), np.cos(ang)).astype(np.float32)
    return np.ascontiguousarray((code * np.float32(P ** 0.5)).reshape(T, P, P).transpose(1, 0, 2))


def constants():
    head = np.arange(P) // DH
    mask = np.concatenate([head[:, None] == head[None, :], head[:, None] == np.arange(HEADS)[None, :]], axis=1)
    return np.concatenate([np.eye(P, dtype=np.float32), mask.astype(np.float32)], axis=1)


def kernel(**inputs):
    import concourse.bacc as bacc
    from concourse.bass_utils import run_bass_kernel_spmd

    a = {k: np.asarray(v) for k, v in inputs.items()}

    def blocks(w):
        return w.reshape(*w.shape[:-2], J, P, P).swapaxes(-3, -2).reshape(*w.shape[:-2], P, J * P)

    def col(v):
        return v[..., None]

    def cols(v):
        return v.reshape(*v.shape[:-1], J, P).swapaxes(-1, -2)

    t = {k[7:]: v for k, v in a.items() if k.startswith("L0_tok_")}
    l = {k[8:]: v for k, v in a.items() if k.startswith("L0_attn_")}
    m = {k[7:]: v for k, v in a.items() if k.startswith("L0_ffn_")}
    one, zero = np.ones((P, 1), np.float32), np.zeros((P, 1), np.float32)
    ffn_tok = np.concatenate([t["w1"], blocks(t["w2"]), one, zero, cols(t["b1"]), col(t["b2"])], axis=1)
    ffn_l = np.concatenate([l["w1"], blocks(l["w2"]), col(l["ln2_g"]), col(l["ln2_b"]), cols(l["b1"]), col(l["b2"])],
                           axis=2)
    arrays = {
        "ids": np.ascontiguousarray(a["x"].reshape(B * T, P).T),
        "emb": t["emb"],
        "pos": position_code(),
        "consts": constants(),
        "tok_w": np.concatenate([t["wk"], t["wq"], t["wv"], col(t["bk"]), col(t["bq"])], axis=1),
        "tok_rows": np.stack([t["bv"], t["ln_g"], t["ln_b"]]),
        "attn_w": np.concatenate([l["wq"], l["wk"], l["wv"], l["wo"], col(l["ln1_g"]), col(l["ln1_b"])], axis=2),
        "attn_bo": l["bo"],
        "ffn_w": np.concatenate([ffn_tok[None], ffn_l], axis=0),
        "moe_w": np.ascontiguousarray(np.concatenate([m["W1"], blocks(m["W2"])], axis=2).transpose(1, 0, 2)),
        "moe_c": np.concatenate([m["Wg"], cols(m["b1"]).transpose(1, 0, 2).reshape(P, E * J), m["b2"].T], axis=1),
    }
    nc = bacc.Bacc("TRN2", target_bir_lowering=False, num_devices=1)
    args = []
    for name, v in arrays.items():
        arrays[name] = v = np.ascontiguousarray(v)
        args.append(nc.dram_tensor(name, v.shape, mybir.dt.from_np(v.dtype), kind="ExternalInput").ap())
    out = nc.dram_tensor("out", (B, S, P), mybir.dt.float32, kind="ExternalOutput").ap()
    build(nc, *args, out)
    r = run_bass_kernel_spmd(nc, [arrays], core_ids=[0])
    return r.results[0]["out"]
```

```python
from contextlib import ExitStack

import numpy as np

import concourse.bass as bass
from concourse import mybir

P = 128
B = 8
S = 512
T = S // P
PAIRS = B // 2
LAYERS = 4
HEADS = 8
DH = P // HEADS
BUCKET = 64
NB = S // BUCKET
FF = 512
J = FF // P
E = 8
CW = P + HEADS
OW = CW + HEADS
EPS_LN = 1e-5
EPS_ATTN = 1e-3
LA_COLS = 4 * P + 2
UP_COLS = E * FF // LAYERS
F_COLS = 2 * FF + 2 + J + 1

DVE_STEPS = dict(ta=12, tf=24, la_front=2, la_back=14, lf=8, mg=1)
POOL_STEPS = dict(ta=4, tf=12, la_front=10, la_back=4, lf=4, mg=9)


AT = dict(stats=2, gate_T=9, transposed=9, logits=12, top=13, share=15, input_T=18, input_hi=18, input_lo=21, ratios=22,
          result_T=3, result=3)


class Steps:

    def __init__(self, eng, sem, base, per):
        self.eng, self.sem, self.base, self.per, self.n = eng, sem, base, per, 0

    def done(self, ins):
        self.n += 1
        ins.then_inc(self.sem, 1)
        self.eng.wait_ge(self.sem, self.base + self.n)

    def close(self):
        assert self.n == self.per, (self.n, self.per)


def build(nc, ids, emb, pos, consts, tok_w, tok_rows, attn_w, attn_bo, ffn_w, moe_up, moe_down, moe_c, out):
    ACT = mybir.ActivationFunctionType
    ALU = mybir.AluOpType
    AX = mybir.AxisListType
    F32 = mybir.dt.float32
    F32R = mybir.dt.float32r
    I32 = mybir.dt.int32
    U32 = mybir.dt.uint32
    ctx = ExitStack()
    with ctx:
        def sb(name, shape, dt=F32):
            return ctx.enter_context(nc.sbuf_tensor(name, shape, dt))

        def sem(name):
            return ctx.enter_context(nc.semaphore(name))

        def sem2(name):
            return [sem(f"{name}_{s}") for s in range(2)]

        x = sb("x", [P, B * T, P])
        h_tok = sb("h_tok", [P, B * T, P])
        rstd = sb("rstd", [P, B * T])
        nbias = sb("nbias", [P, B * T])
        idx = sb("idx", [P, B * T], I32)
        pos_sb = sb("pos_sb", [P, T, P])
        con = sb("con", [P, P + CW])
        ident = con[:, 0:P]
        head_mask = con[:, P:P + CW]
        w_tok = sb("w_tok", [P, 3 * P + 2])
        rows = sb("rows", [P, 3, P])
        w_la = sb("w_la", [P, LA_COLS])
        bo = sb("bo", [P, P])
        w_f = sb("w_f", [P, F_COLS])
        w_up = sb("w_up", [P, UP_COLS])
        w_up_hi = sb("w_up_hi", [P, E * FF], F32R)
        w_up_lo = sb("w_up_lo", [P, E * FF], F32R)
        w_down = sb("w_down", [P, E * FF])
        c_moe = sb("c_moe", [P, E + J * E + E])
        scratch = sb("scratch", [P, 1])
        mark = [sb(f"mark{s}", [P, 1]) for s in range(2)]
        pool_scratch = sb("pool_scratch", [P, T])
        b2_sum = sb("b2_sum", [P, 1])
        b2_twice = sb("b2_twice", [P, 1])
        eps_t = sb("eps_t", [P, T])
        mhalf_t = sb("mhalf_t", [P, T])
        quarter_t = sb("quarter_t", [P, T])
        share_t = sb("share_t", [P, T])
        one_t = sb("one_t", [P, T])
        e_t = sb("e_t", [P, T])

        n = [sb(f"n{s}", [P, T, P]) for s in range(2)]
        hT = [sb(f"hT{s}", [P, S]) for s in range(2)]
        nrm = [sb(f"nrm{s}", [P, T, P]) for s in range(2)]
        aff = [sb(f"aff{s}", [P, T, P]) for s in range(2)]
        st = [sb(f"st{s}", [P, T, 6]) for s in range(2)]
        st_sum = [sb(f"st_sum{s}", [P, T]) for s in range(2)]
        st_dif = [sb(f"st_dif{s}", [P, T]) for s in range(2)]
        st_m2 = [sb(f"st_m2{s}", [P, T]) for s in range(2)]
        st_dd = [sb(f"st_dd{s}", [P, T]) for s in range(2)]
        st_nmean = [sb(f"st_nmean{s}", [P, T]) for s in range(2)]
        st_var = [sb(f"st_var{s}", [P, T]) for s in range(2)]
        st_ve = [sb(f"st_ve{s}", [P, T]) for s in range(2)]
        st_rs = [sb(f"st_rs{s}", [P, T]) for s in range(2)]
        st_nb = [sb(f"st_nb{s}", [P, T]) for s in range(2)]

        kT = [sb(f"kT{s}", [P, S]) for s in range(2)]
        qT = [sb(f"qT{s}", [P, S]) for s in range(2)]
        v = [sb(f"v{s}", [P, T, CW]) for s in range(2)]
        pr = [[sb(f"pr{s}{i}", [P, S]) for i in range(2)] for s in range(2)]
        prT = [[sb(f"prT{s}{i}", [P, T, P]) for i in range(2)] for s in range(2)]
        nmax = [sb(f"nmax{s}", [P, T]) for s in range(2)]
        psums = [sb(f"psums{s}", [P, T]) for s in range(2)]
        rsum = [sb(f"rsum{s}", [P, T]) for s in range(2)]

        ek = [sb(f"ek{s}", [P, T, P]) for s in range(2)]
        qs = [pr[s][0] for s in range(2)]
        eq = [pr[s][1] for s in range(2)]
        qmax = [sb(f"qmax{s}", [P, T * HEADS]) for s in range(2)]
        qeps = [sb(f"qeps{s}", [P, T * HEADS]) for s in range(2)]
        den = [sb(f"den{s}", [P, T * HEADS]) for s in range(2)]
        rden = [sb(f"rden{s}", [P, T * HEADS]) for s in range(2)]
        cm = [sb(f"cm{s}", [P, NB - 1, OW]) for s in range(2)]
        zero_ctx = sb("zero_ctx", [P, OW])
        att = [sb(f"att{s}", [P, T, P]) for s in range(2)]
        aT = [kT[s] for s in range(2)]

        g = [sb(f"g{i}", [P, S]) for i in range(3)]
        yT = [sb(f"yT{s}", [P, S]) for s in range(2)]

        x1_hi = sb("x1_hi", [P, 2 * S], F32R)
        x1_lo = sb("x1_lo", [P, 2 * S], F32R)
        rb = sb("rb", [P, 2 * S])
        mg_sq = sb("mg_sq", [P, T])
        mg_m2 = sb("mg_m2", [P, T])
        top = sb("top", [P, T, 8])
        gap = sb("gap", [P, T])
        ratio = sb("ratio", [P, T])
        gden = sb("gden", [P, T])
        p1 = sb("p1", [P, T])
        gx, xs, gT = n[0], nrm[0], yT[1]
        z2 = [hT[i] for i in range(2)]
        g1 = [pr[0][0], pr[0][1]]
        g2 = [pr[1][0], pr[1][1]]
        hid = [kT[0], kT[1], qT[0], qT[1]]

        ps = ctx.enter_context(nc.psum_tensor("ps", [P, 8, 512], F32))

        def bank(i):
            return ps[:, i, :]

        TB = [0, 1]
        UB = [[2, 3, 4], [5, 6, 7]]
        QB, KVB, GB = 2, [3, 4], [5, 6, 7]
        ZB, YB = [2, 3, 4, 5], [6, 7]
        MZB, MTB, MYB, GTB, GLB = [0, 1, 2, 3], 4, 5, 6, 7

        d_idx, d_con, d_tok, d_rows, d_pos = (sem(f"d_{k}") for k in ("idx", "con", "tok", "rows", "pos"))
        d_la, d_bo, d_f, d_up, d_down, d_cmoe, d_out = (sem(f"d_{k}") for k in ("la", "bo", "f", "up", "down", "cmoe", "out"))
        d_gather = sem2("d_gather")
        setup_pool, setup_dve = sem("setup_pool"), sem("setup_dve")
        dve_steps = {k: sem(f"dve_steps_{k}") for k in ("su", *DVE_STEPS)}
        pool_steps = {k: sem(f"pool_steps_{k}") for k in POOL_STEPS}
        stats_ready, ln_rstd, next_rstd = sem2("stats_ready"), sem2("ln_rstd"), sem2("next_rstd")
        nrm_ready = sem2("nrm_ready")
        n_ready, nT_ps, hT_ready, t_free = sem2("n_ready"), sem2("nT_ps"), sem2("hT_ready"), sem2("t_free")
        tok_x, tok_xbv, tok_xT_ps, tok_xT = sem2("tok_x"), sem2("tok_xbv"), sem2("tok_xT_ps"), sem2("tok_xT")
        tok_kqv_ps, tok_kT, tok_qT, tok_v = sem2("tok_kqv_ps"), sem2("tok_kT"), sem2("tok_qT"), sem2("tok_v")
        tok_s_ps, tok_max, tok_p, tok_pT_ps, tok_pT, tok_o_ps, tok_r = (
            sem2(f"tok_{k}") for k in ("s_ps", "max", "p", "pT_ps", "pT", "o_ps", "r"))
        tok_o_read = sem2("tok_o_read")
        q_ps, kv_ps, qs_ready, v_ready, eq_ready, g_ps, qT_ps, qT_ready = (
            sem2(k) for k in ("q_ps", "kv_ps", "qs_ready", "v_ready", "eq_ready", "g_ps", "qT_ps", "qT_ready"))
        cm_ready, ctx_ready, o_ps, att_ready, aT_ps, aT_ready, wo_ps, bo_added = (
            sem2(k) for k in ("cm_ready", "ctx_ready", "o_ps", "att_ready", "aT_ps", "aT_ready", "wo_ps", "bo_added"))
        z_ps, g_ready, y_ps, yT_ready, yT_ps = sem("z_ps"), sem("g_ready"), sem2("y_ps"), sem2("yT_ready"), sem2("yT_ps")
        h_aff = sem2("h_aff")
        gh_ready, gst_ready, gx_ready, gxT_ps, gxT_ready, gl_ps, gap_ready, xs_ready, xs_ps = (
            sem(k) for k in ("gh_ready", "gst_ready", "gx_ready", "gxT_ps", "gxT_ready", "gl_ps", "gap_ready",
                             "xs_ready", "xs_ps"))
        gden_ready, p1_ready = sem("gden_ready"), sem("p1_ready")
        x1_hi_ready, x1_ready, rb_ready, up_hi_ready, up_ready = (
            sem(k) for k in ("x1_hi_ready", "x1_ready", "rb_ready", "up_hi_ready", "up_ready"))
        mz_ps, mz2_ready, mg_ready, mh_ready, my_ps, myT_ready, myT_ps, out_ready = (
            sem(k) for k in ("mz_ps", "mz2_ready", "mg_ready", "mh_ready", "my_ps", "myT_ready", "myT_ps",
                             "out_ready"))

        def tiles(pair, s):
            return bass.ds(pair * (2 * T) + s * T, T)

        def seq(b):
            return bass.ds(b * T, T)

        def tile_of(tensor, b, t):
            return tensor[:, bass.ds(b * T + t, 1), :].rearrange("p a d -> p (a d)")

        def turn(b):
            return bass.ds((b % 2) * S, S)

        def one(tensor, pair, s, t):
            at = bass.ds(pair * (2 * T) + (s * T + t), 1)
            if len(tensor.shape) == 2:
                return tensor[:, at]
            return tensor[:, at, :].rearrange("p a d -> p (a d)")

        def transposes(pe, dst, src_tile):
            for t in range(T):
                last = pe.transpose(bank(dst)[:, t * P:(t + 1) * P], src_tile(t), ident)
            return last

        block = ctx.enter_context(nc.Block())

        @block.sync
        def _(sp):
            sp.dma_start(idx[:, :], ids).then_inc(d_idx, 16)
            sp.dma_start(con[:, :], consts).then_inc(d_con, 16)
            sp.dma_start(pos_sb[:, :, :], pos).then_inc(d_pos, 16)
            sp.dma_start(w_tok[:, :], tok_w).then_inc(d_tok, 16)
            sp.dma_start(rows[:, :, :], tok_rows.partition_broadcast(P)).then_inc(d_rows, 16)
            sp.dma_start(w_f[:, :], ffn_w[0]).then_inc(d_f, 16)
            sp.dma_start(w_la[:, :], attn_w[0]).then_inc(d_la, 16)
            sp.dma_start(bo[:, :], attn_bo[0].partition_broadcast(P)).then_inc(d_bo, 16)
            sp.dma_start(c_moe[:, :], moe_c).then_inc(d_cmoe, 16)
            sp.dma_start(w_up[:, :], moe_up[:, 0:UP_COLS]).then_inc(d_up, 16)
            sp.dma_start(w_down[:, :], moe_down).then_inc(d_down, 16)
            with sp.Fori(0, LAYERS - 1) as l:
                sp.wait_ge(yT_ready[1], PAIRS * l + PAIRS)
                sp.dma_start(w_f[:, :], ffn_w[bass.ds(l + 1, 1)].rearrange("a p c -> (a p) c")).then_inc(d_f, 16)
                sp.wait_ge(wo_ps[1], PAIRS * l + PAIRS)
                sp.dma_start(w_la[:, :], attn_w[bass.ds(l + 1, 1)].rearrange("a p c -> (a p) c")).then_inc(d_la, 16)
                sp.wait_ge(bo_added[0], PAIRS * l + PAIRS)
                sp.wait_ge(bo_added[1], PAIRS * l + PAIRS)
                sp.dma_start(bo[:, :], attn_bo[bass.ds(l + 1, 1)].rearrange("a d -> (a d)").partition_broadcast(P)
                             ).then_inc(d_bo, 16)
                sp.wait_ge(up_ready, l + 1)
                sp.dma_start(w_up[:, :], moe_up[:, bass.ds((l + 1) * UP_COLS, UP_COLS)]).then_inc(d_up, 16)
            sp.wait_ge(yT_ready[1], PAIRS * LAYERS)
            sp.dma_start(w_f[:, :], ffn_w[LAYERS]).then_inc(d_f, 16)
            with sp.Fori(0, B) as b:
                sp.wait_ge(out_ready, b + 1)
                sp.dma_start(out[bass.ds(b, 1)].rearrange("b (t p) d -> p (b t) d", p=P),
                             h_tok[:, bass.ds(b * T, T), :]).then_inc(d_out, 16)
            sp.wait_ge(d_out, 16 * B)

        @block.gpsimd
        def _(pool):
            def carry_wait():
                pool.tensor_tensor(pool_scratch[:, :], one_t[:, :], one_t[:, :], ALU.add)

            def pool_rstd(stp, s, count, rs, nb, done):
                pool.wait_ge(stats_ready[s], count)
                stp.done(pool.tensor_tensor(st_ve[s][:, :], st_var[s][:, :], eps_t[:, :], ALU.add))
                stp.done(pool.tensor_tensor(rs, st_ve[s][:, :], mhalf_t[:, :], ALU.pow))
                pool.tensor_tensor(nb, st_nmean[s][:, :], rs, ALU.mult).then_inc(done[s], 1)

            def inner_rstd(stp, s, count):
                pool_rstd(stp, s, count, st_rs[s][:, :], st_nb[s][:, :], ln_rstd)

            def phase_rstd(stp, s, pair, count):
                pool_rstd(stp, s, count, rstd[:, tiles(pair, s)], nbias[:, tiles(pair, s)], next_rstd)

            def add_row(dst, src, row):
                return pool.tensor_tensor(dst, src, row.unsqueeze(1).broadcast_to([P, T, P]), ALU.add)

            pool.wait_ge(d_idx, 16)
            for p in range(PAIRS):
                for t in range(2 * T * p, 2 * T * (p + 1)):
                    if p >= 1 and t % T == 0:
                        pool.wait_ge(d_gather[t // T % 2], 16 * T * p)
                    pool.indirect_dma_start(x[:, t, :], None, emb,
                                            bass.IndirectOffsetOnAxis(ap=idx[:, t:t + 1], axis=0)
                                            ).then_inc(d_gather[t // T % 2], 16)
                if p == 0:
                    pool.memset(eps_t[:, :], EPS_LN).then_inc(setup_pool, 1)
                    pool.memset(mhalf_t[:, :], -0.5).then_inc(setup_pool, 1)
                    for dst, value in ((quarter_t, 0.25), (share_t, 1.0 / P), (one_t, 1.0), (e_t, float(np.e))):
                        pool.memset(dst[:, :], value).then_inc(setup_pool, 1)
                    for q in range(PAIRS):
                        for s in range(2):
                            a = (2 * q + s) * T
                            pool.memset(nbias[:, a:a + T], 0.0).then_inc(setup_pool, 1)
                            pool.memset(rstd[:, a:a + T], 1.0).then_inc(next_rstd[s], 1)
                    pool.wait_ge(setup_pool, 6 + 2 * PAIRS)
            pool.wait_ge(d_rows, 16)

            with pool.Fori(0, PAIRS) as pair:
                stp = Steps(pool, pool_steps["ta"], pair * POOL_STEPS["ta"], POOL_STEPS["ta"])
                for s in range(2):
                    pool.wait_ge(tok_x[s], pair + 1)
                    add_row(nrm[s][:, :, :], n[s][:, :, :], rows[:, 0, :]).then_inc(tok_xbv[s], 1)
                for s in range(2):
                    inner_rstd(stp, s, pair + 1)
                for s in range(2):
                    pool.wait_ge(nrm_ready[s], pair + 1)
                    add_row(x[:, tiles(pair, s), :], aff[s][:, :, :], rows[:, 2, :]).then_inc(tok_r[s], 1)
                stp.close()

            with pool.Fori(0, PAIRS) as pair:
                stp = Steps(pool, pool_steps["tf"], pair * POOL_STEPS["tf"], POOL_STEPS["tf"])
                for s in range(2):
                    inner_rstd(stp, s, pair * 3 + (PAIRS + 1))
                for s in range(2):
                    pool.wait_ge(nrm_ready[s], pair + (PAIRS + 1))
                    add_row(h_tok[:, tiles(pair, s), :], aff[s][:, :, :], rows[:, 2, :]).then_inc(h_aff[s], 1)
                for s in range(2):
                    inner_rstd(stp, s, pair * 3 + (PAIRS + 2))
                for s in range(2):
                    phase_rstd(stp, s, pair, pair * 3 + (PAIRS + 3))
                stp.close()

            with pool.Fori(0, LAYERS) as layer:
                def attn_front(pair, cum):
                    a = layer * PAIRS + pair
                    k = layer * (2 * PAIRS) + pair + PAIRS
                    for s in range(2):
                        pool.wait_ge(n_ready[s], k + 1)
                        xs_ = x[:, tiles(pair, s), :]
                        add_row(xs_, xs_, bo[:, :]).then_inc(bo_added[s], 1)

                def contexts(pair, stp, s):
                    a = layer * PAIRS + pair
                    pool.wait_ge(cm_ready[s], a + 1)
                    for u in range(1, NB - 1):
                        ins = pool.tensor_tensor(cm[s][:, u, 0:CW], cm[s][:, u - 1, 0:CW], cm[s][:, u, 0:CW], ALU.add)
                        if u < NB - 2:
                            stp.done(ins)
                    ins.then_inc(ctx_ready[s], 1)

                def steps(pair, which):
                    return Steps(pool, pool_steps[which], (layer * PAIRS + pair) * POOL_STEPS[which], POOL_STEPS[which])

                def back_rstd(pair, stp, s):
                    phase_rstd(stp, s, pair, layer * (2 * PAIRS) + pair + (PAIRS + 13))

                pool.wait_ge(d_bo, layer * 16 + 16)
                attn_front(0, None)
                stp = steps(0, "la_front")
                for s in range(2):
                    contexts(0, stp, s)
                stp.close()
                with pool.Fori(1, PAIRS) as pair:
                    attn_front(pair, None)
                    front, back = steps(pair, "la_front"), steps(pair - 1, "la_back")
                    for s in range(2):
                        contexts(pair, front, s)
                        back_rstd(pair - 1, back, s)
                    front.close()
                    back.close()
                stp = steps(PAIRS - 1, "la_back")
                for s in range(2):
                    back_rstd(PAIRS - 1, stp, s)
                stp.close()
                part = bass.ds(layer * UP_COLS, UP_COLS)
                pool.wait_ge(d_up, layer * 16 + 16)
                pool.tensor_copy(w_up_hi[:, part], w_up[:, :]).then_inc(up_hi_ready, 1)
                pool.wait_ge(up_hi_ready, layer + 1)
                carry_wait()
                pool.tensor_tensor(w_up_lo[:, part], w_up[:, :], w_up_hi[:, part].bitcast(F32),
                                   ALU.subtract).then_inc(up_ready, 1)
                with pool.Fori(0, PAIRS) as pair:
                    stp = steps(pair, "lf")
                    for s in range(2):
                        phase_rstd(stp, s, pair, layer * (2 * PAIRS) + pair + (2 * PAIRS + 13))
                    stp.close()

            def spread(column):
                return column[:, :].unsqueeze(2).broadcast_to([P, T, P])

            def gating(b):
                stp = Steps(pool, pool_steps["mg"], b * POOL_STEPS["mg"], POOL_STEPS["mg"])
                hs = h_tok[:, seq(b), :]
                pool.tensor_tensor(hs, hs, x[:, seq(b), :], ALU.add).then_inc(gh_ready, 1)
                pool.wait_ge(gst_ready, b + 1)
                pool.tensor_tensor(st_sum[0][:, :], st[0][:, :, 1], st[0][:, :, 4], ALU.add)
                pool.tensor_tensor(mg_m2[:, :], st[0][:, :, 2], st[0][:, :, 5], ALU.add)
                stp.done(pool.tensor_tensor(st_dif[0][:, :], st[0][:, :, 1], st[0][:, :, 4], ALU.subtract))
                pool.tensor_tensor(st_nmean[0][:, :], st_sum[0][:, :], mhalf_t[:, :], ALU.mult)
                pool.tensor_tensor(st_m2[0][:, :], mg_m2[:, :], share_t[:, :], ALU.mult)
                stp.done(pool.tensor_tensor(mg_sq[:, :], st_dif[0][:, :], st_dif[0][:, :], ALU.mult))
                stp.done(pool.tensor_tensor(st_dd[0][:, :], mg_sq[:, :], quarter_t[:, :], ALU.mult))
                stp.done(pool.tensor_tensor(st_var[0][:, :], st_dd[0][:, :], st_m2[0][:, :], ALU.add))
                stp.done(pool.tensor_tensor(st_ve[0][:, :], st_var[0][:, :], eps_t[:, :], ALU.add))
                stp.done(pool.tensor_tensor(st_rs[0][:, :], st_ve[0][:, :], mhalf_t[:, :], ALU.pow))
                stp.done(pool.tensor_tensor(st_nb[0][:, :], st_nmean[0][:, :], st_rs[0][:, :], ALU.mult))
                carry_wait()
                stp.done(pool.tensor_tensor(xs[:, :, :], hs, spread(st_rs[0]), ALU.mult))
                pool.tensor_tensor(gx[:, :, :], xs[:, :, :], spread(st_nb[0]), ALU.add).then_inc(gx_ready, 1)
                pool.wait_ge(gap_ready, b + 1)
                stp.done(pool.tensor_tensor(ratio[:, :], e_t[:, :], gap[:, :], ALU.pow))
                pool.tensor_tensor(gden[:, :], ratio[:, :], one_t[:, :], ALU.add).then_inc(gden_ready, 1)
                pool.wait_ge(p1_ready, b + 1)
                pool.tensor_tensor(xs[:, :, :], gx[:, :, :], spread(p1), ALU.mult).then_inc(xs_ready, 1)
                stp.close()

            pool.wait_ge(n_ready[0], 1 + (1 + 2 * LAYERS) * PAIRS)
            gating(0)
            with pool.Fori(1, B) as b:
                gating(b)

        @block.vector
        def _(dve):
            def carry_wait():
                dve.memset(scratch[:, :], 0.0)

            def stats(stp, s, src, count, first=None):
                carry_wait()
                for t in range(T):
                    ins = dve.bn_stats(st[s][:, t, :], src(t))
                    if t == 0 and first is not None:
                        ins.then_inc(first, 1)
                stp.done(ins)
                dve.tensor_tensor(st_sum[s][:, :], st[s][:, :, 1], st[s][:, :, 4], ALU.add)
                dve.tensor_tensor(st_dif[s][:, :], st[s][:, :, 1], st[s][:, :, 4], ALU.subtract)
                stp.done(dve.tensor_tensor(st_m2[s][:, :], st[s][:, :, 2], st[s][:, :, 5], ALU.add))
                if count is not None:
                    dve.wait_ge(next_rstd[s], count)
                dve.tensor_scalar(st_nmean[s][:, :], st_sum[s][:, :], -0.5, None, ALU.mult)
                stp.done(dve.scalar_tensor_tensor(st_dd[s][:, :], st_dif[s][:, :], 0.25, st_dif[s][:, :],
                                                  ALU.mult, ALU.mult))
                dve.scalar_tensor_tensor(st_var[s][:, :], st_m2[s][:, :], 1.0 / P, st_dd[s][:, :],
                                         ALU.mult, ALU.add).then_inc(stats_ready[s], 1)

            def normalise(dst, src, rstd_of, nbias_of):
                for t in range(T):
                    ins = dve.tensor_scalar(dst(t), src(t), rstd_of(t), nbias_of(t), ALU.mult, ALU.add)
                return ins

            def gain(stp, s):
                stp.done(normalise(lambda t: aff[s][:, t, :], lambda t: nrm[s][:, t, :], *inner(s)))
                dve.tensor_tensor(aff[s][:, :, :], aff[s][:, :, :], rows[:, 1, :].unsqueeze(1).broadcast_to([P, T, P]),
                                  ALU.mult).then_inc(nrm_ready[s], 1)

            def prepare(pair, k):
                nxt = (pair + 1) % PAIRS
                for s in range(2):
                    dve.wait_ge(nT_ps[s], k + 1)
                    dve.wait_ge(next_rstd[s], k + 2)
                    normalise(lambda t: n[s][:, t, :], lambda t: one(x, nxt, s, t),
                              lambda t: one(rstd, nxt, s, t), lambda t: one(nbias, nxt, s, t)
                              ).then_inc(n_ready[s], 1)

            def inner(s):
                return lambda t: st_rs[s][:, t:t + 1], lambda t: st_nb[s][:, t:t + 1]

            dve.wait_ge(d_con, 16)
            dve.memset(zero_ctx[:, 0:CW], 0.0)
            floor = head_mask[:, P:CW]
            for c in (zero_ctx[:, CW:OW], *(cm[s][:, u, CW:OW] for s in range(2) for u in range(NB - 1))):
                ins = dve.tensor_scalar(c, floor, EPS_ATTN * float(DH) ** 0.5, None, ALU.mult)
            ins.then_inc(setup_dve, 1)
            dve.wait_ge(d_cmoe, 16)
            dve.tensor_reduce(b2_sum[:, :], c_moe[:, E + J * E:], AX.X, ALU.add).then_inc(dve_steps["su"], 1)
            dve.wait_ge(dve_steps["su"], 1)
            dve.tensor_scalar(b2_twice[:, :], b2_sum[:, :], 2.0, None, ALU.mult).then_inc(setup_dve, 1)
            dve.wait_ge(d_pos, 16)
            dve.wait_ge(d_tok, 16)

            dve.wait_ge(d_rows, 16)

            def token_x(pair):
                for s in range(2):
                    dve.wait_ge(d_gather[s], pair * (16 * T) + 16 * T)
                    dve.scalar_tensor_tensor(n[s][:, :, :], x[:, tiles(pair, s), :], float(P) ** 0.5, pos_sb[:, :, :],
                                             ALU.mult, ALU.add).then_inc(tok_x[s], 1)

            def token_attention(pair, last):
                stp = Steps(dve, dve_steps["ta"], pair * DVE_STEPS["ta"], DVE_STEPS["ta"])
                for s in range(2):
                    dve.wait_ge(tok_kqv_ps[s], pair * 3 + 2)
                    dve.tensor_scalar(qT[s][:, :], bank(UB[s][1]), w_tok[:, 3 * P + 1:3 * P + 2], float(P) ** -0.5,
                                      ALU.add, ALU.mult).then_inc(tok_qT[s], 1)
                for i in range(T + 1):
                    for s in range(2):
                        if i < T:
                            dve.wait_ge(tok_s_ps[s], pair * T + (i + 1))
                            dve.tensor_reduce(nmax[s][:, i:i + 1], bank(UB[s][i % 2]), AX.X, ALU.max,
                                              negate=True).then_inc(tok_max[s], 1)
                    for s in range(2):
                        if i >= 1:
                            dve.wait_ge(tok_pT_ps[s], pair * T + i)
                            dve.tensor_copy(prT[s][(i - 1) % 2][:, :, :],
                                            bank(TB[s]).rearrange("p (t q) -> p t q", t=T)).then_inc(tok_pT[s], 1)
                for s in range(2):
                    dve.wait_ge(tok_xbv[s], pair + 1)
                if not last:
                    token_x(pair + 1)
                for s in range(2):
                    stp.done(dve.reciprocal(rsum[s][:, :], psums[s][:, :]))
                    dve.wait_ge(tok_o_ps[s], pair + 1)
                    for t in range(T):
                        ins = dve.scalar_tensor_tensor(nrm[s][:, t, :], bank(UB[s][2])[:, t * P:(t + 1) * P],
                                                       rsum[s][:, t:t + 1], nrm[s][:, t, :], ALU.mult, ALU.add)
                        if t == T - 1:
                            ins.then_inc(tok_o_read[s], 1)
                    stp.done(dve.memset(mark[s][:, :], 0.0))
                    stats(stp, s, lambda t: nrm[s][:, t, :], None)
                for s in range(2):
                    dve.wait_ge(ln_rstd[s], pair + 1)
                    gain(stp, s)
                stp.close()

            token_x(0)
            with dve.Fori(0, PAIRS - 1) as pair:
                token_attention(pair, False)
            token_attention(PAIRS - 1, True)

            for s in range(2):
                dve.memset(v[s][:, :, P:CW], 1.0).then_inc(t_free[s], 1)
                dve.wait_ge(tok_r[s], PAIRS)
                dve.wait_ge(next_rstd[s], 1)
                normalise(lambda t: n[s][:, t, :], lambda t: x[:, s * T + t, :],
                          lambda t: rstd[:, s * T + t:s * T + t + 1], lambda t: nbias[:, s * T + t:s * T + t + 1]
                          ).then_inc(n_ready[s], 1)

            with dve.Fori(0, PAIRS) as pair:
                stp = Steps(dve, dve_steps["tf"], pair * DVE_STEPS["tf"], DVE_STEPS["tf"])
                prepare(pair, pair)
                for s in range(2):
                    dve.wait_ge(yT_ps[s], pair + 1)
                    stp.done(dve.tensor_tensor(nrm[s][:, :, :], bank(TB[s]).rearrange("p (t q) -> p t q", t=T),
                                               x[:, tiles(pair, s), :], ALU.add))
                    stats(stp, s, lambda t: nrm[s][:, t, :], pair + PAIRS, t_free[s])
                for s in range(2):
                    dve.wait_ge(ln_rstd[s], pair * 2 + (PAIRS + 1))
                    gain(stp, s)
                for s in range(2):
                    dve.wait_ge(h_aff[s], pair + 1)
                    stats(stp, s, lambda t: one(h_tok, pair, s, t), None)
                for s in range(2):
                    dve.wait_ge(ln_rstd[s], pair * 2 + (PAIRS + 2))
                    stp.done(normalise(lambda t: one(x, pair, s, t), lambda t: one(h_tok, pair, s, t), *inner(s)))
                    stats(stp, s, lambda t: one(x, pair, s, t), None)
                stp.close()

            def residual(stp, s, pair):
                xs_ = x[:, tiles(pair, s), :]
                stp.done(dve.tensor_tensor(xs_, bank(TB[s]).rearrange("p (t q) -> p t q", t=T), xs_, ALU.add))
                dve.memset(mark[s][:, :], 0.0).then_inc(t_free[s], 1)

            def x_stats(stp, s, pair, k):
                stats(stp, s, lambda t: one(x, pair, s, t), k + PAIRS)

            with dve.Fori(0, LAYERS) as layer:
                def steps(pair, which):
                    return Steps(dve, dve_steps[which], (layer * PAIRS + pair) * DVE_STEPS[which], DVE_STEPS[which])

                def queries(pair, stp, s):
                    dve.wait_ge(q_ps[s], layer * PAIRS + pair + 1)
                    q = bank(QB).rearrange("p (g d) -> p g d", d=DH)
                    stp.done(dve.tensor_reduce(qmax[s][:, :], q, AX.X, ALU.max))
                    dve.tensor_tensor(qs[s][:, :].rearrange("p (g d) -> p g d", d=DH), q,
                                      qmax[s][:, :].unsqueeze(2).broadcast_to([P, T * HEADS, DH]),
                                      ALU.subtract).then_inc(qs_ready[s], 1)

                def masked(pair, s):
                    dve.wait_ge(g_ps[s], layer * PAIRS + pair + 1)
                    for r in range(2):
                        dve.tensor_tensor(cm[s][:, r:NB - 2:2, 0:CW],
                                          bank(GB[r])[:, 0:3 * CW].rearrange("p (u c) -> p u c", c=CW),
                                          head_mask.unsqueeze(1).broadcast_to([P, 3, CW]), ALU.mult)
                    dve.tensor_tensor(cm[s][:, NB - 2, 0:CW], bank(GB[2])[:, 0:CW], head_mask,
                                      ALU.mult).then_inc(cm_ready[s], 1)

                def attended(pair, stp, s):
                    dve.wait_ge(o_ps[s], layer * PAIRS + pair + 1)
                    o = ps[:, KVB[0]:KVB[0] + 2, 0:2 * OW].rearrange("p b (t c) -> p b t c", c=OW)
                    by_head = "p (b t h) -> p b t h"
                    stp.done(dve.tensor_copy(qeps[s][:, :].rearrange(by_head, b=2, t=2), o[:, :, :, CW:OW]))
                    stp.done(dve.tensor_tensor(den[s][:, :].rearrange(by_head, b=2, t=2), o[:, :, :, P:CW],
                                               qeps[s][:, :].rearrange(by_head, b=2, t=2), ALU.max))
                    stp.done(dve.reciprocal(rden[s][:, :], den[s][:, :]))
                    for i in range(2):
                        r = rden[s][:, 2 * i * HEADS:2 * (i + 1) * HEADS].rearrange("p (t h) -> p t h", h=HEADS)
                        ins = dve.tensor_tensor(att[s][:, 2 * i:2 * i + 2, :].rearrange("p t (h d) -> p t h d", d=DH),
                                                o[:, i, :, 0:P].rearrange("p t (h d) -> p t h d", d=DH),
                                                r.unsqueeze(3).broadcast_to([P, 2, HEADS, DH]), ALU.mult)
                    ins.then_inc(att_ready[s], 1)

                def attn_residual(pair, stp, s):
                    a = layer * PAIRS + pair
                    dve.wait_ge(wo_ps[s], a + 1)
                    dve.wait_ge(bo_added[s], a + 1)
                    residual(stp, s, pair)

                def k_of(pair):
                    return layer * (2 * PAIRS) + pair + PAIRS

                stp = steps(0, "la_front")
                for s in range(2):
                    queries(0, stp, s)
                for s in range(2):
                    masked(0, s)
                stp.close()
                with dve.Fori(1, PAIRS) as pair:
                    front, back = steps(pair, "la_front"), steps(pair - 1, "la_back")
                    attended(pair - 1, back, 0)
                    queries(pair, front, 0)
                    queries(pair, front, 1)
                    attended(pair - 1, back, 1)
                    for s in range(2):
                        attn_residual(pair - 1, back, s)
                        masked(pair, s)
                        x_stats(back, s, pair - 1, k_of(pair - 1))
                    front.close()
                    back.close()
                stp = steps(PAIRS - 1, "la_back")
                for s in range(2):
                    attended(PAIRS - 1, stp, s)
                for s in range(2):
                    attn_residual(PAIRS - 1, stp, s)
                    x_stats(stp, s, PAIRS - 1, k_of(PAIRS - 1))
                stp.close()
                with dve.Fori(0, PAIRS) as pair:
                    a = layer * PAIRS + pair
                    k = layer * (2 * PAIRS) + pair + 2 * PAIRS
                    stp = Steps(dve, dve_steps["lf"], a * DVE_STEPS["lf"], DVE_STEPS["lf"])
                    prepare(pair, k)
                    for s in range(2):
                        dve.wait_ge(yT_ps[s], a + (PAIRS + 1))
                        residual(stp, s, pair)
                        x_stats(stp, s, pair, k)
                    stp.close()

            def gate_stats(b):
                dve.wait_ge(gh_ready, b + 1)
                carry_wait()
                for t in range(T):
                    ins = dve.bn_stats(st[0][:, t, :], tile_of(h_tok, b, t))
                ins.then_inc(gst_ready, 1)

            def gate_top(b):
                stp = Steps(dve, dve_steps["mg"], b * DVE_STEPS["mg"], DVE_STEPS["mg"])
                dve.wait_ge(gl_ps, b + 1)
                carry_wait()
                for t in range(T):
                    ins = dve.max(top[:, t, :], bank(GLB)[:, t * E:(t + 1) * E])
                stp.done(ins)
                dve.tensor_tensor(gap[:, :], top[:, :, 1], top[:, :, 0], ALU.subtract).then_inc(gap_ready, 1)
                stp.close()

            def gate_share(b):
                dve.wait_ge(gden_ready, b + 1)
                dve.reciprocal(p1[:, :], gden[:, :]).then_inc(p1_ready, 1)

            def input_lo(b):
                dve.wait_ge(x1_hi_ready, b + 1)
                dve.tensor_tensor(x1_lo[:, turn(b)], bank(GTB), x1_hi[:, turn(b)].bitcast(F32),
                                  ALU.subtract).then_inc(x1_ready, 1)

            def second(b, u):
                dve.wait_ge(mz_ps, b * (E * J) + (u + 1))
                dve.tensor_tensor(z2[u % 2][:, :], bank(MZB[u % 4]), rb[:, turn(b)], ALU.mult).then_inc(mz2_ready, 1)

            def result(b):
                dve.wait_ge(myT_ps, b + 1)
                hs = h_tok[:, seq(b), :]
                dve.tensor_tensor(hs, bank(MTB).rearrange("p (t q) -> p t q", t=T), hs, ALU.add).then_inc(out_ready, 1)

            def experts(b, first=False, last=False):
                for u in range(E * J):
                    if u + 1 < E * J:
                        second(b, u + 1)
                    elif not last:
                        dve.wait_ge(rb_ready, b + 2)
                        second(b + 1, 0)
                    dve.wait_ge(mg_ready, b * (E * J) + (u + 1))
                    dve.tensor_tensor(hid[u % 4][:, :], g1[u % 2][:, :], g2[u % 2][:, :], ALU.add).then_inc(mh_ready, 1)
                    if u == AT["result"] and not first:
                        result(b - 1)
                    if not last:
                        if u == AT["stats"]:
                            gate_stats(b + 1)
                        if u == AT["top"]:
                            gate_top(b + 1)
                        if u == AT["share"]:
                            gate_share(b + 1)
                        if u == AT["input_lo"]:
                            input_lo(b + 1)

            gate_stats(0)
            gate_top(0)
            gate_share(0)
            input_lo(0)
            dve.wait_ge(rb_ready, 1)
            second(0, 0)
            experts(0, first=True)
            with dve.Fori(1, B - 1) as b:
                experts(b)
            experts(B - 1, last=True)
            result(B - 1)

        @block.scalar
        def _(act):
            act.wait_ge(d_tok, 16)
            act.preload_act_table_set("exp_and_others")
            with act.Fori(0, PAIRS) as pair:
                for s in range(2):
                    act.wait_ge(tok_xT_ps[s], pair + 1)
                    act.activation(hT[s][:, :], bank(TB[s]), ACT.Copy).then_inc(tok_xT[s], 1)
                for s in range(2):
                    act.wait_ge(tok_kqv_ps[s], pair * 3 + 1)
                    act.activation(kT[s][:, :], bank(UB[s][0]), ACT.Identity,
                                   bias=w_tok[:, 3 * P:3 * P + 1]).then_inc(tok_kT[s], 1)
                    act.wait_ge(tok_kqv_ps[s], pair * 3 + 3)
                    act.activation(v[s][:, :, 0:P], bank(UB[s][2]).rearrange("p (t q) -> p t q", t=T),
                                   ACT.Copy).then_inc(tok_v[s], 1)
                for i in range(T):
                    for s in range(2):
                        act.wait_ge(tok_max[s], pair * T + (i + 1))
                        act.activation(pr[s][i % 2][:, :], bank(UB[s][i % 2]), ACT.Exp, bias=nmax[s][:, i:i + 1],
                                       accum_out=psums[s][:, i:i + 1]).then_inc(tok_p[s], 1)

            def norm_affine(w, at, k):
                for s in range(2):
                    act.wait_ge(nT_ps[s], k + 1)
                    act.activation(hT[s][:, :], bank(TB[s]), ACT.Identity, scale=w[:, at:at + 1],
                                   bias=w[:, at + 1:at + 2]).then_inc(hT_ready[s], 1)

            def feed_forward(k, f):
                norm_affine(w_f, 2 * FF, k)

                def out_bias(s):
                    act.wait_ge(y_ps[s], f + 1)
                    act.activation(yT[s][:, :], bank(YB[s]), ACT.Identity,
                                   bias=w_f[:, F_COLS - 1:F_COLS]).then_inc(yT_ready[s], 1)

                for u in range(2 * J):
                    act.wait_ge(z_ps, f * (2 * J) + (u + 1))
                    c = 2 * FF + 2 + u % J
                    act.activation(g[u % 3][:, :], bank(ZB[u % 4]), ACT.Gelu, bias=w_f[:, c:c + 1]).then_inc(g_ready, 1)
                    if u == J + 1:
                        out_bias(0)
                out_bias(1)

            act.preload_act_table_set("gelu_and_others")
            with act.Fori(0, PAIRS) as pair:
                act.wait_ge(d_f, 16)
                feed_forward(pair, pair)
            with act.Fori(0, LAYERS) as layer:
                act.preload_act_table_set("exp_and_others")

                def k_of(pair):
                    return layer * (2 * PAIRS) + pair + PAIRS

                def keys_values(pair, s):
                    a = layer * PAIRS + pair
                    for i in range(2):
                        act.wait_ge(kv_ps[s], a * 2 + (i + 1))
                        kv = bank(KVB[i]).rearrange("p (t c) -> p t c", t=2)
                        act.activation(ek[s][:, 2 * i:2 * i + 2, :], kv[:, :, 0:P], ACT.Exp)
                        ins = act.activation(v[s][:, 2 * i:2 * i + 2, 0:P], kv[:, :, P:2 * P], ACT.Copy)
                    ins.then_inc(v_ready[s], 1)

                def exp_queries(pair, s):
                    act.wait_ge(qs_ready[s], layer * PAIRS + pair + 1)
                    act.activation(eq[s][:, :], qs[s][:, :], ACT.Exp).then_inc(eq_ready[s], 1)

                def transposed(pair, s, ps_ready, dst, done):
                    act.wait_ge(ps_ready[s], layer * PAIRS + pair + 1)
                    act.activation(dst[s][:, :], bank(TB[s]), ACT.Copy).then_inc(done[s], 1)

                def prepare(pair, s):
                    k, nxt = k_of(pair), (pair + 1) % PAIRS
                    act.wait_ge(nT_ps[s], k + 1)
                    act.wait_ge(next_rstd[s], k + 2)
                    for t in range(T):
                        ins = act.activation(n[s][:, t, :], one(x, nxt, s, t), ACT.Identity,
                                             scale=one(rstd, nxt, s, t), bias=one(nbias, nxt, s, t))
                    ins.then_inc(n_ready[s], 1)

                act.wait_ge(d_la, layer * 16 + 16)
                norm_affine(w_la, 4 * P, k_of(0))
                for s in range(2):
                    keys_values(0, s)
                    exp_queries(0, s)
                    prepare(0, s)
                for s in range(2):
                    transposed(0, s, qT_ps, qT, qT_ready)
                with act.Fori(1, PAIRS) as pair:
                    norm_affine(w_la, 4 * P, k_of(pair))
                    exp_queries(pair, 0)
                    keys_values(pair, 0)
                    transposed(pair - 1, 0, aT_ps, aT, aT_ready)
                    exp_queries(pair, 1)
                    prepare(pair, 0)
                    transposed(pair, 0, qT_ps, qT, qT_ready)
                    keys_values(pair, 1)
                    transposed(pair - 1, 1, aT_ps, aT, aT_ready)
                    prepare(pair, 1)
                    transposed(pair, 1, qT_ps, qT, qT_ready)
                for s in range(2):
                    transposed(PAIRS - 1, s, aT_ps, aT, aT_ready)
                act.preload_act_table_set("gelu_and_others")
                with act.Fori(0, PAIRS) as pair:
                    a = layer * PAIRS + pair
                    act.wait_ge(d_f, layer * 16 + 32)
                    feed_forward(layer * (2 * PAIRS) + pair + 2 * PAIRS, a + PAIRS)

            def gate_transposed(b):
                act.wait_ge(gxT_ps, b + 1)
                act.activation(gT[:, :], bank(GTB), ACT.Copy).then_inc(gxT_ready, 1)

            def input_hi(b):
                act.wait_ge(xs_ps, b + 1)
                act.activation(x1_hi[:, turn(b)], bank(GTB), ACT.Copy).then_inc(x1_hi_ready, 1)

            def ratios(b):
                act.activation(rb[:, turn(b)], bank(GLB), ACT.Copy).then_inc(rb_ready, 1)

            def out_bias(b):
                act.wait_ge(my_ps, b + 1)
                act.activation(yT[0][:, :], bank(MYB), ACT.Identity, bias=b2_twice[:, 0:1]).then_inc(myT_ready, 1)

            def experts(b, first=False, last=False):
                for u in range(E * J):
                    act.wait_ge(mz2_ready, b * (E * J) + (u + 1))
                    b1 = c_moe[:, E + u:E + u + 1]
                    act.activation(g1[u % 2][:, :], bank(MZB[u % 4]), ACT.Gelu, bias=b1)
                    act.activation(g2[u % 2][:, :], z2[u % 2][:, :], ACT.Gelu, bias=b1).then_inc(mg_ready, 1)
                    if u == 0 and not first:
                        out_bias(b - 1)
                    if not last:
                        if u == AT["transposed"]:
                            gate_transposed(b + 1)
                        if u == AT["input_hi"]:
                            input_hi(b + 1)
                        if u == AT["ratios"]:
                            ratios(b + 1)

            act.wait_ge(d_cmoe, 16)
            act.wait_ge(setup_dve, 2)
            gate_transposed(0)
            input_hi(0)
            ratios(0)
            experts(0, first=True)
            with act.Fori(1, B - 1) as b:
                experts(b)
            experts(B - 1, last=True)
            out_bias(B - 1)

        @block.tensor
        def _(pe):
            pe.wait_ge(d_con, 16)
            pe.wait_ge(d_tok, 16)
            def token_attention(pair, later):
                for s in range(2):
                    pe.wait_ge(tok_x[s], pair + 1)
                    transposes(pe, TB[s], lambda t: n[s][:, t, :]).then_inc(tok_xT_ps[s], 1)
                for s in range(2):
                    pe.wait_ge(tok_xT[s], pair + 1)
                    for i in range(2):
                        pe.matmul(bank(UB[s][i]), w_tok[:, i * P:(i + 1) * P], hT[s][:, :],
                                  start=True, stop=True).then_inc(tok_kqv_ps[s], 1)
                    if later:
                        pe.wait_ge(tok_o_read[s], pair)
                    for t in range(T):
                        ins = pe.matmul(bank(UB[s][2])[:, t * P:(t + 1) * P], hT[s][:, t * P:(t + 1) * P],
                                        w_tok[:, 2 * P:3 * P], start=True, stop=True)
                    ins.then_inc(tok_kqv_ps[s], 1)
                for i in range(T + 2):
                    for s in range(2):
                        if i < T:
                            if i == 0:
                                pe.wait_ge(tok_kT[s], pair + 1)
                                pe.wait_ge(tok_qT[s], pair + 1)
                            pe.matmul(bank(UB[s][i % 2]), kT[s][:, i * P:(i + 1) * P], qT[s][:, :],
                                      start=True, stop=True).then_inc(tok_s_ps[s], 1)
                    for s in range(2):
                        if 1 <= i <= T:
                            pe.wait_ge(tok_p[s], pair * T + i)
                            if i >= 2:
                                pe.wait_ge(tok_pT[s], pair * T + (i - 1))
                            transposes(pe, TB[s], lambda t: pr[s][(i - 1) % 2][:, t * P:(t + 1) * P]
                                       ).then_inc(tok_pT_ps[s], 1)
                    for s in range(2):
                        if i >= 2:
                            if i == 2:
                                pe.wait_ge(tok_v[s], pair + 1)
                            pe.wait_ge(tok_pT[s], pair * T + (i - 1))
                            for t in range(T):
                                ins = pe.matmul(bank(UB[s][2])[:, (i - 2) * P:(i - 1) * P], prT[s][i % 2][:, t, :],
                                                v[s][:, t, 0:P], start=(t == 0), stop=(t == T - 1))
                            if i == T + 1:
                                ins.then_inc(tok_o_ps[s], 1)

            token_attention(0, False)
            with pe.Fori(1, PAIRS) as pair:
                token_attention(pair, True)

            def norm_transposes(k):
                for s in range(2):
                    pe.wait_ge(n_ready[s], k + 1)
                    pe.wait_ge(t_free[s], k + 1)
                    transposes(pe, TB[s], lambda t: n[s][:, t, :]).then_inc(nT_ps[s], 1)

            def feed_forward(k, f):
                norm_transposes(k)
                lag = 2
                for u in range(2 * J + lag):
                    if u < 2 * J:
                        s, j = divmod(u, J)
                        if j == 0:
                            pe.wait_ge(hT_ready[s], k + 1)
                        pe.matmul(bank(ZB[u % 4]), w_f[:, j * P:(j + 1) * P], hT[s][:, :],
                                  start=True, stop=True).then_inc(z_ps, 1)
                    if u >= lag:
                        s, j = divmod(u - lag, J)
                        pe.wait_ge(g_ready, f * (2 * J) + (u - lag + 1))
                        ins = pe.matmul(bank(YB[s]), w_f[:, FF + j * P:FF + (j + 1) * P], g[(u - lag) % 3][:, :],
                                        start=(j == 0), stop=(j == J - 1))
                        if j == J - 1:
                            ins.then_inc(y_ps[s], 1)
                for s in range(2):
                    pe.wait_ge(yT_ready[s], f + 1)
                    transposes(pe, TB[s], lambda t: yT[s][:, t * P:(t + 1) * P]).then_inc(yT_ps[s], 1)

            with pe.Fori(0, PAIRS) as pair:
                pe.wait_ge(d_f, 16)
                feed_forward(pair, pair)
            pe.wait_ge(setup_dve, 1)
            with pe.Fori(0, LAYERS) as layer:
                def k_of(pair):
                    return layer * (2 * PAIRS) + pair + PAIRS

                def queries(pair, s):
                    pe.wait_ge(hT_ready[s], k_of(pair) + 1)
                    if s == 1:
                        pe.wait_ge(qs_ready[0], layer * PAIRS + pair + 1)
                    for t in range(T):
                        ins = pe.matmul(bank(QB)[:, t * P:(t + 1) * P], hT[s][:, t * P:(t + 1) * P], w_la[:, 0:P],
                                        start=True, stop=True)
                    ins.then_inc(q_ps[s], 1)

                def keys_values(s):
                    for t in range(T):
                        c = (t % 2) * 2 * P
                        ins = pe.matmul(bank(KVB[t // 2])[:, c:c + 2 * P], hT[s][:, t * P:(t + 1) * P],
                                        w_la[:, P:3 * P], start=True, stop=True)
                        if t % 2:
                            ins.then_inc(kv_ps[s], 1)

                def contexts(pair, s):
                    pe.wait_ge(v_ready[s], layer * PAIRS + pair + 1)
                    if s == 1:
                        pe.wait_ge(cm_ready[0], layer * PAIRS + pair + 1)
                    for u in range(NB - 1):
                        r = BUCKET * (u % 2)
                        dst = bank(GB[2])[:, 0:CW] if u == NB - 2 else bank(GB[u % 2])[:, (u // 2) * CW:(u // 2 + 1) * CW]
                        ins = pe.matmul(dst, ek[s][r:r + BUCKET, u // 2, :], v[s][r:r + BUCKET, u // 2, :],
                                        start=True, stop=True)
                    ins.then_inc(g_ps[s], 1)

                def query_transposes(pair, s, later):
                    pe.wait_ge(eq_ready[s], layer * PAIRS + pair + 1)
                    if later:
                        pe.wait_ge(t_free[s], k_of(pair) + 1)
                    transposes(pe, TB[s], lambda t: eq[s][:, t * P:(t + 1) * P]).then_inc(qT_ps[s], 1)

                def products(pair, s):
                    pe.wait_ge(qT_ready[s], layer * PAIRS + pair + 1)
                    pe.wait_ge(ctx_ready[s], layer * PAIRS + pair + 1)
                    for u in range(NB):
                        t, r = u // 2, BUCKET * (u % 2)
                        ctx_u = zero_ctx[:, :] if u == 0 else cm[s][:, u - 1, :]
                        ins = pe.matmul(bank(KVB[t // 2])[r:r + BUCKET, (t % 2) * OW:(t % 2 + 1) * OW],
                                        qT[s][:, u * BUCKET:(u + 1) * BUCKET], ctx_u, start=True, stop=True)
                    ins.then_inc(o_ps[s], 1)

                def attended_transposes(s):
                    transposes(pe, TB[s], lambda t: att[s][:, t, :]).then_inc(aT_ps[s], 1)

                def output(pair, s):
                    pe.wait_ge(aT_ready[s], layer * PAIRS + pair + 1)
                    for t in range(T):
                        ins = pe.matmul(bank(TB[s])[:, t * P:(t + 1) * P], aT[s][:, t * P:(t + 1) * P],
                                        w_la[:, 3 * P:4 * P], start=True, stop=True)
                    ins.then_inc(wo_ps[s], 1)

                def later_norm(pair, s):
                    pe.wait_ge(n_ready[s], k_of(pair) + 1)
                    pe.wait_ge(qT_ready[s], layer * PAIRS + pair)
                    transposes(pe, TB[s], lambda t: n[s][:, t, :]).then_inc(nT_ps[s], 1)

                pe.wait_ge(d_la, layer * 16 + 16)
                norm_transposes(k_of(0))
                queries(0, 0)
                keys_values(0)
                queries(0, 1)
                pe.wait_ge(v_ready[0], layer * PAIRS + 1)
                keys_values(1)
                for s in range(2):
                    contexts(0, s)
                    query_transposes(0, s, False)
                with pe.Fori(1, PAIRS) as pair:
                    a = layer * PAIRS + pair
                    later_norm(pair, 0)
                    products(pair - 1, 0)
                    later_norm(pair, 1)
                    queries(pair, 0)
                    pe.wait_ge(att_ready[0], a)
                    keys_values(0)
                    attended_transposes(0)
                    queries(pair, 1)
                    pe.wait_ge(v_ready[0], a + 1)
                    products(pair - 1, 1)
                    output(pair - 1, 0)
                    contexts(pair, 0)
                    query_transposes(pair, 0, True)
                    pe.wait_ge(att_ready[1], a)
                    keys_values(1)
                    attended_transposes(1)
                    output(pair - 1, 1)
                    contexts(pair, 1)
                    query_transposes(pair, 1, True)
                products(PAIRS - 1, 0)
                pe.wait_ge(att_ready[0], layer * PAIRS + PAIRS)
                products(PAIRS - 1, 1)
                attended_transposes(0)
                output(PAIRS - 1, 0)
                pe.wait_ge(att_ready[1], layer * PAIRS + PAIRS)
                attended_transposes(1)
                output(PAIRS - 1, 1)
                with pe.Fori(0, PAIRS) as pair:
                    pe.wait_ge(d_f, layer * 16 + 32)
                    feed_forward(layer * (2 * PAIRS) + pair + 2 * PAIRS, layer * PAIRS + pair + PAIRS)

            def gate_transposes(b):
                pe.wait_ge(gx_ready, b + 1)
                transposes(pe, GTB, lambda t: gx[:, t, :]).then_inc(gxT_ps, 1)

            def logits(b):
                pe.wait_ge(gxT_ready, b + 1)
                for t in range(T):
                    ins = pe.matmul(bank(GLB)[:, t * E:(t + 1) * E], gT[:, t * P:(t + 1) * P], c_moe[:, 0:E],
                                    start=True, stop=True)
                ins.then_inc(gl_ps, 1)

            def input_transposes(b):
                pe.wait_ge(xs_ready, b + 1)
                transposes(pe, GTB, lambda t: xs[:, t, :])
                for t in range(T):
                    ins = pe.matmul(bank(GLB)[:, t * P:(t + 1) * P], ratio[:, t:t + 1].broadcast_to([P, P]), ident,
                                    start=True, stop=True)
                ins.then_inc(xs_ps, 1)

            def up(b, u):
                w = slice(u * P, (u + 1) * P)
                dst = bank(MZB[u % 4])
                pe.matmul(dst, w_up_hi[:, w], x1_hi[:, turn(b)], start=True, stop=False)
                pe.matmul(dst, w_up_hi[:, w], x1_lo[:, turn(b)], start=False, stop=False)
                pe.matmul(dst, w_up_lo[:, w], x1_hi[:, turn(b)], start=False, stop=True).then_inc(mz_ps, 1)

            def result_transposes(b):
                pe.wait_ge(myT_ready, b + 1)
                transposes(pe, MTB, lambda t: yT[0][:, t * P:(t + 1) * P]).then_inc(myT_ps, 1)

            lead = 3

            def experts(b, first=False, last=False):
                for u in range(E * J):
                    if u + lead < E * J:
                        up(b, u + lead)
                    elif not last:
                        if u + lead == E * J:
                            pe.wait_ge(x1_ready, b + 2)
                        up(b + 1, u + lead - E * J)
                    if u == 0 and not first:
                        pe.wait_ge(myT_ready, b)
                    pe.wait_ge(mh_ready, b * (E * J) + (u + 1))
                    ins = pe.matmul(bank(MYB), w_down[:, u * P:(u + 1) * P], hid[u % 4][:, :],
                                    start=(u == 0), stop=(u == E * J - 1))
                    if u == AT["result_T"] and not first:
                        result_transposes(b - 1)
                    if not last:
                        if u == AT["gate_T"]:
                            gate_transposes(b + 1)
                        if u == AT["logits"]:
                            logits(b + 1)
                        if u == AT["input_T"]:
                            input_transposes(b + 1)
                ins.then_inc(my_ps, 1)

            pe.wait_ge(d_cmoe, 16)
            gate_transposes(0)
            logits(0)
            input_transposes(0)
            pe.wait_ge(d_down, 16)
            pe.wait_ge(up_ready, LAYERS)
            pe.wait_ge(x1_ready, 1)
            for u in range(lead):
                up(0, u)
            experts(0, first=True)
            with pe.Fori(1, B - 1) as b:
                experts(b)
            experts(B - 1, last=True)
            result_transposes(B - 1)


def position_code():
    at = np.arange(S, dtype=np.float32)[:, None]
    i = np.arange(P, dtype=np.float32)[None, :]
    ang = at / np.power(np.float32(10000.0), np.float32(2.0) * i / np.float32(P))
    code = np.where((np.arange(P) % 2 == 0)[None, :], np.sin(ang), np.cos(ang)).astype(np.float32)
    return np.ascontiguousarray((code * np.float32(P ** 0.5)).reshape(T, P, P).transpose(1, 0, 2))


def constants():
    head = np.arange(P) // DH
    mask = np.concatenate([head[:, None] == head[None, :], head[:, None] == np.arange(HEADS)[None, :]], axis=1)
    return np.concatenate([np.eye(P, dtype=np.float32), mask.astype(np.float32)], axis=1)


def kernel(**inputs):
    import concourse.bacc as bacc
    from concourse.bass_utils import run_bass_kernel_spmd

    a = {k: np.asarray(v) for k, v in inputs.items()}

    def blocks(w):
        return w.reshape(*w.shape[:-2], J, P, P).swapaxes(-3, -2).reshape(*w.shape[:-2], P, J * P)

    def col(v):
        return v[..., None]

    def cols(v):
        return v.reshape(*v.shape[:-1], J, P).swapaxes(-1, -2)

    t = {k[7:]: v for k, v in a.items() if k.startswith("L0_tok_")}
    l = {k[8:]: v for k, v in a.items() if k.startswith("L0_attn_")}
    m = {k[7:]: v for k, v in a.items() if k.startswith("L0_ffn_")}
    one, zero = np.ones((P, 1), np.float32), np.zeros((P, 1), np.float32)
    ffn_tok = np.concatenate([t["w1"], blocks(t["w2"]), one, zero, cols(t["b1"]), col(t["b2"])], axis=1)
    ffn_l = np.concatenate([l["w1"], blocks(l["w2"]), col(l["ln2_g"]), col(l["ln2_b"]), cols(l["b1"]), col(l["b2"])],
                           axis=2)
    arrays = {
        "ids": np.ascontiguousarray(a["x"].reshape(B * T, P).T),
        "emb": t["emb"],
        "pos": position_code(),
        "consts": constants(),
        "tok_w": np.concatenate([t["wk"], t["wq"], t["wv"], col(t["bk"]), col(t["bq"])], axis=1),
        "tok_rows": np.stack([t["bv"], t["ln_g"], t["ln_b"]]),
        "attn_w": np.concatenate([l["wq"], l["wk"], l["wv"], l["wo"], col(l["ln1_g"]), col(l["ln1_b"])], axis=2),
        "attn_bo": l["bo"],
        "ffn_w": np.concatenate([ffn_tok[None], ffn_l], axis=0),
        "moe_up": m["W1"].transpose(1, 0, 2).reshape(P, E * FF),
        "moe_down": blocks(m["W2"]).transpose(1, 0, 2).reshape(P, E * FF),
        "moe_c": np.concatenate([m["Wg"], cols(m["b1"]).transpose(1, 0, 2).reshape(P, E * J), m["b2"].T], axis=1),
    }
    nc = bacc.Bacc("TRN2", target_bir_lowering=False, num_devices=1)
    args = []
    for name, v in arrays.items():
        arrays[name] = v = np.ascontiguousarray(v)
        args.append(nc.dram_tensor(name, v.shape, mybir.dt.from_np(v.dtype), kind="ExternalInput").ap())
    out = nc.dram_tensor("out", (B, S, P), mybir.dt.float32, kind="ExternalOutput").ap()
    build(nc, *args, out)
    r = run_bass_kernel_spmd(nc, [arrays], core_ids=[0])
    return r.results[0]["out"]
```

```python
from contextlib import ExitStack

import numpy as np

import concourse.bass as bass
from concourse import mybir

P = 128
B = 8
S = 512
T = S // P
PAIRS = B // 2
LAYERS = 4
HEADS = 8
DH = P // HEADS
BUCKET = 64
NB = S // BUCKET
FF = 512
J = FF // P
E = 8
CW = P + HEADS
OW = CW + HEADS
EPS_LN = 1e-5
EPS_ATTN = 1e-3
LA_COLS = 4 * P + 2
UP_COLS = E * FF // LAYERS
F_COLS = 2 * FF + 2 + J + 1

DVE_STEPS = dict(ta=4, ta_ln=8, tf_0=4, tf_1=12, la_front=2, la_back=14, lf=4, end=1, mg=1)
POOL_STEPS = dict(ta=4, tf_0=2, tf_1=12, la_front=10, la_back=4, lf=2, mg=9)


AT = dict(result_T=3, result=6, stats=2, gate_T=8, transposed=11, logits=12, top=15, share=18, input_T=21,
          input_hi=24, ratios=25, input_lo=26)
GATE_AT = dict(norm=1, ratio=15, input=17)

SPLIT = [u for u in range(E * J) if u % 2 and u not in (3, 5, 19, E * J - 1)]
WHOLE = [u for u in range(E * J) if u not in SPLIT]
SPLIT_LAG = 2
DN_COLS = -(-len(SPLIT) // LAYERS) * P

TOK_INPUT = (0, 2)


class Steps:

    def __init__(self, eng, sem, base, per):
        self.eng, self.sem, self.base, self.per, self.n = eng, sem, base, per, 0

    def done(self, ins):
        self.n += 1
        ins.then_inc(self.sem, 1)
        self.eng.wait_ge(self.sem, self.base + self.n)

    def close(self):
        assert self.n == self.per, (self.n, self.per)


def build(nc, ids, emb, pos, consts, tok_w, tok_rows, attn_w, attn_bo, ffn_w, moe_up, moe_dn, moe_down, moe_c, out):
    ACT = mybir.ActivationFunctionType
    ALU = mybir.AluOpType
    AX = mybir.AxisListType
    F32 = mybir.dt.float32
    F32R = mybir.dt.float32r
    I32 = mybir.dt.int32
    ctx = ExitStack()
    with ctx:
        def sb(name, shape, dt=F32):
            return ctx.enter_context(nc.sbuf_tensor(name, shape, dt))

        def sem(name):
            return ctx.enter_context(nc.semaphore(name))

        def sem2(name):
            return [sem(f"{name}_{s}") for s in range(2)]

        x = sb("x", [P, B * T, P])
        h_tok = sb("h_tok", [P, B * T, P])
        rstd = sb("rstd", [P, B * T])
        nbias = sb("nbias", [P, B * T])
        idx = sb("idx", [P, B * T], I32)
        pos_sb = sb("pos_sb", [P, T, P])
        con = sb("con", [P, P + CW])
        ident = con[:, 0:P]
        head_mask = con[:, P:P + CW]
        w_tok = sb("w_tok", [P, 3 * P + 2])
        rows = sb("rows", [P, 3, P])
        w_la = sb("w_la", [P, LA_COLS])
        bo = sb("bo", [P, P])
        w_f = sb("w_f", [P, F_COLS])
        w_up = sb("w_up", [P, UP_COLS])
        w_up_hi = sb("w_up_hi", [P, E * FF], F32R)
        w_up_lo = sb("w_up_lo", [P, E * FF], F32R)
        w_down = sb("w_down", [P, len(WHOLE) * P])
        w_dn = sb("w_dn", [P, DN_COLS])
        w_dn_hi = sb("w_dn_hi", [P, LAYERS * DN_COLS], F32R)
        w_dn_lo = sb("w_dn_lo", [P, LAYERS * DN_COLS], F32R)
        c_moe = sb("c_moe", [P, E + J * E + E])
        scratch = sb("scratch", [P, 1])
        mark = [sb(f"mark{s}", [P, 1]) for s in range(2)]
        pool_scratch = [sb(f"pool_scratch{s}", [P, T]) for s in range(2)]
        b2_sum = sb("b2_sum", [P, 1])
        b2_twice = sb("b2_twice", [P, 1])
        eps_t = sb("eps_t", [P, T])
        mhalf_t = sb("mhalf_t", [P, T])
        quarter_t = sb("quarter_t", [P, T])
        share_t = sb("share_t", [P, T])
        one_t = sb("one_t", [P, T])
        e_t = sb("e_t", [P, T])

        n = [sb(f"n{s}", [P, T, P]) for s in range(2)]
        hT = [sb(f"hT{s}", [P, S]) for s in range(2)]
        nrm = [sb(f"nrm{s}", [P, T, P]) for s in range(2)]
        aff = [sb(f"aff{s}", [P, T, P]) for s in range(2)]
        st = [sb(f"st{s}", [P, T, 6]) for s in range(2)]
        st_sum = [sb(f"st_sum{s}", [P, T]) for s in range(2)]
        st_dif = [sb(f"st_dif{s}", [P, T]) for s in range(2)]
        st_m2 = [sb(f"st_m2{s}", [P, T]) for s in range(2)]
        st_dd = [sb(f"st_dd{s}", [P, T]) for s in range(2)]
        st_nmean = [sb(f"st_nmean{s}", [P, T]) for s in range(2)]
        st_var = [sb(f"st_var{s}", [P, T]) for s in range(2)]
        st_ve = [sb(f"st_ve{s}", [P, T]) for s in range(2)]
        st_rs = [sb(f"st_rs{s}", [P, T]) for s in range(2)]
        tower_var = [sb(f"tower_var{s}", [P, T]) for s in range(2)]
        st_nb = [sb(f"st_nb{s}", [P, T]) for s in range(2)]

        kT = [sb(f"kT{s}", [P, S]) for s in range(2)]
        qT = [sb(f"qT{s}", [P, S]) for s in range(2)]
        v = [sb(f"v{s}", [P, T, CW]) for s in range(2)]
        pr = [[sb(f"pr{s}{i}", [P, S]) for i in range(2)] for s in range(2)]
        g = [sb(f"g{i}", [P, S]) for i in range(4)]
        prT = [[g[2 * s + i][:, :].rearrange("p (t q) -> p t q", t=T) for i in range(2)] for s in range(2)]
        nmax = [sb(f"nmax{s}", [P, T]) for s in range(2)]
        psums = [sb(f"psums{s}", [P, T]) for s in range(2)]
        rsum = [sb(f"rsum{s}", [P, T]) for s in range(2)]

        yT = [sb(f"yT{s}", [P, S]) for s in range(2)]
        ek = [yT[s][:, :].rearrange("p (t d) -> p t d", t=T) for s in range(2)]
        qs = [pr[s][0] for s in range(2)]
        eq = [pr[s][1] for s in range(2)]
        qmax = [sb(f"qmax{s}", [P, T * HEADS]) for s in range(2)]
        qeps = [sb(f"qeps{s}", [P, T * HEADS]) for s in range(2)]
        den = [sb(f"den{s}", [P, T * HEADS]) for s in range(2)]
        rden = [sb(f"rden{s}", [P, T * HEADS]) for s in range(2)]
        cm = [sb(f"cm{s}", [P, NB - 1, OW]) for s in range(2)]
        zero_ctx = sb("zero_ctx", [P, OW])
        att = nrm
        aT = [kT[s] for s in range(2)]

        w1_hi = sb("w1_hi", [P, FF], F32R)
        w1_lo = sb("w1_lo", [P, FF], F32R)

        x1_hi = sb("x1_hi", [P, 2 * S], F32R)
        x1_lo = sb("x1_lo", [P, 2 * S], F32R)
        rb = sb("rb", [P, 2 * S])
        h_hi = [x1_hi[:, s * S:(s + 1) * S] for s in range(2)]
        h_lo = [x1_lo[:, s * S:(s + 1) * S] for s in range(2)]
        mg_sq = sb("mg_sq", [P, T])
        mg_m2 = sb("mg_m2", [P, T])
        top = sb("top", [P, T, 8])
        gap = sb("gap", [P, T])
        ratio = sb("ratio", [P, T])
        gden = sb("gden", [P, T])
        p1 = sb("p1", [P, T])
        gx, xs, gT = n[0], nrm[0], nrm[1][:, :, :].rearrange("p t d -> p (t d)")
        HB = [i % 2 for i in range(len(SPLIT))]
        z2 = [hT[i] for i in range(2)]
        g1 = [pr[0][0], pr[0][1]]
        g2 = [pr[1][0], pr[1][1]]
        hid_hi = [sb(f"hid_hi{i}", [P, S], F32R) for i in range(2)]
        hid_lo = [sb(f"hid_lo{i}", [P, S], F32R) for i in range(2)]
        hid = [kT[0], kT[1], qT[0], qT[1]]

        ps = ctx.enter_context(nc.psum_tensor("ps", [P, 8, 512], F32))

        def bank(i):
            return ps[:, i, :]

        TB = [0, 1]
        UB = [[2, 3, 4], [5, 6, 7]]
        QB, KVB, GB = [2, 7], [3, 4], [5, 6, 7]
        LAST_OB = [3, 5]
        FIRST_NB = [2, 7]
        ZB, YB = [2, 3, 4, 5], [6, 7]
        MZB, MTB, MYB, GTB, GLB = [0, 1, 2, 3], 4, 5, 6, 7
        FIRST_GTB, FIRST_GLB = 1, 2

        d_idx = sem("d_idx")
        STARTS = 5
        d_start = sem("d_start")
        d_la, d_bo, d_f, d_up, d_down, d_out = (sem(f"d_{k}") for k in ("la", "bo", "f", "up", "down", "out"))
        d_gather = sem2("d_gather")
        setup_pool, setup_dve = sem("setup_pool"), sem("setup_dve")
        dve_steps = {k: sem(f"dve_steps_{k}") for k in ("su", *DVE_STEPS)}
        pool_steps = {k: sem(f"pool_steps_{k}") for k in POOL_STEPS}
        stats_ready, ln_rstd, next_rstd = sem2("stats_ready"), sem2("ln_rstd"), sem2("next_rstd")
        nrm_ready = sem2("nrm_ready")
        n_ready, nT_ps, hT_ready, t_free = sem2("n_ready"), sem2("nT_ps"), sem2("hT_ready"), sem2("t_free")
        tok_x, tok_xbv, tok_xT_ps, tok_xT = sem2("tok_x"), sem2("tok_xbv"), sem2("tok_xT_ps"), sem2("tok_xT")
        tok_kqv_ps, tok_kT, tok_qT, tok_v = sem2("tok_kqv_ps"), sem2("tok_kT"), sem2("tok_qT"), sem2("tok_v")
        tok_s_ps, tok_max, tok_p, tok_pT_ps, tok_pT, tok_o_ps, tok_r = (
            sem2(f"tok_{k}") for k in ("s_ps", "max", "p", "pT_ps", "pT", "o_ps", "r"))
        tok_o_read = sem2("tok_o_read")
        q_ps, kv_ps, qs_ready, v_ready, eq_ready, g_ps, qT_ps, qT_ready = (
            sem2(k) for k in ("q_ps", "kv_ps", "qs_ready", "v_ready", "eq_ready", "g_ps", "qT_ps", "qT_ready"))
        cm_ready, ctx_ready, o_ps, att_ready, aT_ps, aT_ready, wo_ps, bo_added = (
            sem2(k) for k in ("cm_ready", "ctx_ready", "o_ps", "att_ready", "aT_ps", "aT_ready", "wo_ps", "bo_added"))
        z_ps, g_ready, y_ps, yT_ready, yT_ps = sem("z_ps"), sem("g_ready"), sem2("y_ps"), sem2("yT_ready"), sem2("yT_ps")
        tok_out_ready = sem2("tok_out_ready")
        h_aff, h_hi_ready, h_split = sem2("h_aff"), sem2("h_hi_ready"), sem2("h_split")
        w1_hi_ready, w1_split = sem("w1_hi_ready"), sem("w1_split")
        gh_ready, gst_ready, gx_ready, gxT_ps, gxT_ready, gl_ps, gap_ready, xs_ready, xs_ps = (
            sem(k) for k in ("gh_ready", "gst_ready", "gx_ready", "gxT_ps", "gxT_ready", "gl_ps", "gap_ready",
                             "xs_ready", "xs_ps"))
        gden_ready, p1_ready = sem("gden_ready"), sem("p1_ready")
        x1_hi_ready, x1_ready, rb_ready, moe_hi_ready, moe_split = (
            sem(k) for k in ("x1_hi_ready", "x1_ready", "rb_ready", "moe_hi_ready", "moe_split"))
        hid_hi_ready, hid_split, hid_used = sem("hid_hi_ready"), sem("hid_split"), sem("hid_used")
        mz_ps, mz2_ready, mg_ready, mh_ready, my_ps, myT_ready, myT_ps, out_ready = (
            sem(k) for k in ("mz_ps", "mz2_ready", "mg_ready", "mh_ready", "my_ps", "myT_ready", "myT_ps",
                             "out_ready"))

        def tiles(pair, s):
            return bass.ds(pair * (2 * T) + s * T, T)

        def seq(b):
            return bass.ds(b * T, T)

        def tile_of(tensor, b, t):
            return tensor[:, bass.ds(b * T + t, 1), :].rearrange("p a d -> p (a d)")

        def turn(b):
            return bass.ds((b % 2) * S, S)

        def one(tensor, pair, s, t):
            at = bass.ds(pair * (2 * T) + (s * T + t), 1)
            if len(tensor.shape) == 2:
                return tensor[:, at]
            return tensor[:, at, :].rearrange("p a d -> p (a d)")

        def transposes(pe, dst, src_tile):
            for t in range(T):
                last = pe.transpose(bank(dst)[:, t * P:(t + 1) * P], src_tile(t), ident)
            return last

        block = ctx.enter_context(nc.Block())

        @block.sync
        def _(sp):
            sp.dma_start(idx[:, :], ids).then_inc(d_idx, 16)
            sp.dma_start(con[:, :], consts).then_inc(d_start, 16)
            sp.dma_start(pos_sb[:, :, :], pos).then_inc(d_start, 16)
            sp.dma_start(w_tok[:, :], tok_w).then_inc(d_start, 16)
            sp.dma_start(rows[:, :, :], tok_rows.partition_broadcast(P)).then_inc(d_start, 16)
            sp.dma_start(c_moe[:, :], moe_c).then_inc(d_start, 16)
            for s in range(2):
                sp.wait_ge(tok_x[s], 1)
            sp.dma_start(w_f[:, :], ffn_w[0]).then_inc(d_f, 16)
            sp.dma_start(w_la[:, :], attn_w[0]).then_inc(d_la, 16)
            sp.dma_start(bo[:, :], attn_bo[0].partition_broadcast(P)).then_inc(d_bo, 16)
            sp.dma_start(w_up[:, :], moe_up[:, 0:UP_COLS]).then_inc(d_up, 16)
            sp.dma_start(w_dn[:, :], moe_dn[:, 0:DN_COLS]).then_inc(d_up, 16)
            sp.dma_start(w_down[:, :], moe_down).then_inc(d_down, 16)
            with sp.Fori(0, LAYERS - 1) as l:
                sp.wait_ge(yT_ready[1], PAIRS * l + PAIRS)
                sp.dma_start(w_f[:, :], ffn_w[bass.ds(l + 1, 1)].rearrange("a p c -> (a p) c")).then_inc(d_f, 16)
                sp.wait_ge(wo_ps[1], PAIRS * l + PAIRS)
                sp.dma_start(w_la[:, :], attn_w[bass.ds(l + 1, 1)].rearrange("a p c -> (a p) c")).then_inc(d_la, 16)
                sp.wait_ge(bo_added[0], PAIRS * l + PAIRS)
                sp.wait_ge(bo_added[1], PAIRS * l + PAIRS)
                sp.dma_start(bo[:, :], attn_bo[bass.ds(l + 1, 1)].rearrange("a d -> (a d)").partition_broadcast(P)
                             ).then_inc(d_bo, 16)
                sp.wait_ge(moe_split, 2 * l + 2)
                sp.dma_start(w_up[:, :], moe_up[:, bass.ds((l + 1) * UP_COLS, UP_COLS)]).then_inc(d_up, 16)
                sp.dma_start(w_dn[:, :], moe_dn[:, bass.ds((l + 1) * DN_COLS, DN_COLS)]).then_inc(d_up, 16)
            sp.wait_ge(yT_ready[1], PAIRS * LAYERS)
            sp.dma_start(w_f[:, :], ffn_w[LAYERS]).then_inc(d_f, 16)
            with sp.Fori(0, B) as b:
                sp.wait_ge(out_ready, b + 1)
                sp.dma_start(out[bass.ds(b, 1)].rearrange("b (t p) d -> p (b t) d", p=P),
                             h_tok[:, bass.ds(b * T, T), :]).then_inc(d_out, 16)
            sp.wait_ge(d_out, 16 * B)

        @block.gpsimd
        def _(pool):
            def carry_wait(s=0):
                pool.tensor_tensor(pool_scratch[s][:, :], one_t[:, :], one_t[:, :], ALU.add)

            def pool_rstd(stp, s, count, rs, nb, done):
                pool.wait_ge(stats_ready[s], count)
                stp.done(pool.tensor_tensor(st_ve[s][:, :], st_var[s][:, :], eps_t[:, :], ALU.add))
                stp.done(pool.tensor_tensor(rs, st_ve[s][:, :], mhalf_t[:, :], ALU.pow))
                pool.tensor_tensor(nb, st_nmean[s][:, :], rs, ALU.mult).then_inc(done[s], 1)

            def inner_rstd(stp, s, count):
                pool_rstd(stp, s, count, st_rs[s][:, :], st_nb[s][:, :], ln_rstd)

            def phase_rstd(stp, s, pair, count):
                pool_rstd(stp, s, count, rstd[:, tiles(pair, s)], nbias[:, tiles(pair, s)], next_rstd)

            def add_row(dst, src, row):
                return pool.tensor_tensor(dst, src, row.unsqueeze(1).broadcast_to([P, T, P]), ALU.add)

            pool.wait_ge(d_idx, 16)
            def gather(p):
                for t in range(2 * T * p, 2 * T * (p + 1)):
                    if p >= 1 and t % T == 0:
                        pool.wait_ge(d_gather[t // T % 2], 16 * T * p)
                    pool.indirect_dma_start(x[:, t, :], None, emb,
                                            bass.IndirectOffsetOnAxis(ap=idx[:, t:t + 1], axis=0)
                                            ).then_inc(d_gather[t // T % 2], 16)

            gather(0)
            for dst, value in ((eps_t, EPS_LN), (mhalf_t, -0.5), (quarter_t, 0.25), (share_t, 1.0 / P), (one_t, 1.0),
                               (e_t, float(np.e))):
                pool.memset(dst[:, :], value).then_inc(setup_pool, 1)
            for q in range(PAIRS):
                for s in range(2):
                    a = (2 * q + s) * T
                    pool.memset(nbias[:, a:a + T], 0.0).then_inc(setup_pool, 1)
                    pool.memset(rstd[:, a:a + T], 1.0).then_inc(next_rstd[s], 1)
            pool.wait_ge(setup_pool, 6 + 2 * PAIRS)
            gather(1)
            pool.wait_ge(d_start, STARTS * 16)

            def split(hi, lo, w, hi_done, count, done, scratch=0):
                pool.tensor_tensor(hi, w, one_t[:, 0:1].broadcast_to([P, w.shape[1]]), ALU.mult).then_inc(hi_done, 1)
                pool.wait_ge(hi_done, count)
                carry_wait(scratch)
                pool.tensor_tensor(lo, w, hi.bitcast(F32), ALU.subtract).then_inc(done, 1)

            def attn_ln(pair, s):
                pool.wait_ge(nrm_ready[s], pair + 1)
                add_row(x[:, tiles(pair, s), :], aff[s][:, :, :], rows[:, 2, :]).then_inc(tok_r[s], 1)

            def attn_input(pair, s):
                pool.wait_ge(tok_x[s], pair + 1)
                add_row(nrm[s][:, :, :], n[s][:, :, :], rows[:, 0, :]).then_inc(tok_xbv[s], 1)

            def attn_rstd(pair):
                stp = Steps(pool, pool_steps["ta"], pair * POOL_STEPS["ta"], POOL_STEPS["ta"])
                for s in range(2):
                    inner_rstd(stp, s, pair + 1)
                stp.close()

            for s in range(2):
                attn_input(0, s)
            gather(2)
            gather(3)
            pool.wait_ge(d_f, 16)
            split(w1_hi[:, :], w1_lo[:, :], w_f[:, 0:FF], w1_hi_ready, 1, w1_split)
            with pool.Fori(1, PAIRS) as pair:
                attn_rstd(pair - 1)
                for s in range(2):
                    attn_ln(pair - 1, s)
                    attn_input(pair, s)
            attn_rstd(PAIRS - 1)
            for s in range(2):
                attn_ln(PAIRS - 1, s)

            def tok_steps(pair, which):
                return Steps(pool, pool_steps[which], pair * POOL_STEPS[which], POOL_STEPS[which])

            def tok_first(pair):
                stp = tok_steps(pair, "tf_0")
                inner_rstd(stp, 0, pair * 2 + (PAIRS + 1))
                stp.close()

            def tok_bias(pair, s):
                pool.wait_ge(nrm_ready[s], pair + (PAIRS + 1))
                add_row(h_tok[:, tiles(pair, s), :], aff[s][:, :, :], rows[:, 2, :]).then_inc(h_aff[s], 1)

            def tok_out_rstd(stp, pair, s):
                inner_rstd(stp, s, pair * 2 + (PAIRS + 2))

            def tower_rstd(stp, pair, s):
                rs, ve = st_rs[s][:, :], st_ve[s][:, :]
                pool.wait_ge(ln_rstd[s], pair * 2 + (PAIRS + 2))
                stp.done(pool.tensor_tensor(ve, rs, rs, ALU.mult))
                stp.done(pool.tensor_tensor(tower_var[s][:, :], ve, st_var[s][:, :], ALU.mult))
                stp.done(pool.tensor_tensor(ve, tower_var[s][:, :], eps_t[:, :], ALU.add))
                carry_wait(s)
                pool.tensor_tensor(rstd[:, tiles(pair, s)], ve, mhalf_t[:, :], ALU.pow).then_inc(next_rstd[s], 1)

            def tok_rest(pair):
                stp = tok_steps(pair, "tf_1")
                inner_rstd(stp, 1, pair * 2 + (PAIRS + 1))
                for s in range(2):
                    tok_bias(pair, s)
                for s in range(2):
                    tok_out_rstd(stp, pair, s)
                for s in range(2):
                    tower_rstd(stp, pair, s)
                stp.close()

            tok_first(0)
            with pool.Fori(1, PAIRS - 1) as pair:
                tok_rest(pair - 1)
                tok_first(pair)
            tok_rest(PAIRS - 2)
            tok_first(PAIRS - 1)

            def layer_phases(layer, first=False, last=False):
                def ff_rstd(layer, pair, s):
                    done = layer * (2 * PAIRS) + pair * 2 + s
                    stp = Steps(pool, pool_steps["lf"], done * POOL_STEPS["lf"], POOL_STEPS["lf"])
                    phase_rstd(stp, s, pair, layer * (2 * PAIRS) + pair + (2 * PAIRS + 9))
                    stp.close()

                def attn_front(pair):
                    k = layer * (2 * PAIRS) + pair + PAIRS
                    for s in range(2):
                        pool.wait_ge(n_ready[s], k + 1)
                        xs_ = x[:, tiles(pair, s), :]
                        add_row(xs_, xs_, bo[:, :]).then_inc(bo_added[s], 1)

                def contexts(pair, stp, s):
                    a = layer * PAIRS + pair
                    pool.wait_ge(cm_ready[s], a + 1)
                    for u in range(1, NB - 1):
                        ins = pool.tensor_tensor(cm[s][:, u, 0:CW], cm[s][:, u - 1, 0:CW], cm[s][:, u, 0:CW], ALU.add)
                        if u < NB - 2:
                            stp.done(ins)
                    ins.then_inc(ctx_ready[s], 1)

                def steps(pair, which):
                    return Steps(pool, pool_steps[which], (layer * PAIRS + pair) * POOL_STEPS[which], POOL_STEPS[which])

                def back_rstd(pair, stp, s):
                    phase_rstd(stp, s, pair, layer * (2 * PAIRS) + pair + (PAIRS + 9))

                pool.wait_ge(d_bo, layer * 16 + 16)
                if first:
                    tok = tok_steps(PAIRS - 1, "tf_1")
                    inner_rstd(tok, 1, (PAIRS - 1) * 2 + (PAIRS + 1))
                    for s in range(2):
                        tok_bias(PAIRS - 1, s)
                if first:
                    for s in range(2):
                        tok_out_rstd(tok, PAIRS - 1, s)
                stp = steps(0, "la_front")
                for s in range(2):
                    contexts(0, stp, s)
                    if first:
                        tower_rstd(tok, PAIRS - 1, s)
                    elif s == 0:
                        ff_rstd(layer - 1, PAIRS - 1, 1)
                stp.close()
                attn_front(0)
                if first:
                    tok.close()
                pool.wait_ge(d_f, layer * 16 + 32)
                split(w1_hi[:, :], w1_lo[:, :], w_f[:, 0:FF], w1_hi_ready, layer + 2, w1_split)
                with pool.Fori(1, PAIRS) as pair:
                    attn_front(pair)
                    front, back = steps(pair, "la_front"), steps(pair - 1, "la_back")
                    for s in range(2):
                        contexts(pair, front, s)
                        back_rstd(pair - 1, back, s)
                    front.close()
                    back.close()
                stp = steps(PAIRS - 1, "la_back")
                for s in range(2):
                    back_rstd(PAIRS - 1, stp, s)
                stp.close()
                part = bass.ds(layer * UP_COLS, UP_COLS)
                pool.wait_ge(d_up, layer * 32 + 32)
                split(w_up_hi[:, part], w_up_lo[:, part], w_up[:, :], moe_hi_ready, 2 * layer + 1, moe_split)
                part = bass.ds(layer * DN_COLS, DN_COLS)
                split(w_dn_hi[:, part], w_dn_lo[:, part], w_dn[:, :], moe_hi_ready, 2 * layer + 2, moe_split, 1)

                if not last:
                    ff_rstd(layer, 0, 0)
                    with pool.Fori(1, PAIRS) as pair:
                        ff_rstd(layer, pair - 1, 1)
                        ff_rstd(layer, pair, 0)

            layer_phases(0, first=True)
            with pool.Fori(1, LAYERS - 1) as layer:
                layer_phases(layer)
            layer_phases(LAYERS - 1, last=True)

            def spread(column):
                return column[:, :].unsqueeze(2).broadcast_to([P, T, P])

            def gate_sum(b):
                hs = h_tok[:, seq(b), :]
                pool.tensor_tensor(hs, hs, x[:, seq(b), :], ALU.add).then_inc(gh_ready, 1)

            def gate_norm(stp, b):
                hs = h_tok[:, seq(b), :]
                pool.wait_ge(gst_ready, b + 1)
                pool.tensor_tensor(st_sum[0][:, :], st[0][:, :, 1], st[0][:, :, 4], ALU.add)
                pool.tensor_tensor(mg_m2[:, :], st[0][:, :, 2], st[0][:, :, 5], ALU.add)
                stp.done(pool.tensor_tensor(st_dif[0][:, :], st[0][:, :, 1], st[0][:, :, 4], ALU.subtract))
                pool.tensor_tensor(st_nmean[0][:, :], st_sum[0][:, :], mhalf_t[:, :], ALU.mult)
                pool.tensor_tensor(st_m2[0][:, :], mg_m2[:, :], share_t[:, :], ALU.mult)
                stp.done(pool.tensor_tensor(mg_sq[:, :], st_dif[0][:, :], st_dif[0][:, :], ALU.mult))
                stp.done(pool.tensor_tensor(st_dd[0][:, :], mg_sq[:, :], quarter_t[:, :], ALU.mult))
                stp.done(pool.tensor_tensor(st_var[0][:, :], st_dd[0][:, :], st_m2[0][:, :], ALU.add))
                stp.done(pool.tensor_tensor(st_ve[0][:, :], st_var[0][:, :], eps_t[:, :], ALU.add))
                stp.done(pool.tensor_tensor(st_rs[0][:, :], st_ve[0][:, :], mhalf_t[:, :], ALU.pow))
                stp.done(pool.tensor_tensor(st_nb[0][:, :], st_nmean[0][:, :], st_rs[0][:, :], ALU.mult))
                carry_wait()
                stp.done(pool.tensor_tensor(xs[:, :, :], hs, spread(st_rs[0]), ALU.mult))
                pool.tensor_tensor(gx[:, :, :], xs[:, :, :], spread(st_nb[0]), ALU.add).then_inc(gx_ready, 1)

            def gate_ratio(stp, b):
                pool.wait_ge(gap_ready, b + 1)
                stp.done(pool.tensor_tensor(ratio[:, :], e_t[:, :], gap[:, :], ALU.pow))
                pool.tensor_tensor(gden[:, :], ratio[:, :], one_t[:, :], ALU.add).then_inc(gden_ready, 1)

            def gate_input(b):
                pool.wait_ge(p1_ready, b + 1)
                pool.tensor_tensor(xs[:, :, :], gx[:, :, :], spread(p1), ALU.mult).then_inc(xs_ready, 1)

            def gate_steps(b):
                return Steps(pool, pool_steps["mg"], b * POOL_STEPS["mg"], POOL_STEPS["mg"])

            def split_hidden(b, i, wait_used):
                at = b * len(SPLIT) + i
                pool.wait_ge(mh_ready, b * (E * J) + (SPLIT[i] + 1))
                if wait_used:
                    pool.wait_ge(hid_used, at - 1)
                src = hid[SPLIT[i] % 4][:, :]
                pool.tensor_tensor(hid_hi[HB[i]][:, :], src, one_t[:, 0:1].broadcast_to([P, S]), ALU.mult
                                   ).then_inc(hid_hi_ready, 1)
                pool.wait_ge(hid_hi_ready, at + 1)
                pool.tensor_tensor(hid_lo[HB[i]][:, :], src, hid_hi[HB[i]][:, :].bitcast(F32), ALU.subtract
                                   ).then_inc(hid_split, 1)

            def experts(b, first=False, last=False):
                if not last:
                    stp = gate_steps(b + 1)
                    gate_sum(b + 1)
                for i, u in enumerate(SPLIT):
                    split_hidden(b, i, i >= 2 or not first)
                    if not last:
                        if u == GATE_AT["norm"]:
                            gate_norm(stp, b + 1)
                        if u == GATE_AT["ratio"]:
                            gate_ratio(stp, b + 1)
                        if u == GATE_AT["input"]:
                            gate_input(b + 1)
                if not last:
                    stp.close()

            pool.wait_ge(t_free[0], 2 * LAYERS * PAIRS + 2)
            pool.wait_ge(nT_ps[0], (1 + 2 * LAYERS) * PAIRS)
            stp = gate_steps(0)
            gate_sum(0)
            gate_norm(stp, 0)
            gate_ratio(stp, 0)
            gate_input(0)
            stp.close()
            for s in range(2):
                pool.wait_ge(t_free[s], (1 + 2 * LAYERS) * PAIRS + 1)
            experts(0, first=True)
            with pool.Fori(1, B - 1) as b:
                experts(b)
            experts(B - 1, last=True)

        @block.vector
        def _(dve):
            def carry_wait():
                dve.memset(scratch[:, :], 0.0)

            def stats(stp, s, src, count, first=None):
                carry_wait()
                for t in range(T):
                    ins = dve.bn_stats(st[s][:, t, :], src(t))
                    if t == 0 and first is not None:
                        ins.then_inc(first, 1)
                stp.done(ins)
                dve.tensor_tensor(st_sum[s][:, :], st[s][:, :, 1], st[s][:, :, 4], ALU.add)
                dve.tensor_tensor(st_dif[s][:, :], st[s][:, :, 1], st[s][:, :, 4], ALU.subtract)
                stp.done(dve.tensor_tensor(st_m2[s][:, :], st[s][:, :, 2], st[s][:, :, 5], ALU.add))
                if count is not None:
                    dve.wait_ge(next_rstd[s], count)
                dve.tensor_scalar(st_nmean[s][:, :], st_sum[s][:, :], -0.5, None, ALU.mult)
                stp.done(dve.scalar_tensor_tensor(st_dd[s][:, :], st_dif[s][:, :], 0.25, st_dif[s][:, :],
                                                  ALU.mult, ALU.mult))
                dve.scalar_tensor_tensor(st_var[s][:, :], st_m2[s][:, :], 1.0 / P, st_dd[s][:, :],
                                         ALU.mult, ALU.add).then_inc(stats_ready[s], 1)

            def normalise(dst, src, rstd_of, nbias_of):
                for t in range(T):
                    ins = dve.tensor_scalar(dst(t), src(t), rstd_of(t), nbias_of(t), ALU.mult, ALU.add)
                return ins

            def gain(stp, s):
                stp.done(normalise(lambda t: aff[s][:, t, :], lambda t: nrm[s][:, t, :], *inner(s)))
                dve.tensor_tensor(aff[s][:, :, :], aff[s][:, :, :], rows[:, 1, :].unsqueeze(1).broadcast_to([P, T, P]),
                                  ALU.mult).then_inc(nrm_ready[s], 1)

            def split_input(k, f, s):
                dve.wait_ge(hT_ready[s], k + 1)
                dve.tensor_copy(h_hi[s], hT[s][:, :]).then_inc(h_hi_ready[s], 1)
                dve.wait_ge(h_hi_ready[s], f + 1)
                dve.tensor_tensor(h_lo[s], hT[s][:, :], h_hi[s].bitcast(F32), ALU.subtract).then_inc(h_split[s], 1)

            def prepare(pair, k):
                nxt = (pair + 1) % PAIRS
                for s in range(2):
                    dve.wait_ge(nT_ps[s], k + 1)
                    dve.wait_ge(next_rstd[s], k + 2)
                    normalise(lambda t: n[s][:, t, :], lambda t: one(x, nxt, s, t),
                              lambda t: one(rstd, nxt, s, t), lambda t: one(nbias, nxt, s, t)
                              ).then_inc(n_ready[s], 1)

            def inner(s):
                return lambda t: st_rs[s][:, t:t + 1], lambda t: st_nb[s][:, t:t + 1]

            dve.wait_ge(d_start, STARTS * 16)
            dve.memset(zero_ctx[:, 0:CW], 0.0)
            floor = head_mask[:, P:CW]
            for c in (zero_ctx[:, CW:OW], *(cm[s][:, u, CW:OW] for s in range(2) for u in range(NB - 1))):
                ins = dve.tensor_scalar(c, floor, EPS_ATTN * float(DH) ** 0.5, None, ALU.mult)
            ins.then_inc(setup_dve, 1)
            dve.tensor_reduce(b2_sum[:, :], c_moe[:, E + J * E:], AX.X, ALU.add).then_inc(dve_steps["su"], 1)
            dve.wait_ge(dve_steps["su"], 1)
            dve.tensor_scalar(b2_twice[:, :], b2_sum[:, :], 2.0, None, ALU.mult).then_inc(setup_dve, 1)


            def token_x(pair):
                for s in range(2):
                    dve.wait_ge(d_gather[s], pair * (16 * T) + 16 * T)
                    dve.scalar_tensor_tensor(n[s][:, :, :], x[:, tiles(pair, s), :], float(P) ** 0.5, pos_sb[:, :, :],
                                             ALU.mult, ALU.add).then_inc(tok_x[s], 1)

            def attn_stats(stp, s):
                stats(stp, s, lambda t: nrm[s][:, t, :], None)

            def attn_gain(stp, pair, s):
                dve.wait_ge(ln_rstd[s], pair + 1)
                gain(stp, s)

            def ln_steps(pair):
                return Steps(dve, dve_steps["ta_ln"], pair * DVE_STEPS["ta_ln"], DVE_STEPS["ta_ln"])

            def token_attention(pair, first=False, last=False):
                for s in range(2):
                    dve.wait_ge(tok_kqv_ps[s], pair * 3 + 2)
                    dve.tensor_scalar(qT[s][:, :], bank(UB[s][1]), w_tok[:, 3 * P + 1:3 * P + 2], float(P) ** -0.5,
                                      ALU.add, ALU.mult).then_inc(tok_qT[s], 1)
                ln = None if first else ln_steps(pair - 1)
                for i in range(T + 1):
                    for s in range(2):
                        if i < T:
                            dve.wait_ge(tok_s_ps[s], pair * T + (i + 1))
                            dve.tensor_reduce(nmax[s][:, i:i + 1], bank(UB[s][i % 2]), AX.X, ALU.max,
                                              negate=True).then_inc(tok_max[s], 1)
                    for s in range(2):
                        if i >= 1:
                            dve.wait_ge(tok_pT_ps[s], pair * T + i)
                            dve.tensor_copy(prT[s][(i - 1) % 2][:, :, :],
                                            bank(TB[s]).rearrange("p (t q) -> p t q", t=T)).then_inc(tok_pT[s], 1)
                    if not first:
                        if i < 2:
                            attn_stats(ln, i)
                        if 1 <= i <= 2:
                            attn_gain(ln, pair - 1, i - 1)
                if not first:
                    ln.close()
                for s in range(2):
                    dve.wait_ge(tok_xbv[s], pair + 1)
                if last:
                    tok_ff_input()
                else:
                    token_x(pair + 1)
                stp = Steps(dve, dve_steps["ta"], pair * DVE_STEPS["ta"], DVE_STEPS["ta"])
                for s in range(2):
                    stp.done(dve.reciprocal(rsum[s][:, :], psums[s][:, :]))
                    dve.wait_ge(tok_o_ps[s], pair + 1)
                    for t in range(T):
                        ins = dve.scalar_tensor_tensor(nrm[s][:, t, :], bank(UB[s][2])[:, t * P:(t + 1) * P],
                                                       rsum[s][:, t:t + 1], nrm[s][:, t, :], ALU.mult, ALU.add)
                        if t == T - 1:
                            ins.then_inc(tok_o_read[s], 1)
                    stp.done(dve.memset(mark[s][:, :], 0.0))
                stp.close()

            def tok_ff_input():
                for s in range(2):
                    dve.memset(v[s][:, :, P:CW], 1.0).then_inc(t_free[s], 1)
                    dve.wait_ge(tok_r[s], 1)
                    dve.wait_ge(next_rstd[s], 1)
                    normalise(lambda t: n[s][:, t, :], lambda t: x[:, s * T + t, :],
                              lambda t: rstd[:, s * T + t:s * T + t + 1], lambda t: nbias[:, s * T + t:s * T + t + 1]
                              ).then_inc(n_ready[s], 1)

            token_x(0)
            token_attention(0, first=True)
            with dve.Fori(1, PAIRS - 1) as pair:
                token_attention(pair)
            token_attention(PAIRS - 1, last=True)

            def tok_steps(pair, which):
                return Steps(dve, dve_steps[which], pair * DVE_STEPS[which], DVE_STEPS[which])

            def tok_sum(stp, pair, s):
                dve.wait_ge(yT_ps[s], pair + 1)
                stp.done(dve.tensor_tensor(nrm[s][:, :, :], bank(TB[s]).rearrange("p (t q) -> p t q", t=T),
                                           x[:, tiles(pair, s), :], ALU.add))
                stats(stp, s, lambda t: nrm[s][:, t, :], pair + PAIRS, t_free[s])

            def tok_gain(stp, pair, s):
                dve.wait_ge(ln_rstd[s], pair * 2 + (PAIRS + 1))
                gain(stp, s)

            def tok_out_stats(stp, pair, s):
                dve.wait_ge(h_aff[s], pair + 1)
                stats(stp, s, lambda t: one(h_tok, pair, s, t), None)

            def tok_out(pair, s):
                dve.wait_ge(ln_rstd[s], pair * 2 + (PAIRS + 2))
                normalise(lambda t: one(x, pair, s, t), lambda t: one(h_tok, pair, s, t), *inner(s)
                          ).then_inc(tok_out_ready[s], 1)

            def tok_ff(pair, first=False, last=False):
                if not first:
                    stp = tok_steps(pair - 1, "tf_1")
                    tok_sum(stp, pair - 1, 1)
                    for s in range(2):
                        tok_gain(stp, pair - 1, s)
                if not last:
                    split_input(pair + 1, pair + 1, 0)
                if not first:
                    for s in range(2):
                        tok_out_stats(stp, pair - 1, s)
                    stp.close()
                if not last:
                    split_input(pair + 1, pair + 1, 1)
                if not first:
                    for s in range(2):
                        tok_out(pair - 1, s)
                stp = tok_steps(pair, "tf_0")
                tok_sum(stp, pair, 0)
                stp.close()

            for s in range(2):
                split_input(0, 0, s)
            ln = ln_steps(PAIRS - 1)
            for s in range(2):
                attn_stats(ln, s)
            for s in range(2):
                attn_gain(ln, PAIRS - 1, s)
            ln.close()
            tok_ff(0, first=True)
            with dve.Fori(1, PAIRS - 1) as pair:
                tok_ff(pair)
            tok_ff(PAIRS - 1, last=True)

            def residual(stp, s, pair):
                xs_ = x[:, tiles(pair, s), :]
                stp.done(dve.tensor_tensor(xs_, bank(TB[s]).rearrange("p (t q) -> p t q", t=T), xs_, ALU.add))
                dve.memset(mark[s][:, :], 0.0).then_inc(t_free[s], 1)

            def x_stats(stp, s, pair, k):
                stats(stp, s, lambda t: one(x, pair, s, t), k + PAIRS)

            def gate_stats(b):
                dve.wait_ge(gh_ready, b + 1)
                carry_wait()
                for t in range(T):
                    ins = dve.bn_stats(st[0][:, t, :], tile_of(h_tok, b, t))
                ins.then_inc(gst_ready, 1)

            def gate_top(b, src=GLB):
                stp = Steps(dve, dve_steps["mg"], b * DVE_STEPS["mg"], DVE_STEPS["mg"])
                dve.wait_ge(gl_ps, b + 1)
                carry_wait()
                for t in range(T):
                    ins = dve.max(top[:, t, :], bank(src)[:, t * E:(t + 1) * E])
                stp.done(ins)
                dve.tensor_tensor(gap[:, :], top[:, :, 1], top[:, :, 0], ALU.subtract).then_inc(gap_ready, 1)
                stp.close()

            def gate_share(b):
                dve.wait_ge(gden_ready, b + 1)
                dve.reciprocal(p1[:, :], gden[:, :]).then_inc(p1_ready, 1)

            def layer_phases(layer, first=False, last=False):
                def steps(pair, which):
                    return Steps(dve, dve_steps[which], (layer * PAIRS + pair) * DVE_STEPS[which], DVE_STEPS[which])

                def queries(pair, stp, s):
                    dve.wait_ge(q_ps[s], layer * PAIRS + pair + 1)
                    q = bank(QB[s]).rearrange("p (g d) -> p g d", d=DH)
                    stp.done(dve.tensor_reduce(qmax[s][:, :], q, AX.X, ALU.max))
                    dve.tensor_tensor(qs[s][:, :].rearrange("p (g d) -> p g d", d=DH), q,
                                      qmax[s][:, :].unsqueeze(2).broadcast_to([P, T * HEADS, DH]),
                                      ALU.subtract).then_inc(qs_ready[s], 1)

                def masked(pair, s):
                    dve.wait_ge(g_ps[s], layer * PAIRS + pair + 1)
                    for r in range(2):
                        dve.tensor_tensor(cm[s][:, r:NB - 2:2, 0:CW],
                                          bank(GB[r])[:, 0:3 * CW].rearrange("p (u c) -> p u c", c=CW),
                                          head_mask.unsqueeze(1).broadcast_to([P, 3, CW]), ALU.mult)
                    dve.tensor_tensor(cm[s][:, NB - 2, 0:CW], bank(GB[2])[:, 0:CW], head_mask,
                                      ALU.mult).then_inc(cm_ready[s], 1)

                def attended(pair, stp, s, at=KVB[0]):
                    dve.wait_ge(o_ps[s], layer * PAIRS + pair + 1)
                    o = ps[:, at:at + 2, 0:2 * OW].rearrange("p b (t c) -> p b t c", c=OW)
                    by_head = "p (b t h) -> p b t h"
                    stp.done(dve.tensor_copy(qeps[s][:, :].rearrange(by_head, b=2, t=2), o[:, :, :, CW:OW]))
                    stp.done(dve.tensor_tensor(den[s][:, :].rearrange(by_head, b=2, t=2), o[:, :, :, P:CW],
                                               qeps[s][:, :].rearrange(by_head, b=2, t=2), ALU.max))
                    stp.done(dve.reciprocal(rden[s][:, :], den[s][:, :]))
                    for i in range(2):
                        r = rden[s][:, 2 * i * HEADS:2 * (i + 1) * HEADS].rearrange("p (t h) -> p t h", h=HEADS)
                        ins = dve.tensor_tensor(att[s][:, 2 * i:2 * i + 2, :].rearrange("p t (h d) -> p t h d", d=DH),
                                                o[:, i, :, 0:P].rearrange("p t (h d) -> p t h d", d=DH),
                                                r.unsqueeze(3).broadcast_to([P, 2, HEADS, DH]), ALU.mult)
                    ins.then_inc(att_ready[s], 1)

                def attn_residual(pair, stp, s):
                    a = layer * PAIRS + pair
                    dve.wait_ge(wo_ps[s], a + 1)
                    dve.wait_ge(bo_added[s], a + 1)
                    residual(stp, s, pair)

                def k_of(pair):
                    return layer * (2 * PAIRS) + pair + PAIRS

                def ff_k(pair):
                    return layer * (2 * PAIRS) + pair + 2 * PAIRS

                def ff_steps(layer, pair, s):
                    done = layer * (2 * PAIRS) + pair * 2 + s
                    return Steps(dve, dve_steps["lf"], done * DVE_STEPS["lf"], DVE_STEPS["lf"])

                def ff_sum(stp, layer, pair, s):
                    dve.wait_ge(yT_ps[s], layer * PAIRS + pair + (PAIRS + 1))
                    residual(stp, s, pair)

                def ff_stats(stp, layer, pair, s):
                    x_stats(stp, s, pair, layer * (2 * PAIRS) + pair + 2 * PAIRS)

                def ff_residual(pair, s):
                    if last:
                        stp = Steps(dve, dve_steps["end"], pair * 2 + s, DVE_STEPS["end"])
                    else:
                        stp = ff_steps(layer, pair, s)
                    ff_sum(stp, layer, pair, s)
                    if not last:
                        ff_stats(stp, layer, pair, s)
                    stp.close()

                def ff_split(pair, s):
                    split_input(ff_k(pair), layer * PAIRS + pair + PAIRS, s)

                stp = steps(0, "la_front")
                queries(0, stp, 0)
                if first:
                    tok = tok_steps(PAIRS - 1, "tf_1")
                    tok_sum(tok, PAIRS - 1, 1)
                    queries(0, stp, 1)
                    for s in range(2):
                        tok_gain(tok, PAIRS - 1, s)
                else:
                    lf = ff_steps(layer - 1, PAIRS - 1, 1)
                    ff_sum(lf, layer - 1, PAIRS - 1, 1)
                    queries(0, stp, 1)
                    ff_stats(lf, layer - 1, PAIRS - 1, 1)
                    lf.close()
                if first:
                    for s in range(2):
                        tok_out_stats(tok, PAIRS - 1, s)
                    tok.close()
                for s in range(2):
                    masked(0, s)
                stp.close()
                if first:
                    for s in range(2):
                        tok_out(PAIRS - 1, s)
                with dve.Fori(1, PAIRS) as pair:
                    front, back = steps(pair, "la_front"), steps(pair - 1, "la_back")
                    attended(pair - 1, back, 0)
                    queries(pair, front, 0)
                    queries(pair, front, 1)
                    attended(pair - 1, back, 1)
                    for s in range(2):
                        attn_residual(pair - 1, back, s)
                        masked(pair, s)
                        x_stats(back, s, pair - 1, k_of(pair - 1))
                    front.close()
                    back.close()
                stp = steps(PAIRS - 1, "la_back")
                for s in range(2):
                    attended(PAIRS - 1, stp, s, LAST_OB[s])
                    ff_split(0, s)
                for s in range(2):
                    attn_residual(PAIRS - 1, stp, s)
                    x_stats(stp, s, PAIRS - 1, k_of(PAIRS - 1))
                stp.close()

                def ff(pair, first_pair=False, last_pair=False):
                    if not (last and last_pair):
                        prepare(pair, ff_k(pair))
                    else:
                        gate_stats(0)
                    if not first_pair:
                        ff_residual(pair - 1, 1)
                    if not last_pair:
                        ff_split(pair + 1, 0)
                    ff_residual(pair, 0)
                    if not last_pair:
                        ff_split(pair + 1, 1)

                ff(0, first_pair=True)
                with dve.Fori(1, PAIRS - 1) as pair:
                    ff(pair)
                ff(PAIRS - 1, last_pair=True)
                if last:
                    gate_top(0, FIRST_GLB)
                    ff_residual(PAIRS - 1, 1)

            layer_phases(0, first=True)
            with dve.Fori(1, LAYERS - 1) as layer:
                layer_phases(layer)
            layer_phases(LAYERS - 1, last=True)

            def input_lo(b):
                dve.wait_ge(x1_hi_ready, b + 1)
                dve.tensor_tensor(x1_lo[:, turn(b)], bank(GTB), x1_hi[:, turn(b)].bitcast(F32),
                                  ALU.subtract).then_inc(x1_ready, 1)

            def second(b, u):
                dve.wait_ge(mz_ps, b * (E * J) + (u + 1))
                dve.tensor_tensor(z2[u % 2][:, :], bank(MZB[u % 4]), rb[:, turn(b)], ALU.mult).then_inc(mz2_ready, 1)

            def result(b):
                dve.wait_ge(myT_ps, b + 1)
                hs = h_tok[:, seq(b), :]
                dve.tensor_tensor(hs, bank(MTB).rearrange("p (t q) -> p t q", t=T), hs, ALU.add).then_inc(out_ready, 1)

            def experts(b, first=False, last=False):
                for u in range(E * J):
                    if u + 1 < E * J:
                        second(b, u + 1)
                    elif not last:
                        dve.wait_ge(rb_ready, b + 2)
                        second(b + 1, 0)
                    if not first and u < 4 or u >= 4:
                        free = (u - 4) % (E * J)
                        if free in SPLIT:
                            dve.wait_ge(hid_split, (b if u >= 4 else b - 1) * len(SPLIT) + (SPLIT.index(free) + 1))
                    dve.wait_ge(mg_ready, b * (E * J) + (u + 1))
                    dve.tensor_tensor(hid[u % 4][:, :], g1[u % 2][:, :], g2[u % 2][:, :], ALU.add).then_inc(mh_ready, 1)
                    if u == AT["result"] and not first:
                        result(b - 1)
                    if not last:
                        if u == AT["stats"]:
                            gate_stats(b + 1)
                        if u == AT["top"]:
                            gate_top(b + 1)
                        if u == AT["share"]:
                            gate_share(b + 1)
                        if u == AT["input_lo"]:
                            input_lo(b + 1)

            gate_share(0)
            input_lo(0)
            dve.wait_ge(rb_ready, 1)
            second(0, 0)
            experts(0, first=True)
            with dve.Fori(1, B - 1) as b:
                experts(b)
            experts(B - 1, last=True)
            result(B - 1)

        @block.scalar
        def _(act):
            act.wait_ge(d_start, STARTS * 16)
            act.preload_act_table_set("exp_and_others")
            with act.Fori(0, PAIRS) as pair:
                for s in range(2):
                    act.wait_ge(tok_xT_ps[s], pair + 1)
                    act.activation(hT[s][:, :], bank(TB[s]), ACT.Copy).then_inc(tok_xT[s], 1)
                for s in range(2):
                    act.wait_ge(tok_kqv_ps[s], pair * 3 + 1)
                    act.activation(kT[s][:, :], bank(UB[s][0]), ACT.Identity,
                                   bias=w_tok[:, 3 * P:3 * P + 1]).then_inc(tok_kT[s], 1)
                    act.wait_ge(tok_kqv_ps[s], pair * 3 + 3)
                    act.activation(v[s][:, :, 0:P], bank(UB[s][2]).rearrange("p (t q) -> p t q", t=T),
                                   ACT.Copy).then_inc(tok_v[s], 1)
                for i in range(T):
                    for s in range(2):
                        act.wait_ge(tok_max[s], pair * T + (i + 1))
                        act.activation(pr[s][i % 2][:, :], bank(UB[s][i % 2]), ACT.Exp, bias=nmax[s][:, i:i + 1],
                                       accum_out=psums[s][:, i:i + 1]).then_inc(tok_p[s], 1)

            def affine(w, at, k, s, src):
                act.wait_ge(nT_ps[s], k + 1)
                act.activation(hT[s][:, :], bank(src), ACT.Identity, scale=w[:, at:at + 1],
                               bias=w[:, at + 1:at + 2]).then_inc(hT_ready[s], 1)

            def ff_affine(k, s, src=None):
                affine(w_f, 2 * FF, k, s, TB[s] if src is None else src)

            def ff_bias(f, s):
                act.wait_ge(y_ps[s], f + 1)
                act.activation(yT[s][:, :], bank(YB[s]), ACT.Identity, bias=w_f[:, F_COLS - 1:F_COLS]
                               ).then_inc(yT_ready[s], 1)

            def prepare(k, nxt, s):
                act.wait_ge(nT_ps[s], k + 1)
                act.wait_ge(next_rstd[s], k + 2)
                for t in range(T):
                    ins = act.activation(n[s][:, t, :], one(x, nxt, s, t), ACT.Identity,
                                         scale=one(rstd, nxt, s, t), bias=one(nbias, nxt, s, t))
                ins.then_inc(n_ready[s], 1)

            def next_affine(k, s, last, layer):
                if last == "attention":
                    act.wait_ge(d_la, layer * 16 + 16)
                    affine(w_la, 4 * P, k + 1, s, TB[s])
                elif last is None:
                    ff_affine(k + 1, s)

            def gate_transposed(b, src=GTB):
                act.wait_ge(gxT_ps, b + 1)
                act.activation(gT, bank(src), ACT.Copy).then_inc(gxT_ready, 1)

            def tok_input(pair, s):
                act.wait_ge(nT_ps[s], pair)
                act.wait_ge(tok_r[s], pair + 1)
                act.activation(n[s][:, :, :], x[:, tiles(pair, s), :], ACT.Copy).then_inc(n_ready[s], 1)

            def feed_forward(k, f, first=False, last=None, tok=False, layer=None):
                for u in range(2 * J):
                    act.wait_ge(z_ps, f * (2 * J) + (u + 1))
                    c = 2 * FF + 2 + u % J
                    act.activation(g[u % 4][:, :], bank(ZB[u % 4]), ACT.Gelu, bias=w_f[:, c:c + 1]).then_inc(g_ready, 1)
                    if tok and u in TOK_INPUT:
                        s = TOK_INPUT.index(u)
                        if last is None:
                            tok_input(k + 1, s)
                        else:
                            act.wait_ge(tok_out_ready[s], 1)
                            prepare(k, 0, s)
                    if u == 1 and not first:
                        ff_bias(f - 1, 1)
                    if u == 5:
                        next_affine(k, 0, last, layer)
                        ff_bias(f, 0)
                    if u == 6 and last == "gating":
                        gate_transposed(0, FIRST_GTB)
                    if u == 7:
                        next_affine(k, 1, last, layer)

            act.preload_act_table_set("gelu_and_others")
            act.wait_ge(d_f, 16)
            for s in range(2):
                ff_affine(0, s)
            feed_forward(0, 0, first=True, tok=True)
            with act.Fori(1, PAIRS - 1) as pair:
                feed_forward(pair, pair, tok=True)
            feed_forward(PAIRS - 1, PAIRS - 1, last="attention", tok=True, layer=0)
            ff_bias(PAIRS - 1, 1)
            def layer_phases(layer, first=False, last=False):
                act.preload_act_table_set("exp_and_others")

                def k_of(pair):
                    return layer * (2 * PAIRS) + pair + PAIRS

                def prepare_next(pair, s):
                    nxt = (pair + 1) % PAIRS
                    if first:
                        act.wait_ge(tok_out_ready[s], nxt + 1)
                    prepare(k_of(pair), nxt, s)

                def keys_values(pair, s):
                    a = layer * PAIRS + pair
                    for i in range(2):
                        act.wait_ge(kv_ps[s], a * 2 + (i + 1))
                        kv = bank(KVB[i]).rearrange("p (t c) -> p t c", t=2)
                        act.activation(ek[s][:, 2 * i:2 * i + 2, :], kv[:, :, 0:P], ACT.Exp)
                        ins = act.activation(v[s][:, 2 * i:2 * i + 2, 0:P], kv[:, :, P:2 * P], ACT.Copy)
                    ins.then_inc(v_ready[s], 1)

                def exp_queries(pair, s):
                    act.wait_ge(qs_ready[s], layer * PAIRS + pair + 1)
                    act.activation(eq[s][:, :], qs[s][:, :], ACT.Exp).then_inc(eq_ready[s], 1)

                def transposed(pair, s, ps_ready, dst, done):
                    act.wait_ge(ps_ready[s], layer * PAIRS + pair + 1)
                    act.activation(dst[s][:, :], bank(TB[s]), ACT.Copy).then_inc(done[s], 1)

                for s in range(2):
                    keys_values(0, s)
                    exp_queries(0, s)
                    prepare_next(0, s)
                for s in range(2):
                    transposed(0, s, qT_ps, qT, qT_ready)
                with act.Fori(1, PAIRS) as pair:
                    for s in range(2):
                        affine(w_la, 4 * P, k_of(pair), s, TB[s])
                    transposed(pair - 1, 0, aT_ps, aT, aT_ready)
                    exp_queries(pair, 0)
                    keys_values(pair, 0)
                    exp_queries(pair, 1)
                    prepare_next(pair, 0)
                    transposed(pair, 0, qT_ps, qT, qT_ready)
                    transposed(pair - 1, 1, aT_ps, aT, aT_ready)
                    keys_values(pair, 1)
                    prepare_next(pair, 1)
                    transposed(pair, 1, qT_ps, qT, qT_ready)
                act.wait_ge(d_f, layer * 16 + 32)
                for s in range(2):
                    ff_affine(layer * (2 * PAIRS) + 2 * PAIRS, s, FIRST_NB[s])
                for s in range(2):
                    transposed(PAIRS - 1, s, aT_ps, aT, aT_ready)
                act.preload_act_table_set("gelu_and_others")

                def ff(pair, **which):
                    feed_forward(layer * (2 * PAIRS) + pair + 2 * PAIRS, layer * PAIRS + pair + PAIRS, **which)

                ff(0, first=True)
                with act.Fori(1, PAIRS - 1) as pair:
                    ff(pair)
                if last:
                    ff(PAIRS - 1, last="gating")
                else:
                    ff(PAIRS - 1, last="attention", layer=layer + 1)
                ff_bias(layer * PAIRS + (2 * PAIRS - 1), 1)

            layer_phases(0, first=True)
            with act.Fori(1, LAYERS - 1) as layer:
                layer_phases(layer)
            layer_phases(LAYERS - 1, last=True)


            def input_hi(b):
                act.wait_ge(xs_ps, b + 1)
                act.activation(x1_hi[:, turn(b)], bank(GTB), ACT.Copy).then_inc(x1_hi_ready, 1)

            def ratios(b):
                act.activation(rb[:, turn(b)], bank(GLB), ACT.Copy).then_inc(rb_ready, 1)

            def out_bias(b):
                act.wait_ge(my_ps, b + 1)
                act.activation(yT[0][:, :], bank(MYB), ACT.Identity, bias=b2_twice[:, 0:1]).then_inc(myT_ready, 1)

            def experts(b, first=False, last=False):
                for u in range(E * J):
                    act.wait_ge(mz2_ready, b * (E * J) + (u + 1))
                    b1 = c_moe[:, E + u:E + u + 1]
                    act.activation(g1[u % 2][:, :], bank(MZB[u % 4]), ACT.Gelu, bias=b1)
                    act.activation(g2[u % 2][:, :], z2[u % 2][:, :], ACT.Gelu, bias=b1).then_inc(mg_ready, 1)
                    if u == 1 and not first:
                        out_bias(b - 1)
                    if not last:
                        if u == AT["transposed"]:
                            gate_transposed(b + 1)
                        if u == AT["input_hi"]:
                            input_hi(b + 1)
                        if u == AT["ratios"]:
                            ratios(b + 1)

            act.wait_ge(setup_dve, 2)
            input_hi(0)
            ratios(0)
            experts(0, first=True)
            with act.Fori(1, B - 1) as b:
                experts(b)
            experts(B - 1, last=True)
            out_bias(B - 1)

        @block.tensor
        def _(pe):
            pe.wait_ge(d_start, STARTS * 16)

            def token_attention(pair, later):
                for s in range(2):
                    pe.wait_ge(tok_x[s], pair + 1)
                    transposes(pe, TB[s], lambda t: n[s][:, t, :]).then_inc(tok_xT_ps[s], 1)
                for s in range(2):
                    pe.wait_ge(tok_xT[s], pair + 1)
                    for i in range(2):
                        pe.matmul(bank(UB[s][i]), w_tok[:, i * P:(i + 1) * P], hT[s][:, :],
                                  start=True, stop=True).then_inc(tok_kqv_ps[s], 1)
                    if later:
                        pe.wait_ge(tok_o_read[s], pair)
                    for t in range(T):
                        ins = pe.matmul(bank(UB[s][2])[:, t * P:(t + 1) * P], hT[s][:, t * P:(t + 1) * P],
                                        w_tok[:, 2 * P:3 * P], start=True, stop=True)
                    ins.then_inc(tok_kqv_ps[s], 1)
                for i in range(T + 2):
                    for s in range(2):
                        if i < T:
                            if i == 0:
                                pe.wait_ge(tok_kT[s], pair + 1)
                                pe.wait_ge(tok_qT[s], pair + 1)
                            pe.matmul(bank(UB[s][i % 2]), kT[s][:, i * P:(i + 1) * P], qT[s][:, :],
                                      start=True, stop=True).then_inc(tok_s_ps[s], 1)
                    for s in range(2):
                        if 1 <= i <= T:
                            pe.wait_ge(tok_p[s], pair * T + i)
                            if i >= 2:
                                pe.wait_ge(tok_pT[s], pair * T + (i - 1))
                            transposes(pe, TB[s], lambda t: pr[s][(i - 1) % 2][:, t * P:(t + 1) * P]
                                       ).then_inc(tok_pT_ps[s], 1)
                    for s in range(2):
                        if i >= 2:
                            if i == 2:
                                pe.wait_ge(tok_v[s], pair + 1)
                            pe.wait_ge(tok_pT[s], pair * T + (i - 1))
                            for t in range(T):
                                ins = pe.matmul(bank(UB[s][2])[:, (i - 2) * P:(i - 1) * P], prT[s][i % 2][:, t, :],
                                                v[s][:, t, 0:P], start=(t == 0), stop=(t == T - 1))
                            if i == T + 1:
                                ins.then_inc(tok_o_ps[s], 1)

            token_attention(0, False)
            with pe.Fori(1, PAIRS) as pair:
                token_attention(pair, True)

            def norm_transposes(k, s, freed):
                pe.wait_ge(n_ready[s], k + 1)
                pe.wait_ge(t_free[s], freed)
                transposes(pe, TB[s], lambda t: n[s][:, t, :]).then_inc(nT_ps[s], 1)

            def ff_up(f, u):
                s, j = divmod(u, J)
                if j == 0:
                    pe.wait_ge(h_split[s], f + 1)
                w = slice(j * P, (j + 1) * P)
                dst = bank(ZB[u % 4])
                pe.matmul(dst, w1_hi[:, w], h_hi[s], start=True, stop=False)
                pe.matmul(dst, w1_hi[:, w], h_lo[s], start=False, stop=False)
                pe.matmul(dst, w1_lo[:, w], h_hi[s], start=False, stop=True).then_inc(z_ps, 1)

            def ff_transposes(f, s):
                pe.wait_ge(yT_ready[s], f + 1)
                transposes(pe, TB[s], lambda t: yT[s][:, t * P:(t + 1) * P]).then_inc(yT_ps[s], 1)

            ff_lead = 2

            def gate_transposes(b, dst=GTB):
                pe.wait_ge(gx_ready, b + 1)
                transposes(pe, dst, lambda t: gx[:, t, :]).then_inc(gxT_ps, 1)

            def logits(b, dst=GLB):
                pe.wait_ge(gxT_ready, b + 1)
                for t in range(T):
                    ins = pe.matmul(bank(dst)[:, t * E:(t + 1) * E], gT[:, t * P:(t + 1) * P], c_moe[:, 0:E],
                                    start=True, stop=True)
                ins.then_inc(gl_ps, 1)

            def feed_forward(k, f, first=False, last=None):
                for u in range(2 * J):
                    if u + ff_lead < 2 * J:
                        ff_up(f, u + ff_lead)
                    elif not last:
                        ff_up(f + 1, u + ff_lead - 2 * J)
                    s, j = divmod(u, J)
                    pe.wait_ge(g_ready, f * (2 * J) + (u + 1))
                    ins = pe.matmul(bank(YB[s]), w_f[:, FF + j * P:FF + (j + 1) * P], g[u % 4][:, :],
                                    start=(j == 0), stop=(j == J - 1))
                    if j == J - 1:
                        ins.then_inc(y_ps[s], 1)
                    if u == 1 and not first:
                        ff_transposes(f - 1, 1)
                    if u == 3 and last != "gating":
                        norm_transposes(k + 1, 0, k + 1)
                    if u == 5:
                        if last != "gating":
                            pe.wait_ge(hT_ready[0], k + 2)
                        else:
                            pe.wait_ge(t_free[0], k + 1)
                        ff_transposes(f, 0)
                    if u == 6 and last != "gating":
                        norm_transposes(k + 1, 1, k + 1)
                    if last == "gating" and u == 4:
                        pe.wait_ge(t_free[1], k + 1)
                        gate_transposes(0, FIRST_GTB)
                    if last == "gating" and u == 6:
                        logits(0, FIRST_GLB)

            pe.wait_ge(d_f, 16)
            pe.wait_ge(w1_split, 1)
            for s in range(2):
                norm_transposes(0, s, 1)
            for u in range(ff_lead):
                ff_up(0, u)
            feed_forward(0, 0, first=True)
            with pe.Fori(1, PAIRS - 1) as pair:
                feed_forward(pair, pair)
            feed_forward(PAIRS - 1, PAIRS - 1, last="attention")
            pe.wait_ge(setup_dve, 1)

            def layer_phases(layer, first=False, last=False):
                def k_of(pair):
                    return layer * (2 * PAIRS) + pair + PAIRS

                def queries(pair, s, later):
                    pe.wait_ge(hT_ready[s], k_of(pair) + 1)
                    if s == 1 and later:
                        pe.wait_ge(cm_ready[1], layer * PAIRS + pair)
                    for t in range(T):
                        ins = pe.matmul(bank(QB[s])[:, t * P:(t + 1) * P], hT[s][:, t * P:(t + 1) * P], w_la[:, 0:P],
                                        start=True, stop=True)
                    ins.then_inc(q_ps[s], 1)

                def keys_values(s):
                    for t in range(T):
                        c = (t % 2) * 2 * P
                        ins = pe.matmul(bank(KVB[t // 2])[:, c:c + 2 * P], hT[s][:, t * P:(t + 1) * P],
                                        w_la[:, P:3 * P], start=True, stop=True)
                        if t % 2:
                            ins.then_inc(kv_ps[s], 1)

                def contexts(pair, s):
                    pe.wait_ge(v_ready[s], layer * PAIRS + pair + 1)
                    if s == 0:
                        pe.wait_ge(qs_ready[1], layer * PAIRS + pair + 1)
                    else:
                        pe.wait_ge(cm_ready[0], layer * PAIRS + pair + 1)
                    for u in range(NB - 1):
                        r = BUCKET * (u % 2)
                        dst = bank(GB[2])[:, 0:CW] if u == NB - 2 else bank(GB[u % 2])[:, (u // 2) * CW:(u // 2 + 1) * CW]
                        ins = pe.matmul(dst, ek[s][r:r + BUCKET, u // 2, :], v[s][r:r + BUCKET, u // 2, :],
                                        start=True, stop=True)
                    ins.then_inc(g_ps[s], 1)

                def query_transposes(pair, s):
                    pe.wait_ge(eq_ready[s], layer * PAIRS + pair + 1)
                    pe.wait_ge(t_free[s], k_of(pair) + 1)
                    transposes(pe, TB[s], lambda t: eq[s][:, t * P:(t + 1) * P]).then_inc(qT_ps[s], 1)

                def products(pair, s, at=KVB[0]):
                    pe.wait_ge(qT_ready[s], layer * PAIRS + pair + 1)
                    pe.wait_ge(ctx_ready[s], layer * PAIRS + pair + 1)
                    for u in range(NB):
                        t, r = u // 2, BUCKET * (u % 2)
                        ctx_u = zero_ctx[:, :] if u == 0 else cm[s][:, u - 1, :]
                        ins = pe.matmul(bank(at + t // 2)[r:r + BUCKET, (t % 2) * OW:(t % 2 + 1) * OW],
                                        qT[s][:, u * BUCKET:(u + 1) * BUCKET], ctx_u, start=True, stop=True)
                    ins.then_inc(o_ps[s], 1)

                def attended_transposes(s):
                    transposes(pe, TB[s], lambda t: att[s][:, t, :]).then_inc(aT_ps[s], 1)

                def output(pair, s):
                    pe.wait_ge(aT_ready[s], layer * PAIRS + pair + 1)
                    for t in range(T):
                        ins = pe.matmul(bank(TB[s])[:, t * P:(t + 1) * P], aT[s][:, t * P:(t + 1) * P],
                                        w_la[:, 3 * P:4 * P], start=True, stop=True)
                    ins.then_inc(wo_ps[s], 1)

                def later_norm(pair, s):
                    pe.wait_ge(n_ready[s], k_of(pair) + 1)
                    pe.wait_ge(qT_ready[s], layer * PAIRS + pair)
                    transposes(pe, TB[s], lambda t: n[s][:, t, :]).then_inc(nT_ps[s], 1)

                pe.wait_ge(d_la, layer * 16 + 16)
                queries(0, 0, False)
                keys_values(0)
                pe.wait_ge(hT_ready[1], k_of(0) + 1)
                ff_transposes(layer * PAIRS + (PAIRS - 1), 1)
                queries(0, 1, False)
                pe.wait_ge(v_ready[0], layer * PAIRS + 1)
                keys_values(1)
                for s in range(2):
                    contexts(0, s)
                    query_transposes(0, s)
                with pe.Fori(1, PAIRS) as pair:
                    a = layer * PAIRS + pair
                    later_norm(pair, 0)
                    products(pair - 1, 0)
                    later_norm(pair, 1)
                    queries(pair, 0, True)
                    queries(pair, 1, True)
                    pe.wait_ge(att_ready[0], a)
                    attended_transposes(0)
                    keys_values(0)
                    pe.wait_ge(v_ready[0], a + 1)
                    products(pair - 1, 1)
                    output(pair - 1, 0)
                    contexts(pair, 0)
                    query_transposes(pair, 0)
                    pe.wait_ge(att_ready[1], a)
                    attended_transposes(1)
                    keys_values(1)
                    output(pair - 1, 1)
                    contexts(pair, 1)
                    query_transposes(pair, 1)
                k, f = layer * (2 * PAIRS) + 2 * PAIRS, layer * PAIRS + PAIRS
                pe.wait_ge(n_ready[0], k + 1)
                transposes(pe, FIRST_NB[0], lambda t: n[0][:, t, :]).then_inc(nT_ps[0], 1)
                pe.wait_ge(n_ready[1], k + 1)
                pe.wait_ge(cm_ready[1], layer * PAIRS + PAIRS)
                transposes(pe, FIRST_NB[1], lambda t: n[1][:, t, :]).then_inc(nT_ps[1], 1)
                for s in range(2):
                    products(PAIRS - 1, s, LAST_OB[s])
                for s in range(2):
                    pe.wait_ge(att_ready[s], layer * PAIRS + PAIRS)
                    attended_transposes(s)
                pe.wait_ge(d_f, layer * 16 + 32)
                pe.wait_ge(w1_split, layer + 2)
                for s in range(2):
                    ff_up(f, s)
                    output(PAIRS - 1, s)

                def ff(pair, **which):
                    feed_forward(layer * (2 * PAIRS) + pair + 2 * PAIRS, layer * PAIRS + pair + PAIRS, **which)

                ff(0, first=True)
                with pe.Fori(1, PAIRS - 1) as pair:
                    ff(pair)
                ff(PAIRS - 1, last="gating" if last else "attention")
                if last:
                    pe.wait_ge(t_free[1], layer * (2 * PAIRS) + 3 * PAIRS)
                    ff_transposes(layer * PAIRS + (2 * PAIRS - 1), 1)

            layer_phases(0, first=True)
            with pe.Fori(1, LAYERS - 1) as layer:
                layer_phases(layer)
            layer_phases(LAYERS - 1, last=True)

            def input_transposes(b):
                pe.wait_ge(xs_ready, b + 1)
                transposes(pe, GTB, lambda t: xs[:, t, :])
                for t in range(T):
                    ins = pe.matmul(bank(GLB)[:, t * P:(t + 1) * P], ratio[:, t:t + 1].broadcast_to([P, P]), ident,
                                    start=True, stop=True)
                ins.then_inc(xs_ps, 1)

            def up(b, u):
                w = slice(u * P, (u + 1) * P)
                dst = bank(MZB[u % 4])
                pe.matmul(dst, w_up_hi[:, w], x1_hi[:, turn(b)], start=True, stop=False)
                pe.matmul(dst, w_up_hi[:, w], x1_lo[:, turn(b)], start=False, stop=False)
                pe.matmul(dst, w_up_lo[:, w], x1_hi[:, turn(b)], start=False, stop=True).then_inc(mz_ps, 1)

            def result_transposes(b):
                pe.wait_ge(myT_ready, b + 1)
                transposes(pe, MTB, lambda t: yT[0][:, t * P:(t + 1) * P]).then_inc(myT_ps, 1)

            lead = 3

            def down_split(b, u):
                i = SPLIT.index(u)
                w = slice(i * P, (i + 1) * P)
                pe.wait_ge(hid_split, b * len(SPLIT) + (i + 1))
                pe.matmul(bank(MYB), w_dn_hi[:, w], hid_hi[HB[i]][:, :], start=False, stop=False)
                pe.matmul(bank(MYB), w_dn_hi[:, w], hid_lo[HB[i]][:, :], start=False, stop=False)
                pe.matmul(bank(MYB), w_dn_lo[:, w], hid_hi[HB[i]][:, :], start=False, stop=False
                          ).then_inc(hid_used, 1)

            def experts(b, first=False, last=False):
                for u in range(E * J):
                    if u - 1 in SPLIT:
                        pe.wait_ge(mh_ready, b * (E * J) + u)
                    if u + lead < E * J:
                        up(b, u + lead)
                    elif not last:
                        if u + lead == E * J:
                            pe.wait_ge(x1_ready, b + 2)
                        up(b + 1, u + lead - E * J)
                    if u == 0 and not first:
                        pe.wait_ge(myT_ready, b)
                    if u - SPLIT_LAG in SPLIT:
                        down_split(b, u - SPLIT_LAG)
                    if u in WHOLE:
                        pe.wait_ge(mh_ready, b * (E * J) + (u + 1))
                        w = WHOLE.index(u) * P
                        ins = pe.matmul(bank(MYB), w_down[:, w:w + P], hid[u % 4][:, :],
                                        start=(u == 0), stop=(u == E * J - 1))
                    if u == AT["result_T"] and not first:
                        result_transposes(b - 1)
                    if not last:
                        if u == AT["gate_T"]:
                            gate_transposes(b + 1)
                        if u == AT["logits"]:
                            logits(b + 1)
                        if u == AT["input_T"]:
                            input_transposes(b + 1)
                ins.then_inc(my_ps, 1)

            input_transposes(0)
            pe.wait_ge(d_down, 16)
            pe.wait_ge(moe_split, 2 * LAYERS)
            pe.wait_ge(x1_ready, 1)
            for s in range(2):
                pe.wait_ge(t_free[s], (1 + 2 * LAYERS) * PAIRS + 1)
            for u in range(lead):
                up(0, u)
            experts(0, first=True)
            with pe.Fori(1, B - 1) as b:
                experts(b)
            experts(B - 1, last=True)
            result_transposes(B - 1)


def position_code():
    at = np.arange(S, dtype=np.float32)[:, None]
    i = np.arange(P, dtype=np.float32)[None, :]
    ang = at / np.power(np.float32(10000.0), np.float32(2.0) * i / np.float32(P))
    code = np.where((np.arange(P) % 2 == 0)[None, :], np.sin(ang), np.cos(ang)).astype(np.float32)
    return np.ascontiguousarray((code * np.float32(P ** 0.5)).reshape(T, P, P).transpose(1, 0, 2))


def constants():
    head = np.arange(P) // DH
    mask = np.concatenate([head[:, None] == head[None, :], head[:, None] == np.arange(HEADS)[None, :]], axis=1)
    return np.concatenate([np.eye(P, dtype=np.float32), mask.astype(np.float32)], axis=1)


def kernel(**inputs):
    import concourse.bacc as bacc
    from concourse.bass_utils import run_bass_kernel_spmd

    a = {k: np.asarray(v) for k, v in inputs.items()}

    def blocks(w):
        return w.reshape(*w.shape[:-2], J, P, P).swapaxes(-3, -2).reshape(*w.shape[:-2], P, J * P)

    def col(v):
        return v[..., None]

    def cols(v):
        return v.reshape(*v.shape[:-1], J, P).swapaxes(-1, -2)

    t = {k[7:]: v for k, v in a.items() if k.startswith("L0_tok_")}
    l = {k[8:]: v for k, v in a.items() if k.startswith("L0_attn_")}
    m = {k[7:]: v for k, v in a.items() if k.startswith("L0_ffn_")}
    one, zero = np.ones((P, 1), np.float32), np.zeros((P, 1), np.float32)
    ffn_tok = np.concatenate([t["w1"], blocks(t["w2"]), one, zero, cols(t["b1"]), col(t["b2"])], axis=1)
    ffn_l = np.concatenate([l["w1"], blocks(l["w2"]), col(l["ln2_g"]), col(l["ln2_b"]), cols(l["b1"]), col(l["b2"])],
                           axis=2)
    down = blocks(m["W2"]).transpose(1, 0, 2).reshape(P, E * J, P)
    arrays = {
        "ids": np.ascontiguousarray(a["x"].reshape(B * T, P).T),
        "emb": t["emb"],
        "pos": position_code(),
        "consts": constants(),
        "tok_w": np.concatenate([t["wk"], t["wq"], t["wv"], col(t["bk"]), col(t["bq"])], axis=1),
        "tok_rows": np.stack([t["bv"], t["ln_g"], t["ln_b"]]),
        "attn_w": np.concatenate([l["wq"], l["wk"], l["wv"], l["wo"], col(l["ln1_g"]), col(l["ln1_b"])], axis=2),
        "attn_bo": l["bo"],
        "ffn_w": np.concatenate([ffn_tok[None], ffn_l], axis=0),
        "moe_up": m["W1"].transpose(1, 0, 2).reshape(P, E * FF),
        "moe_dn": down[:, SPLIT + [0] * (LAYERS * DN_COLS // P - len(SPLIT))].reshape(P, LAYERS * DN_COLS),
        "moe_down": down[:, WHOLE].reshape(P, len(WHOLE) * P),
        "moe_c": np.concatenate([m["Wg"], cols(m["b1"]).transpose(1, 0, 2).reshape(P, E * J), m["b2"].T], axis=1),
    }
    nc = bacc.Bacc("TRN2", target_bir_lowering=False, num_devices=1)
    args = []
    for name, v in arrays.items():
        arrays[name] = v = np.ascontiguousarray(v)
        args.append(nc.dram_tensor(name, v.shape, mybir.dt.from_np(v.dtype), kind="ExternalInput").ap())
    out = nc.dram_tensor("out", (B, S, P), mybir.dt.float32, kind="ExternalOutput").ap()
    build(nc, *args, out)
    r = run_bass_kernel_spmd(nc, [arrays], core_ids=[0])
    return r.results[0]["out"]
```
